# Optimizing a Trainium2 kernel written in Bass

```python
import numpy as np
import jax
import jax.numpy as jnp

def _softmax(x, axis=-1):
    return jax.nn.softmax(x, axis=axis)

def _gelu(x):
    return jax.nn.gelu(x, approximate=True)

def _silu(x):
    return jax.nn.silu(x)

def _sigmoid(x):
    return jax.nn.sigmoid(x)

def _layernorm(x, axis=-1, eps=1e-05):
    m = jnp.mean(x, axis=axis, keepdims=True)
    v = jnp.var(x, axis=axis, keepdims=True)
    return (x - m) / jnp.sqrt(v + eps)

def _scatter_add(tgt, idx, src, axis=0):
    return tgt.at[idx].add(src)

def _segment_sum(src, seg, n):
    return jax.ops.segment_sum(src, seg, n)
kernel_name = 'mk_gnn_resnorm_d4_gnn_r16_d8a6ab'

def setup_inputs(seed: int=0):
    np.random.seed(seed)
    _w = jnp.asarray

    def _rec_inputs():
        import jax
        import jax.numpy as jnp
        _gk = jax.random.key(seed)
        x = -0.0003713 + 1 * jax.random.normal(jax.random.fold_in(_gk, 1), (6250, 128), jnp.float32)
        _s = jax.random.randint(jax.random.fold_in(_gk, 2), (100000,), 0, 6250, jnp.int32)
        _d = jax.random.randint(jax.random.fold_in(_gk, 3), (100000,), 0, 6250, jnp.int32)
        _loop = jnp.arange(6250, dtype=jnp.int32)
        src = jnp.concatenate([_s, _d, _loop])
        dst = jnp.concatenate([_d, _s, _loop])
        _o = jnp.argsort(dst, stable=True)
        src = src[_o]
        dst = dst[_o]
        edge_attr_50 = 0.000152336 + 1.00009 * jax.random.normal(jax.random.fold_in(_gk, 12), (206250, 50), jnp.float32)
        edge_type_16 = jax.random.randint(jax.random.fold_in(_gk, 14), (206250,), 0, 16, jnp.int32)
        edge_weight = jax.random.uniform(jax.random.fold_in(_gk, 15), (206250,), jnp.float32, 0.0, 9.99998)
        node_type_8 = jax.random.randint(jax.random.fold_in(_gk, 16), (6250,), 0, 8, jnp.int32)
        return (x, src, dst, edge_attr_50, edge_type_16, edge_weight, node_type_8)
    x, src, dst, edge_attr_50, edge_type_16, edge_weight, node_type_8 = _rec_inputs()

    def _L0_gnn_setup():
        import jax, jax.numpy as jnp
        import numpy as np
        N = 6250
        E = 100000
        D_IN = 128
        D_OUT = 128
        HEADS = 4
        C = D_OUT // HEADS
        NEG_SLOPE = 0.2
        EPS_SOFTMAX = 1e-16
        EPS_LN = 1e-05

        def _gat_edge_conv(x, src, dst, W, att_src, att_dst, gat_bias, skip_W, skip_b, ln_g, ln_b):
            n = x.shape[0]
            h = (x @ W).reshape(n, HEADS, C)
            a_s = jnp.einsum('nhc,hc->nh', h, att_src)
            a_d = jnp.einsum('nhc,hc->nh', h, att_dst)
            e = jax.nn.leaky_relu(a_s[src] + a_d[dst], NEG_SLOPE)
            m = jax.ops.segment_max(e, dst, num_segments=n)
            p = jnp.exp(e - m[dst])
            z = jax.ops.segment_sum(p, dst, num_segments=n)
            alpha = p / (z[dst] + EPS_SOFTMAX)
            msg = h[src] * alpha[:, :, None]
            out = jax.ops.segment_sum(msg, dst, num_segments=n)
            out = out.reshape(n, HEADS * C) + gat_bias
            out = out + x @ skip_W + skip_b
            mu = out.mean(-1, keepdims=True)
            var = ((out - mu) ** 2).mean(-1, keepdims=True)
            return (out - mu) * jax.lax.rsqrt(var + EPS_LN) * ln_g + ln_b
        key = jax.random.key(seed)
        ks = jax.random.split(key, 10)
        x = jax.random.normal(ks[0], (N, D_IN), dtype=jnp.float32)
        edge_index = jax.random.randint(ks[1], (2, E), 0, N, dtype=jnp.int64)
        s = 1.0 / np.sqrt(D_IN)
        W = jax.random.normal(ks[2], (D_IN, HEADS * C), dtype=jnp.float32) * s
        att_src = jax.random.normal(ks[3], (HEADS, C), dtype=jnp.float32) * (1.0 / np.sqrt(C))
        att_dst = jax.random.normal(ks[4], (HEADS, C), dtype=jnp.float32) * (1.0 / np.sqrt(C))
        gat_bias = jax.random.normal(ks[5], (D_OUT,), dtype=jnp.float32) * 0.02
        skip_W = jax.random.normal(ks[6], (D_IN, D_OUT), dtype=jnp.float32) * s
        skip_b = jax.random.normal(ks[7], (D_OUT,), dtype=jnp.float32) * 0.02
        ln_g = jnp.ones((D_OUT,), dtype=jnp.float32)
        ln_b = jnp.zeros((D_OUT,), dtype=jnp.float32)
        return {'x': x, 'edge_index': edge_index, 'W': W, 'att_src': att_src, 'att_dst': att_dst, 'gat_bias': gat_bias, 'skip_W': skip_W, 'skip_b': skip_b, 'ln_g': ln_g, 'ln_b': ln_b}
    _L0_gnn_all = _L0_gnn_setup()
    _L0_gnn_in = {k: v for k, v in _L0_gnn_all.items() if k in ('W', 'att_src', 'att_dst', 'gat_bias', 'skip_W', 'skip_b', 'ln_g', 'ln_b')}
    del _L0_gnn_all

    def _L1_gnn_setup():
        import jax, jax.numpy as jnp
        import numpy as np
        N = 6250
        E = 200000
        IN_DIM = 128
        OUT_DIM = 128
        BN_EPS = 1e-05
        LEAKY_SLOPE = 0.01
        key = jax.random.key(seed)
        ks = jax.random.split(key, 6)
        fea = jax.random.normal(ks[0], (N, IN_DIM), dtype=jnp.float32)
        edges = jax.random.randint(ks[1], (2, E), 0, N, dtype=jnp.int64)
        Wlin = jax.random.normal(ks[2], (IN_DIM, IN_DIM), dtype=jnp.float32) * (1.0 / np.sqrt(IN_DIM))
        blin = jax.random.normal(ks[3], (IN_DIM,), dtype=jnp.float32) * 0.01
        gamma = jnp.ones((IN_DIM,), dtype=jnp.float32)
        beta = jnp.zeros((IN_DIM,), dtype=jnp.float32)
        Wg = jax.random.normal(ks[4], (OUT_DIM, IN_DIM), dtype=jnp.float32) * (1.0 / np.sqrt(IN_DIM))
        bg = jnp.zeros((OUT_DIM,), dtype=jnp.float32)
        return {'fea': fea, 'edges': edges, 'Wlin': Wlin, 'blin': blin, 'gamma': gamma, 'beta': beta, 'Wg': Wg, 'bg': bg}
    _L1_gnn_all = _L1_gnn_setup()
    _L1_gnn_in = {k: v for k, v in _L1_gnn_all.items() if k in ('Wlin', 'blin', 'gamma', 'beta', 'Wg', 'bg')}
    del _L1_gnn_all

    def _L2_gnn_setup():
        import jax, jax.numpy as jnp
        import numpy as np
        N = 3125
        E = 31250
        IN_C = 128
        OUT_C = 128
        N_NODE_TYPES = 8
        N_EDGE_TYPES = 16
        H = 8
        DH = OUT_C // H
        LN_EPS = 1e-05

        def _hgt_forward(x, node_types, edge_src, edge_dst, edge_rel, type_emb, Wk, Wq, Wv, rel_scale, Wo, bo, Wskip, gamma, beta):
            n = x.shape[0]
            x_aug = jnp.concatenate([x, type_emb[node_types]], axis=-1)
            K = (x_aug @ Wk).reshape(n, H, DH)
            Q = (x_aug @ Wq).reshape(n, H, DH)
            V = (x_aug @ Wv).reshape(n, H, DH)
            attn = jnp.einsum('ehd,ehd->eh', Q[edge_dst], K[edge_src])
            attn = attn * rel_scale[edge_rel] / np.sqrt(DH)
            attn = attn - jax.lax.stop_gradient(jnp.max(attn))
            attn_exp = jnp.exp(attn)
            attn_sum = jax.ops.segment_sum(attn_exp, edge_dst, num_segments=n)
            attn_norm = attn_exp / (attn_sum[edge_dst] + 1e-16)
            msg = attn_norm[..., None] * V[edge_src]
            out = jax.ops.segment_sum(msg, edge_dst, num_segments=n).reshape(n, OUT_C)
            out = out @ Wo + bo
            skip = x_aug @ Wskip
            h = out + skip
            mu = jnp.mean(h, axis=-1, keepdims=True)
            var = jnp.mean(jnp.square(h - mu), axis=-1, keepdims=True)
            h = (h - mu) * jax.lax.rsqrt(var + LN_EPS) * gamma + beta
            return jax.nn.elu(h)
        key = jax.random.key(seed)
        ks = jax.random.split(key, 16)
        inp = {'x': jax.random.normal(ks[0], (N, IN_C), dtype=jnp.float32), 'node_types': jax.random.randint(ks[1], (N,), 0, N_NODE_TYPES, dtype=jnp.int32), 'edge_src': jax.random.randint(ks[2], (E,), 0, N, dtype=jnp.int32), 'edge_dst': jax.random.randint(ks[3], (E,), 0, N, dtype=jnp.int32), 'edge_rel': jax.random.randint(ks[4], (E,), 0, N_EDGE_TYPES, dtype=jnp.int32), 'type_emb': 0.1 * jax.random.normal(ks[5], (N_NODE_TYPES, IN_C), dtype=jnp.float32), 'Wk': jax.random.normal(ks[6], (2 * IN_C, OUT_C), dtype=jnp.float32) * (1.0 / np.sqrt(2 * IN_C)), 'Wq': jax.random.normal(ks[7], (2 * IN_C, OUT_C), dtype=jnp.float32) * (1.0 / np.sqrt(2 * IN_C)), 'Wv': jax.random.normal(ks[8], (2 * IN_C, OUT_C), dtype=jnp.float32) * (1.0 / np.sqrt(2 * IN_C)), 'rel_scale': jnp.ones((N_EDGE_TYPES, H), dtype=jnp.float32), 'Wo': jax.random.normal(ks[9], (OUT_C, OUT_C), dtype=jnp.float32) * (1.0 / np.sqrt(OUT_C)), 'bo': jnp.zeros((OUT_C,), dtype=jnp.float32), 'Wskip': jax.random.normal(ks[10], (2 * IN_C, OUT_C), dtype=jnp.float32) * (1.0 / np.sqrt(2 * IN_C)), 'gamma': jnp.ones((OUT_C,), dtype=jnp.float32), 'beta': jnp.zeros((OUT_C,), dtype=jnp.float32)}
        return inp
    _L2_gnn_all = _L2_gnn_setup()
    _L2_gnn_in = {k: v for k, v in _L2_gnn_all.items() if k in ('type_emb', 'Wk', 'Wq', 'Wv', 'rel_scale', 'Wo', 'bo', 'Wskip', 'gamma', 'beta')}
    del _L2_gnn_all

    def _L3_gnn_setup():
        import jax, jax.numpy as jnp
        import numpy as np
        LN2 = float(np.log(2.0))

        def ssp(x):
            return jax.nn.softplus(x) - LN2
        N_NODES = 2500
        N_EDGES = 40000
        HIDDEN = 128
        N_FILTERS = 128
        N_GAUSS = 50
        CUTOFF = 10.0
        key = jax.random.key(seed)
        ks = jax.random.split(key, 12)
        s = 0.05
        x = jax.random.normal(ks[0], (N_NODES, HIDDEN), dtype=jnp.float32)
        edge_index = jax.random.randint(ks[1], (2, N_EDGES), 0, N_NODES)
        edge_weight = jax.random.uniform(ks[2], (N_EDGES,), dtype=jnp.float32) * CUTOFF
        edge_attr = jax.random.normal(ks[3], (N_EDGES, N_GAUSS), dtype=jnp.float32)
        mlp_w1 = jax.random.normal(ks[4], (N_FILTERS, N_GAUSS), dtype=jnp.float32) * s
        mlp_b1 = jnp.zeros((N_FILTERS,), dtype=jnp.float32)
        mlp_w2 = jax.random.normal(ks[5], (N_FILTERS, N_FILTERS), dtype=jnp.float32) * s
        mlp_b2 = jnp.zeros((N_FILTERS,), dtype=jnp.float32)
        lin1_w = jax.random.normal(ks[6], (N_FILTERS, HIDDEN), dtype=jnp.float32) * s
        lin2_w = jax.random.normal(ks[7], (HIDDEN, N_FILTERS), dtype=jnp.float32) * s
        lin2_b = jnp.zeros((HIDDEN,), dtype=jnp.float32)
        lin_w = jax.random.normal(ks[8], (HIDDEN, HIDDEN), dtype=jnp.float32) * s
        lin_b = jnp.zeros((HIDDEN,), dtype=jnp.float32)
        return {'x': x, 'edge_index': edge_index, 'edge_weight': edge_weight, 'edge_attr': edge_attr, 'mlp_w1': mlp_w1, 'mlp_b1': mlp_b1, 'mlp_w2': mlp_w2, 'mlp_b2': mlp_b2, 'lin1_w': lin1_w, 'lin2_w': lin2_w, 'lin2_b': lin2_b, 'lin_w': lin_w, 'lin_b': lin_b}
    _L3_gnn_all = _L3_gnn_setup()
    _L3_gnn_in = {k: v for k, v in _L3_gnn_all.items() if k in ('mlp_w1', 'mlp_b1', 'mlp_w2', 'mlp_b2', 'lin1_w', 'lin2_w', 'lin2_b', 'lin_w', 'lin_b')}
    del _L3_gnn_all
    return {'x': x, 'src': src, 'dst': dst, 'edge_attr_50': edge_attr_50, 'edge_type_16': edge_type_16, 'edge_weight': edge_weight, 'node_type_8': node_type_8, 'L0_gnn_W': _L0_gnn_in['W'], 'L0_gnn_att_src': _L0_gnn_in['att_src'], 'L0_gnn_att_dst': _L0_gnn_in['att_dst'], 'L0_gnn_gat_bias': _L0_gnn_in['gat_bias'], 'L0_gnn_skip_W': _L0_gnn_in['skip_W'], 'L0_gnn_skip_b': _L0_gnn_in['skip_b'], 'L0_gnn_ln_g': _L0_gnn_in['ln_g'], 'L0_gnn_ln_b': _L0_gnn_in['ln_b'], 'L1_gnn_Wlin': _L1_gnn_in['Wlin'], 'L1_gnn_blin': _L1_gnn_in['blin'], 'L1_gnn_gamma': _L1_gnn_in['gamma'], 'L1_gnn_beta': _L1_gnn_in['beta'], 'L1_gnn_Wg': _L1_gnn_in['Wg'], 'L1_gnn_bg': _L1_gnn_in['bg'], 'L2_gnn_type_emb': _L2_gnn_in['type_emb'], 'L2_gnn_Wk': _L2_gnn_in['Wk'], 'L2_gnn_Wq': _L2_gnn_in['Wq'], 'L2_gnn_Wv': _L2_gnn_in['Wv'], 'L2_gnn_rel_scale': _L2_gnn_in['rel_scale'], 'L2_gnn_Wo': _L2_gnn_in['Wo'], 'L2_gnn_bo': _L2_gnn_in['bo'], 'L2_gnn_Wskip': _L2_gnn_in['Wskip'], 'L2_gnn_gamma': _L2_gnn_in['gamma'], 'L2_gnn_beta': _L2_gnn_in['beta'], 'L3_gnn_mlp_w1': _L3_gnn_in['mlp_w1'], 'L3_gnn_mlp_b1': _L3_gnn_in['mlp_b1'], 'L3_gnn_mlp_w2': _L3_gnn_in['mlp_w2'], 'L3_gnn_mlp_b2': _L3_gnn_in['mlp_b2'], 'L3_gnn_lin1_w': _L3_gnn_in['lin1_w'], 'L3_gnn_lin2_w': _L3_gnn_in['lin2_w'], 'L3_gnn_lin2_b': _L3_gnn_in['lin2_b'], 'L3_gnn_lin_w': _L3_gnn_in['lin_w'], 'L3_gnn_lin_b': _L3_gnn_in['lin_b']}

def reference(x, src, dst, edge_attr_50, edge_type_16, edge_weight, node_type_8, L0_gnn_W, L0_gnn_att_src, L0_gnn_att_dst, L0_gnn_gat_bias, L0_gnn_skip_W, L0_gnn_skip_b, L0_gnn_ln_g, L0_gnn_ln_b, L1_gnn_Wlin, L1_gnn_blin, L1_gnn_gamma, L1_gnn_beta, L1_gnn_Wg, L1_gnn_bg, L2_gnn_type_emb, L2_gnn_Wk, L2_gnn_Wq, L2_gnn_Wv, L2_gnn_rel_scale, L2_gnn_Wo, L2_gnn_bo, L2_gnn_Wskip, L2_gnn_gamma, L2_gnn_beta, L3_gnn_mlp_w1, L3_gnn_mlp_b1, L3_gnn_mlp_w2, L3_gnn_mlp_b2, L3_gnn_lin1_w, L3_gnn_lin2_w, L3_gnn_lin2_b, L3_gnn_lin_w, L3_gnn_lin_b):
    import jax
    import jax.numpy as jnp

    def _L0_gnn_ref(x, edge_index, W, att_src, att_dst, gat_bias, skip_W, skip_b, ln_g, ln_b):
        import jax, jax.numpy as jnp
        import numpy as np
        N = 6250
        E = 100000
        D_IN = 128
        D_OUT = 128
        HEADS = 4
        C = D_OUT // HEADS
        NEG_SLOPE = 0.2
        EPS_SOFTMAX = 1e-16
        EPS_LN = 1e-05

        def _gat_edge_conv(x, src, dst, W, att_src, att_dst, gat_bias, skip_W, skip_b, ln_g, ln_b):
            n = x.shape[0]
            h = (x @ W).reshape(n, HEADS, C)
            a_s = jnp.einsum('nhc,hc->nh', h, att_src)
            a_d = jnp.einsum('nhc,hc->nh', h, att_dst)
            e = jax.nn.leaky_relu(a_s[src] + a_d[dst], NEG_SLOPE)
            m = jax.ops.segment_max(e, dst, num_segments=n)
            p = jnp.exp(e - m[dst])
            z = jax.ops.segment_sum(p, dst, num_segments=n)
            alpha = p / (z[dst] + EPS_SOFTMAX)
            msg = h[src] * alpha[:, :, None]
            out = jax.ops.segment_sum(msg, dst, num_segments=n)
            out = out.reshape(n, HEADS * C) + gat_bias
            out = out + x @ skip_W + skip_b
            mu = out.mean(-1, keepdims=True)
            var = ((out - mu) ** 2).mean(-1, keepdims=True)
            return (out - mu) * jax.lax.rsqrt(var + EPS_LN) * ln_g + ln_b
        n = x.shape[0]
        loops = jnp.arange(n, dtype=edge_index.dtype)
        src = jnp.concatenate([edge_index[0], loops])
        dst = jnp.concatenate([edge_index[1], loops])
        return _gat_edge_conv(x, src, dst, W, att_src, att_dst, gat_bias, skip_W, skip_b, ln_g, ln_b)

    def _L1_gnn_ref(fea, edges, Wlin, blin, gamma, beta, Wg, bg):
        import jax, jax.numpy as jnp
        import numpy as np
        N = 6250
        E = 200000
        IN_DIM = 128
        OUT_DIM = 128
        BN_EPS = 1e-05
        LEAKY_SLOPE = 0.01
        n = fea.shape[0]
        x = fea @ Wlin.T + blin
        mean = jnp.mean(x, axis=0)
        var = jnp.var(x, axis=0)
        x = gamma * (x - mean) * jax.lax.rsqrt(var + BN_EPS) + beta
        x = jnp.where(x >= 0, x, LEAKY_SLOPE * x)
        h = x @ Wg.T
        self_idx = jnp.arange(n, dtype=edges.dtype)
        src = jnp.concatenate([edges[0], self_idx])
        dst = jnp.concatenate([edges[1], self_idx])
        deg = jax.ops.segment_sum(jnp.ones_like(dst, dtype=h.dtype), dst, num_segments=n)
        dinv = jnp.where(deg > 0, jax.lax.rsqrt(deg), 0.0)
        norm = dinv[src] * dinv[dst]
        msgs = norm[:, None] * h[src]
        out = jax.ops.segment_sum(msgs, dst, num_segments=n) + bg
        return jax.nn.log_softmax(out, axis=1)

    def _L2_gnn_ref(x, node_types, edge_src, edge_dst, edge_rel, type_emb, Wk, Wq, Wv, rel_scale, Wo, bo, Wskip, gamma, beta):
        import jax, jax.numpy as jnp
        import numpy as np
        N = 3125
        E = 31250
        IN_C = 128
        OUT_C = 128
        N_NODE_TYPES = 8
        N_EDGE_TYPES = 16
        H = 8
        DH = OUT_C // H
        LN_EPS = 1e-05

        def _hgt_forward(x, node_types, edge_src, edge_dst, edge_rel, type_emb, Wk, Wq, Wv, rel_scale, Wo, bo, Wskip, gamma, beta):
            n = x.shape[0]
            x_aug = jnp.concatenate([x, type_emb[node_types]], axis=-1)
            K = (x_aug @ Wk).reshape(n, H, DH)
            Q = (x_aug @ Wq).reshape(n, H, DH)
            V = (x_aug @ Wv).reshape(n, H, DH)
            attn = jnp.einsum('ehd,ehd->eh', Q[edge_dst], K[edge_src])
            attn = attn * rel_scale[edge_rel] / np.sqrt(DH)
            attn = attn - jax.lax.stop_gradient(jnp.max(attn))
            attn_exp = jnp.exp(attn)
            attn_sum = jax.ops.segment_sum(attn_exp, edge_dst, num_segments=n)
            attn_norm = attn_exp / (attn_sum[edge_dst] + 1e-16)
            msg = attn_norm[..., None] * V[edge_src]
            out = jax.ops.segment_sum(msg, edge_dst, num_segments=n).reshape(n, OUT_C)
            out = out @ Wo + bo
            skip = x_aug @ Wskip
            h = out + skip
            mu = jnp.mean(h, axis=-1, keepdims=True)
            var = jnp.mean(jnp.square(h - mu), axis=-1, keepdims=True)
            h = (h - mu) * jax.lax.rsqrt(var + LN_EPS) * gamma + beta
            return jax.nn.elu(h)
        return _hgt_forward(x, node_types, edge_src, edge_dst, edge_rel, type_emb, Wk, Wq, Wv, rel_scale, Wo, bo, Wskip, gamma, beta)

    def _L3_gnn_ref(x, edge_index, edge_weight, edge_attr, mlp_w1, mlp_b1, mlp_w2, mlp_b2, lin1_w, lin2_w, lin2_b, lin_w, lin_b):
        import jax, jax.numpy as jnp
        import numpy as np
        LN2 = float(np.log(2.0))

        def ssp(x):
            return jax.nn.softplus(x) - LN2
        N_NODES = 2500
        N_EDGES = 40000
        HIDDEN = 128
        N_FILTERS = 128
        N_GAUSS = 50
        CUTOFF = 10.0
        src, dst = (edge_index[0], edge_index[1])
        C = 0.5 * (jnp.cos(edge_weight * jnp.pi / CUTOFF) + 1.0)
        W = ssp(edge_attr @ mlp_w1.T + mlp_b1) @ mlp_w2.T + mlp_b2
        W = W * C[:, None]
        h = x @ lin1_w.T
        msg = h[src] * W
        agg = jax.ops.segment_sum(msg, dst, num_segments=x.shape[0])
        h2 = agg @ lin2_w.T + lin2_b
        out = ssp(h2) @ lin_w.T + lin_b
        return out
    edge_index = jnp.stack([src, dst])
    x = _layernorm(x + _L0_gnn_ref(x, edge_index, L0_gnn_W, L0_gnn_att_src, L0_gnn_att_dst, L0_gnn_gat_bias, L0_gnn_skip_W, L0_gnn_skip_b, L0_gnn_ln_g, L0_gnn_ln_b), axis=-1)
    x = _layernorm(x + _L1_gnn_ref(x, edge_index, L1_gnn_Wlin, L1_gnn_blin, L1_gnn_gamma, L1_gnn_beta, L1_gnn_Wg, L1_gnn_bg), axis=-1)
    x = _layernorm(x + _L2_gnn_ref(x, node_type_8, src, dst, edge_type_16, L2_gnn_type_emb, L2_gnn_Wk, L2_gnn_Wq, L2_gnn_Wv, L2_gnn_rel_scale, L2_gnn_Wo, L2_gnn_bo, L2_gnn_Wskip, L2_gnn_gamma, L2_gnn_beta), axis=-1)
    x = _layernorm(x + _L3_gnn_ref(x, edge_index, edge_weight, edge_attr_50, L3_gnn_mlp_w1, L3_gnn_mlp_b1, L3_gnn_mlp_w2, L3_gnn_mlp_b2, L3_gnn_lin1_w, L3_gnn_lin2_w, L3_gnn_lin2_b, L3_gnn_lin_w, L3_gnn_lin_b), axis=-1)
    return x

_drawn_inputs = setup_inputs


def setup_inputs(seed=0):
    import zlib

    import numpy as np

    out = dict(_drawn_inputs(seed))
    spreads = {'L0_gnn_ln_g': (1.0, 0.2),
     'L0_gnn_ln_b': (0.0, 0.1),
     'L1_gnn_gamma': (1.0, 0.2),
     'L1_gnn_beta': (0.0, 0.1),
     'L1_gnn_bg': (0.0, 0.1),
     'L2_gnn_rel_scale': (1.0, 0.6),
     'L2_gnn_bo': (0.0, 0.1),
     'L2_gnn_gamma': (1.0, 0.2),
     'L2_gnn_beta': (0.0, 0.1),
     'L3_gnn_mlp_b1': (0.0, 0.449),
     'L3_gnn_mlp_b2': (0.0, 0.1),
     'L3_gnn_lin2_b': (0.0, 0.318),
     'L3_gnn_lin_b': (0.0, 0.1)}
    factors = {'L0_gnn_gat_bias': 3.159, 'L0_gnn_skip_b': 3.548, 'L1_gnn_blin': 8.0}
    for name, (base, spread) in spreads.items():
        noise = np.random.default_rng([zlib.crc32(name.encode()), seed]).standard_normal(out[name].shape)
        drawn = base * np.exp(spread * noise) if base else spread * noise
        out[name] = jnp.asarray(drawn.astype(out[name].dtype))
    for name, factor in factors.items():
        out[name] = (out[name] * factor).astype(out[name].dtype)
    return out
```

```python
from contextlib import ExitStack

import numpy as np

import concourse.bass as bass
from concourse import mybir

F32 = mybir.dt.float32
BF16 = mybir.dt.bfloat16
I32 = mybir.dt.int32
U32 = mybir.dt.uint32
ALU = mybir.AluOpType
ACT = mybir.ActivationFunctionType
AX = mybir.AxisListType

P = 128
N = 6250
E = 206250
KT = 4
SLOTS = 4
ROUND = KT * SLOTS
NR = -(-E // (P * ROUND))
T = NR * ROUND
EP = T * P
CT = 5
CN = CT * P
NC = -(-(N + P) // CN)
NP = NC * CN
NT = NP // P
RW = ROUND * P
H0, C0 = 4, 32
H2, C2 = 8, 16
ROW0 = P + H0
Z0 = 2 * H0 + 1
NTYPE, NREL, NG = 8, 16, 50
BIG = 1e30
LN_EPS, BN_EPS, SM_EPS = 1e-5, 1e-5, 1e-16
LN2 = float(np.log(2.0))
SP_CAP = 20.0
TW = 6470


class Steps:

    def __init__(self, engine, sem, base=0):
        self.engine, self.sem, self.base, self.n = engine, sem, base, 0

    def link(self, ins):
        ins.then_inc(self.sem, 1)
        self.n += 1
        self.engine.wait_ge(self.sem, self.base + self.n)


class Arena:

    def __init__(self, tensor, lo, hi):
        self.t, self.at, self.hi = tensor, lo, hi

    def take(self, *dims, parts=P, dtype=F32):
        n = int(np.prod(dims))
        words = n if dtype in (F32, I32, U32) else -(-n // 2)
        v = self.t[0:parts, self.at:self.at + words]
        self.at += words
        assert self.at <= self.hi, (self.at, self.hi)
        if dtype != F32:
            v = v.bitcast(dtype)
        names = "abcd"[:len(dims)]
        if len(dims) == 1:
            return v
        return v.rearrange(f"p ({' '.join(names)}) -> p {' '.join(names)}", **dict(zip(names, dims)))


def over(ap, *shape):
    while len(ap.shape) < len(shape):
        ap = ap.unsqueeze(len(ap.shape))
    return ap.to_broadcast(list(shape))


def build(nc, a, out):
    ctx = ExitStack()
    with ctx:
        def sb(name, shape, dt=F32):
            return ctx.enter_context(nc.sbuf_tensor(name, shape, dt))

        layer_sems = []

        def sem(name):
            layer_sems.append(nc.alloc_semaphore(name=name))
            return layer_sems[-1]

        passed = {e: nc.alloc_semaphore(name=f"passed_{e}") for e in ("sync", "gpsimd", "scalar", "vector")}

        def met(engine):
            name = {nc.sync: "sync", nc.gpsimd: "gpsimd", nc.scalar: "scalar", nc.vector: "vector"}[engine]
            engine.sem_inc(passed[name], 1)

        def layer_ends():
            nc.clear_and_free_semaphores(layer_sems)
            layer_sems.clear()
            nc.all_engine_barrier()

        def sems(name, n=SLOTS):
            return [sem(f"{name}{b}") for b in range(n)]

        def scratch(name, shape, dt=F32):
            return nc.dram_tensor(name, shape, dt, kind="Internal").ap()

        lrow_d = scratch("local_dst_row", (1, EP))
        tab0_d = scratch("gat_table", (NP, ROW0))
        adt_d = scratch("gat_dst_scores", (NP, H0))
        tab1_d = scratch("gcn_table", (NP, P))
        kv_d = scratch("hgt_kv_table", (NP, 2 * P))
        q_d = scratch("hgt_q_table", (NP, P))
        tab3_d = scratch("schnet_table", (NP, P))
        edge_d = scratch("edge_rows", (P, T, P))

        xT = sb("xT", [P, NP])
        xn = sb("xn", [P, NT, P])
        AC = sb("AC", [P, T * 2 * H0])
        PM = sb("PM", [P, T * Z0])
        TMP = sb("TMP", [P, TW])
        lr = sb("lr", [P, T])
        first_i = sb("first_i", [1, T], I32)
        iota_f = sb("iota_f", [P, P])
        iota_p = sb("iota_p", [P, 1])
        ident = sb("ident", [P, P])
        ones = sb("ones", [P, P])
        padneg = sb("padneg", [P, ROUND])
        asd = sb("asd", [P, NT, 2 * H0])
        dinv = sb("dinv", [P, NT])
        degs = sb("degs", [P, 3, NT])
        deg, dgc, dgw = degs[:, 0, :], degs[:, 1, :], degs[:, 2, :]
        WA = sb("WA", [P, 3 * P])
        WB = sb("WB", [P, 5 * P])
        rows = sb("rows", [P, 3 * P])
        cols = sb("cols", [P, 16])
        typ = sb("typ", [P, 5 * P])
        headmap = sb("headmap", [H2, P])

        PS = [ctx.enter_context(nc.psum_tensor(f"ps{i}", [P, 2, 512], F32)) for i in range(4)]

        def psv(i, *dims, parts=P):
            v = PS[i][0:parts, :, :].rearrange("p a b -> p (a b)")
            n = int(np.prod(dims))
            names = "abcd"[:len(dims)]
            v = v[:, 0:n]
            return v if len(dims) == 1 else v.rearrange(
                f"p ({' '.join(names)}) -> p {' '.join(names)}", **dict(zip(names, dims)))

        as_e = AC[:, 0:T * H0].rearrange("p (t h) -> p t h", h=H0)
        ad_e = AC[:, T * H0:2 * T * H0].rearrange("p (t h) -> p t h", h=H0)
        pm0 = PM[:, :].rearrange("p (t z) -> p t z", z=Z0)
        pm2 = PM[:, 0:T * H2].rearrange("p (t z) -> p t z", z=H2)
        acc2 = AC[:, 0:2 * NP].rearrange("p (a n) -> p a n", a=2)
        acc1 = AC[:, 0:NP]
        hkeep = AC[:, NP:2 * NP].rearrange("p (t f) -> p t f", f=P)

        def table_rows(d, c, width):
            return d[bass.ds(c * CN, CN), 0:width].rearrange("(t p) f -> p t f", p=P)

        def row_bc(name, n=P, parts=P):
            return a[name].partition_broadcast(parts)

        def col_in(name):
            return a[name].rearrange("(f o) -> f o", o=1)

        load0, c0, v0, st0 = sem("start_loads"), sem("start_consts"), sem("start_dve"), sem("start_stores")
        A = Arena(TMP, 0, TW)
        B = Arena(PM, 0, T * Z0)
        dst_i = B.take(T, dtype=I32)
        dstf = B.take(T)
        firstb = B.take(T, dtype=I32)
        firstf = B.take(T)
        rows_i = A.take(ROUND, P, parts=NR, dtype=I32)
        rows_l = A.take(ROUND, P, parts=NR)
        iw = A.take(P, dtype=I32)
        ip = A.take(1, dtype=I32)
        with nc.Block() as block:
            @block.sync
            def _(sp):
                for dst, src in ((xT[:, :], a["xT"]), (dst_i, a["dst_et"]), (firstb, a["dst_first"][0].partition_broadcast(P)),
                                 (first_i[:, :], a["dst_first"]), (rows_i, a["dst_rows"].rearrange("p (a b) -> p a b", b=P))):
                    sp.dma_start(dst, src).then_inc(load0, 16)
                sp.wait_ge(v0, 100)
                met(sp)
                sp.dma_start(lrow_d.rearrange("o (p a b) -> (o p) a b", a=ROUND, b=P), rows_l).then_inc(st0, 16)
                sp.wait_ge(st0, 16)

            @block.gpsimd
            def _(pool):
                pool.memset(ident[:, :], 0.0).then_inc(c0, 1)
                pool.memset(ones[:, :], 1.0).then_inc(c0, 1)
                pool.memset(headmap[:, :], 1.0).then_inc(c0, 1)
                pool.iota(iw, [[1, P]], base=0, channel_multiplier=0).then_inc(c0, 1)
                pool.iota(ip, [[1, 1]], base=0, channel_multiplier=1).then_inc(c0, 1)
                pool.wait_ge(c0, 5)
                pool.affine_select(out=ident[:, :], in_=ident[:, :], compare_op=ALU.not_equal, fill=1.0, base=0,
                                   pattern=[[-1, P]], channel_multiplier=1).then_inc(c0, 1)
                pool.affine_select(out=headmap[:, :], in_=headmap[:, :], compare_op=ALU.is_ge, fill=0.0, base=0,
                                   pattern=[[1, P]], channel_multiplier=-C2).then_inc(c0, 1)
                pool.wait_ge(c0, 7)
                pool.affine_select(out=headmap[:, :], in_=headmap[:, :], compare_op=ALU.is_ge, fill=0.0, base=C2 - 1,
                                   pattern=[[-1, P]], channel_multiplier=C2).then_inc(c0, 1)

            @block.vector
            def _(dve):
                s = Steps(dve, v0)
                dve.wait_ge(load0, 80)
                dve.wait_ge(c0, 8)
                s.link(dve.tensor_copy(iota_f[:, :], iw))
                s.link(dve.tensor_copy(iota_p[:, :], ip))
                s.link(dve.tensor_copy(dstf, dst_i))
                s.link(dve.tensor_copy(firstf, firstb))
                s.link(dve.tensor_tensor(lr[:, :], dstf, firstf, ALU.subtract))
                s.link(dve.tensor_scalar(padneg[:, :], dstf[:, T - ROUND:T], float(N), -BIG, ALU.is_ge, ALU.mult))
                s.link(dve.tensor_tensor(rows_l, rows_i, rows_i[:, :, 0:1].to_broadcast([NR, ROUND, P]), ALU.subtract))
                dve.sem_inc(v0, 100 - s.n)
                s.n = 100

        def layer_norm(dve, s, t, q, sm, vr, rs, var_ready, rstd_ready, count):
            s.link(dve.tensor_reduce(sm, t, AX.X, ALU.add))
            s.link(dve.tensor_scalar(sm, sm, -1.0 / P, None, ALU.mult))
            s.link(dve.tensor_tensor(t, t, over(sm, P, CT, P), ALU.add))
            s.link(dve.tensor_tensor(q, t, t, ALU.mult))
            s.link(dve.tensor_reduce(vr, q, AX.X, ALU.add))
            s.link(dve.tensor_scalar(vr, vr, 1.0 / P, LN_EPS, ALU.mult, ALU.add))
            dve.sem_inc(var_ready, 1)
            dve.wait_ge(rstd_ready, count + 1)
            newton(dve, s, rs, vr, sm)
            s.link(dve.tensor_tensor(t, t, over(rs, P, CT, P), ALU.mult))

        def newton(dve, s, r, v, w):
            s.link(dve.tensor_tensor(w, r, r, ALU.mult))
            s.link(dve.tensor_tensor(w, w, v, ALU.mult))
            s.link(dve.tensor_scalar(w, w, -0.5, 1.5, ALU.mult, ALU.add))
            s.link(dve.tensor_tensor(r, r, w, ALU.mult))

        def rstd_act(act, ln_done, vr, rs, var_ready, rstd_ready, count, extra=0):
            act.wait_ge(var_ready, count + 1)
            nc.scalar.activation(rs, vr, ACT.Ln).then_inc(ln_done, 1)
            act.wait_ge(ln_done, count + 1 + extra)
            nc.scalar.activation(rs, rs, ACT.Exp, scale=-0.5).then_inc(rstd_ready, 1)

        def accumulate(dve, acc_step, n, window, part):
            for k in range(KT):
                first = dve.value_load(first_i[0:1, bass.ds(n * KT + k, 1)], min_val=0, max_val=N)
                w = window(first)
                dve.wait_ge(acc_step, n * KT + 8 + k)
                dve.tensor_tensor(w, w, part(k), ALU.add).then_inc(acc_step, 1)

        def onehot(dve, dst, n):
            return dve.tensor_tensor(
                dst, iota_f[:, :].unsqueeze(1).to_broadcast([P, KT, P]),
                over(lr[:, bass.ds(n * KT, KT)], P, KT, P), ALU.is_equal)

        ld = sem("gat_tables_loads")
        staged, mm, evac, used, hs = sem("gat_x_staged"), sem("gat_h_ready"), sem("gat_h_copied"), sem("gat_scores_ready"), sem("gat_dve")
        stored, row_free = sem("gat_rows_stored"), sem("gat_row_free")
        A = Arena(TMP, 0, TW)
        xs = A.take(CN)
        row = A.take(CT, ROW0)
        prod = A.take(CT, P)
        adb = A.take(CT, H0)
        W_gat = WA[:, 0:2 * P]
        with nc.Block() as block:
            @block.sync
            def _(sp):
                sp.dma_start(WA[:, 0:P], a["L0_gnn_W"]).then_inc(ld, 16)
                sp.dma_start(WA[:, P:2 * P], a["L0_gnn_skip_W"]).then_inc(ld, 16)
                sp.dma_start(rows[:, 0:P], row_bc("att_src")).then_inc(ld, 16)
                sp.dma_start(rows[:, P:2 * P], row_bc("att_dst")).then_inc(ld, 16)
                sp.sem_inc(row_free, 1)
                with sp.Fori(0, NC) as c:
                    sp.wait_ge(evac, c + 1)
                    met(sp)
                    sp.wait_ge(used, c + 2)
                    met(sp)
                    sp.dma_start(table_rows(tab0_d, c, ROW0), row).then_inc(stored, 16)
                    sp.dma_start(table_rows(adt_d, c, H0), adb).then_inc(stored, 16)
                    sp.wait_ge(stored, 32 * (c + 1))
                    sp.sem_inc(row_free, 1)

            @block.tensor
            def _(pe):
                pe.wait_ge(ld, 64)
                pe.sem_inc(mm, 1)
                with pe.Fori(0, NC) as c:
                    pe.wait_ge(staged, c + 1)
                    pe.wait_ge(used, c + 1)
                    ps = psv(0, CT, P)
                    for k in range(CT):
                        i = nc.tensor.matmul(ps[:, k, :], xs[:, k * P:(k + 1) * P], WA[:, 0:P], start=True, stop=True)
                    i.then_inc(mm, 1)

            @block.scalar
            def _(act):
                with act.Fori(0, NC) as c:
                    act.wait_ge(mm, c + 1)
                    met(act)
                    nc.scalar.copy(xs, xT[:, bass.ds(c * CN, CN)]).then_inc(staged, 1)
                    act.wait_ge(mm, c + 2)
                    act.wait_ge(row_free, c + 1)
                    nc.scalar.copy(row[:, :, 0:P], psv(0, CT, P)).then_inc(evac, 1)

            @block.vector
            def _(dve):
                dve.wait_ge(ld, 64)
                dve.sem_inc(used, 1)
                with dve.Fori(0, NC) as c:
                    s = Steps(dve, hs, c * 5)
                    dve.wait_ge(mm, c + 2)
                    dve.wait_ge(row_free, c + 1)
                    dve.wait_ge(evac, c + 1)
                    h = row[:, :, 0:P]
                    sc = asd[:, bass.ds(c * CT, CT), :]
                    for j, dstv in enumerate((row[:, :, P:ROW0], adb)):
                        s.link(dve.tensor_tensor(prod, h, rows[:, j * P:(j + 1) * P].unsqueeze(1).to_broadcast([P, CT, P]), ALU.mult))
                        s.link(dve.tensor_reduce(dstv, prod.rearrange("p t (h c) -> p t h c", c=C0), AX.X, ALU.add))
                    met(dve)
                    s.link(dve.tensor_copy(sc[:, :, 0:H0], row[:, :, P:ROW0]))
                    met(dve)
                    dve.tensor_copy(sc[:, :, H0:2 * H0], adb).then_inc(used, 1)

        idx_ready, gath, lr_ready, ad_ready, kept = sems("g1_idx"), sems("g1_gathered"), sems("g1_local_dst"), sems("g1_dst_rows"), sems("g1_kept")
        slot_free, as_copied, oh_done, ad_mm, ad_copied = sem("g1_slot_free"), sem("g1_src_scores"), sem("g1_onehot"), sem("g1_product"), sem("g1_dst_scores")
        A = Arena(TMP, 0, TW)
        idx = A.take(SLOTS, KT, dtype=U32)
        g = A.take(SLOTS, KT, ROW0)
        lrb = A.take(SLOTS, KT * P)
        ohT = A.take(2, KT * P)
        adw = A.take(SLOTS, KT, H0)
        with nc.Block() as block:
            @block.sync
            def _(sp):
                def load_idx(i, b):
                    sp.dma_start(idx[:, b, :], a["src_et"][:, bass.ds((i * SLOTS + b) * KT, KT)]).then_inc(idx_ready[b], 16)

                def load_local(i, b):
                    sp.dma_start(lrb[:, b, :], lrow_d[0, bass.ds((i * SLOTS + b) * KT * P, KT * P)].partition_broadcast(P)).then_inc(lr_ready[b], 16)

                def load_windows(i, b):
                    for k in range(KT):
                        first = sp.value_load(first_i[0:1, bass.ds((i * SLOTS + b) * KT + k, 1)], min_val=0, max_val=N)
                        sp.dma_start(adw[:, b, k, :], adt_d[bass.ds(first, P), :]).then_inc(ad_ready[b], 16)

                sp.sem_inc(slot_free, SLOTS)
                for b in range(SLOTS):
                    load_idx(0, b)
                    load_local(0, b)
                    load_windows(0, b)
                with sp.Fori(0, NR - 1) as i:
                    for b in range(SLOTS):
                        n = i * SLOTS + b
                        sp.wait_ge(gath[b], 16 * KT * (i + 1))
                        met(sp)
                        load_idx(i + 1, b)
                        sp.wait_ge(oh_done, n + 1)
                        met(sp)
                        load_local(i + 1, b)
                        sp.wait_ge(ad_mm, n + 3)
                        met(sp)
                        load_windows(i + 1, b)
                        sp.wait_ge(kept[b], 16 * (i + 1))
                        met(sp)
                        sp.wait_ge(as_copied, n + 1)
                        sp.sem_inc(slot_free, 1)
                for b in range(SLOTS):
                    sp.wait_ge(kept[b], 16 * NR)

            @block.gpsimd
            def _(pool):
                with pool.Fori(0, NR) as i:
                    for b in range(SLOTS):
                        pool.wait_ge(idx_ready[b], 16 * (i + 1))
                        pool.wait_ge(slot_free, i * SLOTS + b + 1)
                        met(pool)
                        for k in range(KT):
                            pool.indirect_dma_start(
                                out=g[:, b, k, :], out_offset=None, in_=tab0_d,
                                in_offset=bass.IndirectOffsetOnAxis(ap=idx[:, b, k:k + 1], axis=0)).then_inc(gath[b], 16)

            @block.scalar
            def _(act):
                with act.Fori(0, NR) as i:
                    for b in range(SLOTS):
                        t = (i * SLOTS + b) * KT
                        act.wait_ge(gath[b], 16 * KT * (i + 1))
                        met(act)
                        act.dma_start(edge_d[:, bass.ds(t, KT), :], g[:, b, :, 0:P]).then_inc(kept[b], 16)
                        nc.scalar.copy(as_e[:, bass.ds(t, KT), :], g[:, b, :, P:ROW0]).then_inc(as_copied, 1)

            @block.vector
            def _(dve):
                dve.sem_inc(ad_copied, 2)
                with dve.Fori(0, NR) as i:
                    for b in range(SLOTS):
                        n = i * SLOTS + b
                        dve.wait_ge(lr_ready[b], 16 * (i + 1))
                        dve.wait_ge(ad_mm, n + 1)
                        dve.tensor_scalar(ohT[:, b % 2, :], lrb[:, b, :], iota_p[:, 0:1], None, ALU.is_equal).then_inc(oh_done, 1)
                        dve.wait_ge(ad_mm, n + 3)
                        met(dve)
                        dve.tensor_copy(ad_e[:, bass.ds(n * KT, KT), :], psv(b % 2, KT, H0)).then_inc(ad_copied, 1)

            @block.tensor
            def _(pe):
                pe.sem_inc(ad_mm, 2)
                with pe.Fori(0, NR) as i:
                    for b in range(SLOTS):
                        n = i * SLOTS + b
                        pe.wait_ge(oh_done, n + 1)
                        pe.wait_ge(ad_ready[b], 16 * KT * (i + 1))
                        pe.wait_ge(ad_copied, n + 1)
                        ps = psv(b % 2, KT, H0)
                        for k in range(KT):
                            m = nc.tensor.matmul(ps[:, k, :], ohT[:, b % 2, k * P:(k + 1) * P], adw[:, b, k, :], start=True, stop=True)
                        m.then_inc(ad_mm, 1)

        ld, sd, rt, rc, bt, mt, pa, xld = (sem("seg_loads"), sem("seg_dve"), sem("seg_rows_t"), sem("seg_rows_copied"), sem("seg_carry_t"),
                                      sem("seg_max_t"), sem("seg_exp"), sem("seg_x_loaded"))
        mused, madd = sem("seg_max_used"), sem("seg_carry_ready")
        xn_flat = xn[:, :, :].rearrange("p t f -> p (t f)")
        A = Arena(xn_flat, 0, NP)
        negF = A.take(RW, parts=NR)
        negB = A.take(RW, parts=NR)
        R = A.take(RW, parts=NR)
        A = Arena(TMP, 0, TW)
        F = A.take(RW, parts=NR)
        Bk = A.take(RW, parts=NR)
        rowi = A.take(RW, parts=NR, dtype=I32)
        ends = A.take(4, parts=NR)
        carry = A.take(2, parts=NR)
        A = Arena(WB, 0, 5 * P)
        carry_r = A.take(2, NR + 1, parts=1)
        resets_r = A.take(2, NR, parts=1)
        ends_r = A.take(2, NR, parts=1)
        with nc.Block() as block:
            @block.sync
            def _(sp):
                sp.dma_start(rowi, a["dst_rows"]).then_inc(ld, 16)
                sp.dma_start(F.bitcast(I32), a["dst_prev_rows"]).then_inc(ld, 16)
                sp.dma_start(Bk.bitcast(I32), a["dst_next_rows"]).then_inc(ld, 16)

            @block.tensor
            def _(pe):
                for h in range(H0):
                    for q in range(ROUND // KT):
                        n = h * (ROUND // KT) + q
                        if n >= 2:
                            pe.wait_ge(rc, n - 1)
                        for k in range(KT):
                            m = nc.tensor.transpose(psv(n % 2, KT, P, parts=NR)[:, k, :], as_e[:, q * KT + k::ROUND, h], ident[:, :])
                        m.then_inc(rt, 1)
                    pe.wait_ge(madd, 3 * h + 1)
                    for j in range(2):
                        nc.tensor.matmul(PS[2][0:1, 0, j * P:j * P + NR], ends[:, j:j + 1], ident[0:NR, 0:NR], start=True, stop=True)
                        m = nc.tensor.matmul(PS[2][0:1, 1, j * P:j * P + NR], ends[:, 2 + j:3 + j], ident[0:NR, 0:NR], start=True, stop=True)
                    m.then_inc(bt, 1)
                    pe.wait_ge(madd, 3 * h + 2)
                    nc.tensor.matmul(PS[2][0:NR, 0, 256:257], carry_r[:, 0, 0:NR], ones[0:1, 0:1], start=True, stop=True)
                    nc.tensor.matmul(PS[2][0:NR, 0, 257:258], carry_r[:, 1, 1:NR + 1], ones[0:1, 0:1], start=True, stop=True).then_inc(bt, 1)
                    pe.wait_ge(madd, 3 * h + 3)
                    for q in range(ROUND // KT):
                        n = h * (ROUND // KT) + q
                        if n >= 1:
                            pe.wait_ge(mused, n)
                        for k in range(KT):
                            m = nc.tensor.transpose(PS[3][:, 0, k * NR:(k + 1) * NR], F[:, (q * KT + k) * P:(q * KT + k + 1) * P], ident[0:NR, 0:NR])
                        m.then_inc(mt, 1)

            @block.scalar
            def _(act):
                for h in range(H0):
                    for q in range(ROUND // KT):
                        n = h * (ROUND // KT) + q
                        act.wait_ge(rt, n + 1)
                        if q == 0 and h:
                            act.wait_ge(madd, 3 * h)
                        nc.scalar.copy(R[:, q * KT * P:(q + 1) * KT * P], psv(n % 2, KT * P, parts=NR)).then_inc(rc, 1)

            @block.vector
            def _(dve):
                s = Steps(dve, sd)
                dve.wait_ge(ld, 48)
                s.link(dve.tensor_tensor(negF, rowi, F.bitcast(I32), ALU.not_equal))
                s.link(dve.tensor_tensor(negB, rowi, Bk.bitcast(I32), ALU.not_equal))
                s.link(dve.tensor_scalar(negF, negF, -BIG, None, ALU.mult))
                s.link(dve.tensor_scalar(negB, negB, -BIG, None, ALU.mult))
                s.link(dve.tensor_reduce(ends[:, 2:3], negF, AX.X, ALU.min))
                s.link(dve.tensor_reduce(ends[:, 3:4], negB, AX.X, ALU.min))
                for h in range(H0):
                    dve.wait_ge(rc, (h + 1) * (ROUND // KT))
                    for final in range(2):
                        f0 = carry[:, 0:1] if final else -BIG
                        b0 = carry[:, 1:2] if final else -BIG
                        s.link(dve.tensor_tensor_scan(F, negF, R, f0, ALU.add, ALU.max))
                        s.link(dve.tensor_tensor_scan(Bk[:, ::-1], negB[:, ::-1], R[:, ::-1], b0, ALU.add, ALU.max))
                        if not final:
                            s.link(dve.tensor_copy(ends[:, 0:1], F[:, RW - 1:RW]))
                            s.link(dve.tensor_copy(ends[:, 1:2], Bk[:, 0:1]))
                            dve.sem_inc(madd, 1)
                            dve.wait_ge(bt, 2 * h + 1)
                            s.link(dve.tensor_copy(ends_r[:, :, 0:NR], PS[2][0:1, 0, 0:2 * P].rearrange("p (a b) -> p a b", a=2)[:, :, 0:NR]))
                            s.link(dve.tensor_copy(resets_r, PS[2][0:1, 1, 0:2 * P].rearrange("p (a b) -> p a b", a=2)[:, :, 0:NR]))
                            s.link(dve.memset(carry_r, -BIG))
                            s.link(dve.tensor_tensor_scan(carry_r[:, 0, 1:NR + 1], resets_r[:, 0, :], ends_r[:, 0, 0:NR], -BIG, ALU.add, ALU.max))
                            s.link(dve.tensor_tensor_scan(carry_r[:, 1, 0:NR][:, ::-1], resets_r[:, 1, :][:, ::-1], ends_r[:, 1, 0:NR][:, ::-1], -BIG, ALU.add, ALU.max))
                            dve.sem_inc(madd, 1)
                            dve.wait_ge(bt, 2 * h + 2)
                            s.link(dve.tensor_copy(carry, PS[2][0:NR, 0, 256:258]))
                    s.link(dve.tensor_tensor(F, F, Bk, ALU.max))
                    dve.sem_inc(madd, 1)
                    for q in range(ROUND // KT):
                        n = h * (ROUND // KT) + q
                        dve.wait_ge(mt, n + 1)
                        m = pm0[:, :, H0 + h].rearrange("p (r q) -> p q r", q=ROUND)[:, q * KT:(q + 1) * KT, :]
                        dve.tensor_copy(m, PS[3][:, 0, 0:KT * NR].rearrange("p (k r) -> p k r", r=NR)).then_inc(mused, 1)

        ld, sd, pa = sem("w_loads"), sem("w_dve"), sem("w_exp")
        A = Arena(TMP, 0, TW)
        di = A.take(T, dtype=I32)
        dp = A.take(T, dtype=I32)
        st = A.take(T)
        with nc.Block() as block:
            @block.sync
            def _(sp):
                sp.dma_start(di, a["dst_et"]).then_inc(ld, 16)
                sp.dma_start(dp, a["dst_prev_et"]).then_inc(ld, 16)
                sp.dma_start(xn[:, :, :], a["x"].rearrange("(t p) f -> p t f", p=P)).then_inc(ld, 16)
                sp.wait_ge(ld, 48)

            @block.vector
            def _(dve):
                s = Steps(dve, sd)
                pe_, me_ = pm0[:, :, 0:H0], pm0[:, :, H0:2 * H0]
                s.link(dve.tensor_tensor(as_e, as_e, ad_e, ALU.add))
                s.link(dve.scalar_tensor_tensor(pe_, as_e, 0.2, as_e, ALU.mult, ALU.max))
                s.link(dve.tensor_tensor(me_, me_, ad_e, ALU.add))
                s.link(dve.scalar_tensor_tensor(me_, me_, 0.2, me_, ALU.mult, ALU.max))
                s.link(dve.tensor_tensor(pe_, pe_, me_, ALU.subtract))
                dve.sem_inc(pa, 1)
                dve.wait_ge(ld, 48)
                s.link(dve.tensor_tensor(st, di, dp, ALU.not_equal))
                s.link(dve.tensor_tensor(me_, me_, over(st, P, T, H0), ALU.mult))
                s.link(dve.memset(pm0[:, :, 2 * H0:Z0], 1.0))

            @block.scalar
            def _(act):
                act.wait_ge(pa, 1)
                nc.scalar.activation(pm0[:, :, 0:H0], pm0[:, :, 0:H0], ACT.Exp).then_inc(pa, 1)

        def weighted_pass(tag, pm, heads, width, side):
            loaded, oh_done, msg_done, side_done, agg, acc_step = (sems(tag + "_rows"), sem(tag + "_onehot"), sem(tag + "_messages"),
                                                                   sem(tag + "_side"), sem(tag + "_sums"), sem(tag + "_added"))
            A = Arena(TMP, 0, TW)
            g = A.take(SLOTS, KT, P)
            msg = A.take(2, KT, P)
            oh = A.take(2, KT, P)
            sd = A.take(SLOTS, KT, side)
            with nc.Block() as block:
                @block.sync
                def _(sp):
                    def load(i, b):
                        sp.dma_start(g[:, b, :, :], edge_d[:, bass.ds((i * SLOTS + b) * KT, KT), :]).then_inc(loaded[b], 16)
                    for b in range(SLOTS):
                        load(0, b)
                    with sp.Fori(0, NR - 1) as i:
                        for b in range(SLOTS):
                            sp.wait_ge(msg_done, i * SLOTS + b + 1)
                            met(sp)
                            load(i + 1, b)

                @block.scalar
                def _(act):
                    with act.Fori(0, NR) as i:
                        for b in range(SLOTS):
                            n = i * SLOTS + b
                            act.wait_ge(agg, n + 1)
                            met(act)
                            nc.scalar.copy(sd[:, b, :, :], pm[:, bass.ds(n * KT, KT), :]).then_inc(side_done, 1)

                @block.tensor
                def _(pe):
                    pe.sem_inc(agg, SLOTS)
                    with pe.Fori(0, NR) as i:
                        for b in range(SLOTS):
                            n = i * SLOTS + b
                            pe.wait_ge(oh_done, n + 1)
                            pe.wait_ge(msg_done, n + 1)
                            pe.wait_ge(side_done, n + 1)
                            pe.wait_ge(acc_step, n * KT + 4)
                            for k in range(KT):
                                o = oh[:, b % 2, k, :]
                                nc.tensor.matmul(PS[b % 2][:, 0, k * P:(k + 1) * P], msg[:, b % 2, k, :], o, start=True, stop=True)
                                m = nc.tensor.matmul(PS[b % 2][0:side, 1, k * P:(k + 1) * P], sd[:, b, k, :], o, start=True, stop=True)
                            m.then_inc(agg, 1)

                @block.vector
                def _(dve):
                    def messages(i, b):
                        n = i * SLOTS + b
                        dve.wait_ge(agg, n + 3)
                        onehot(dve, oh[:, b % 2, :, :], n).then_inc(oh_done, 1)
                        dve.wait_ge(loaded[b], 16 * (i + 1))
                        dve.tensor_tensor(
                            msg[:, b % 2, :, :].rearrange("p k (h c) -> p k h c", c=width),
                            g[:, b, :, :].rearrange("p k (h c) -> p k h c", c=width),
                            over(pm[:, bass.ds(n * KT, KT), 0:heads], P, KT, heads, width), ALU.mult).then_inc(msg_done, 1)

                    def add(i, b):
                        n = i * SLOTS + b
                        dve.wait_ge(agg, n + 5)
                        accumulate(dve, acc_step, n, lambda first: acc2[:, :, bass.ds(first, P)],
                                   lambda k: PS[b % 2][:, :, k * P:(k + 1) * P])

                    def round_(i, last):
                        for b in range(SLOTS):
                            if b < SLOTS - 1:
                                messages(i, b + 1)
                            elif not last:
                                messages(i + 1, 0)
                            add(i, b)

                    dve.memset(AC[:, 0:2 * NP], 0.0).then_inc(acc_step, 1)
                    for j in range(2):
                        dve.memset(PS[j][:, 1, :], 0.0).then_inc(acc_step, 1)
                    dve.sem_inc(acc_step, 5)
                    messages(0, 0)
                    with dve.Fori(0, NR - 1) as i:
                        round_(i, False)
                    round_(NR - 1, True)

        weighted_pass("gat_sum", pm0, H0, C0, Z0)

        ld, staged, mm, used, fs, acts, vrdy, rrdy, lnd, xt, xc = (sem("gat_end_loads"), sem("gat_end_staged"), sem("gat_end_products"), sem("gat_end_used"),
            sem("gat_end_dve"), sem("gat_end_exp"), sem("gat_end_var"), sem("gat_end_rstd"), sem("gat_end_ln"), sem("gat_end_x_t"), sem("gat_end_x_copied"))
        A = Arena(TMP, 0, TW)
        xs = A.take(CN)
        ac = A.take(CN)
        zc = A.take(CN)
        t = A.take(CT, P)
        q = A.take(CT, P)
        z = A.take(CT, Z0)
        sv = A.take(CT, H0)
        sm, vr, rs = A.take(CT), A.take(CT), A.take(CT)
        A = Arena(PM, 0, T * Z0)
        rb = A.take(4, P)
        bsum = A.take(P)

        def residual_out(dve, s, t, q, sm, vr, rs, vrdy, rrdy, c, per, j, xnew):
            s.link(dve.tensor_tensor(t, t, xn[:, bass.ds(c * CT, CT), :], ALU.add))
            layer_norm(dve, s, t, q, sm, vr, rs, vrdy, rrdy, c * per + j)
            met(dve)
            s.link(dve.tensor_copy(xn[:, bass.ds(c * CT, CT), :], t))

        with nc.Block() as block:
            @block.sync
            def _(sp):
                for j, n_ in enumerate(("L0_gnn_gat_bias", "L0_gnn_skip_b", "L0_gnn_ln_g", "L0_gnn_ln_b")):
                    sp.dma_start(rb[:, j, :], row_bc(n_)).then_inc(ld, 16)
                sp.wait_ge(ld, 64)

            @block.scalar
            def _(act):
                with act.Fori(0, NC) as c:
                    act.wait_ge(mm, c + 1)
                    met(act)
                    nc.scalar.copy(xs, xT[:, bass.ds(c * CN, CN)]).then_inc(staged, 1)
                    nc.scalar.copy(ac, acc2[:, 0, bass.ds(c * CN, CN)]).then_inc(staged, 1)
                    nc.scalar.copy(zc[0:Z0, :], acc2[0:Z0, 1, bass.ds(c * CN, CN)]).then_inc(staged, 1)
                    act.wait_ge(acts, 2 * c + 1)
                    nc.scalar.activation(sv, sv, ACT.Exp).then_inc(acts, 1)
                    for j in range(2):
                        rstd_act(act, lnd, vr, rs, vrdy, rrdy, 2 * c + j)
                    act.wait_ge(xt, c + 1)
                    met(act)
                    nc.scalar.copy(xT[:, bass.ds(c * CN, CN)], psv(0, CN)).then_inc(xc, 1)

            @block.tensor
            def _(pe):
                pe.sem_inc(mm, 1)
                pe.sem_inc(xc, 1)
                with pe.Fori(0, NC) as c:
                    pe.wait_ge(staged, 3 * c + 3)
                    pe.wait_ge(xc, c + 1)
                    for k in range(CT):
                        w = slice(k * P, (k + 1) * P)
                        nc.tensor.transpose(psv(0, CT, P)[:, k, :], ac[:, w], ident[:, :])
                        nc.tensor.matmul(psv(1, CT, P)[:, k, :], xs[:, w], WA[:, 0:P], start=True, stop=True)
                        nc.tensor.matmul(psv(2, CT, P)[:, k, :], xs[:, w], WA[:, P:2 * P], start=True, stop=True)
                        m = nc.tensor.transpose(psv(3, CT, Z0)[:, k, :], zc[0:Z0, w], ident[0:Z0, 0:Z0])
                    m.then_inc(mm, 1)
                    pe.wait_ge(used, c + 1)
                    for k in range(CT):
                        m = nc.tensor.transpose(psv(0, CT, P)[:, k, :], t[:, k, :], ident[:, :])
                    m.then_inc(xt, 1)

            @block.vector
            def _(dve):
                s = Steps(dve, fs)
                dve.wait_ge(ld, 64)
                s.link(dve.tensor_tensor(bsum, rb[:, 0, :], rb[:, 1, :], ALU.add))
                per = 50
                with dve.Fori(0, NC) as c:
                    s = Steps(dve, fs, c * per + 1)
                    dve.wait_ge(mm, c + 2)
                    dve.wait_ge(xc, c + 1)
                    heads = "p t (h c) -> p t h c"
                    a_s, a_d = asd[:, bass.ds(c * CT, CT), 0:H0], asd[:, bass.ds(c * CT, CT), H0:2 * H0]
                    s.link(dve.tensor_copy(z, psv(3, CT, Z0)))
                    s.link(dve.tensor_scalar(deg[:, bass.ds(c * CT, CT)], z[:, :, 2 * H0], 1.0, None, ALU.add))
                    s.link(dve.tensor_tensor(sv, a_s, a_d, ALU.add))
                    s.link(dve.scalar_tensor_tensor(sv, sv, 0.2, sv, ALU.mult, ALU.max))
                    s.link(dve.tensor_tensor(sv, sv, z[:, :, H0:2 * H0], ALU.subtract))
                    dve.sem_inc(acts, 1)
                    dve.wait_ge(acts, 2 * c + 2)
                    s.link(dve.tensor_tensor(z[:, :, 0:H0], z[:, :, 0:H0], sv, ALU.add))
                    s.link(dve.tensor_tensor(t.rearrange(heads, c=C0), psv(1, CT, P).rearrange(heads, c=C0), over(sv, P, CT, H0, C0), ALU.mult))
                    s.link(dve.tensor_tensor(t, t, psv(0, CT, P), ALU.add))
                    s.link(dve.tensor_scalar(z[:, :, 0:H0], z[:, :, 0:H0], SM_EPS, None, ALU.add))
                    s.link(dve.reciprocal(sv, z[:, :, 0:H0]))
                    s.link(dve.tensor_tensor(t.rearrange(heads, c=C0), t.rearrange(heads, c=C0), over(sv, P, CT, H0, C0), ALU.mult))
                    s.link(dve.tensor_tensor(t, t, psv(2, CT, P), ALU.add))
                    s.link(dve.tensor_tensor(t, t, bsum.unsqueeze(1).to_broadcast([P, CT, P]), ALU.add))
                    layer_norm(dve, s, t, q, sm, vr, rs, vrdy, rrdy, 2 * c)
                    s.link(dve.tensor_tensor(t, t, rb[:, 2, :].unsqueeze(1).to_broadcast([P, CT, P]), ALU.mult))
                    s.link(dve.tensor_tensor(t, t, rb[:, 3, :].unsqueeze(1).to_broadcast([P, CT, P]), ALU.add))
                    residual_out(dve, s, t, q, sm, vr, rs, vrdy, rrdy, c, 2, 1, xn)
                    dve.sem_inc(fs, per - s.n)
                    dve.sem_inc(used, 1)


        layer_ends()

        ld, staged, mm, lin, bs, bact, used, stored, row_free = (sem("gcn_loads"), sem("gcn_staged"), sem("gcn_products"), sem("gcn_linear"),
            sem("gcn_dve"), sem("gcn_act"), sem("gcn_used"), sem("gcn_stored"), sem("gcn_row_free"))
        A = Arena(TMP, 0, TW)
        ys = A.take(CN)
        hrow = A.take(CT, P)
        A = Arena(PM, 0, T * Z0)
        x1 = A.take(NP)
        sq = A.take(N)
        with nc.Block() as block:
            @block.sync
            def _(sp):
                for j, n_ in enumerate(("L1_gnn_Wlin_T", "L1_gnn_Wg_T")):
                    sp.dma_start(WA[:, j * P:(j + 1) * P], a[n_]).then_inc(ld, 16)
                for j, n_ in enumerate(("L1_gnn_blin", "L1_gnn_gamma", "L1_gnn_beta")):
                    sp.dma_start(cols[:, j:j + 1], col_in(n_)).then_inc(ld, 16)
                sp.sem_inc(row_free, 1)
                with sp.Fori(0, NC) as c:
                    sp.wait_ge(used, c + 2)
                    met(sp)
                    sp.dma_start(table_rows(tab1_d, c, P), hrow).then_inc(stored, 16)
                    sp.wait_ge(stored, 16 * (c + 1))
                    sp.sem_inc(row_free, 1)

            @block.tensor
            def _(pe):
                pe.wait_ge(ld, 80)
                half = CN // 2
                with pe.Fori(0, NC) as c:
                    pe.wait_ge(lin, c + 1)
                    for j in range(2):
                        m = nc.tensor.matmul(PS[0][:, j, 0:half], WA[:, 0:P], xT[:, bass.ds(c * CN + j * half, half)], start=True, stop=True)
                    m.then_inc(mm, 1)
                with pe.Fori(0, NC) as c:
                    pe.wait_ge(staged, c + 1)
                    pe.wait_ge(used, c + 1)
                    for k in range(CT):
                        m = nc.tensor.matmul(psv(1, CT, P)[:, k, :], ys[:, k * P:(k + 1) * P], WA[:, P:2 * P], start=True, stop=True)
                    m.then_inc(mm, 1)

            @block.scalar
            def _(act):
                half = CN // 2
                act.sem_inc(lin, 1)
                act.wait_ge(ld, 80)
                with act.Fori(0, NC) as c:
                    act.wait_ge(mm, c + 1)
                    met(act)
                    nc.scalar.activation(x1[:, bass.ds(c * CN, CN)].rearrange("p (a b) -> p a b", a=2), PS[0][:, :, 0:half],
                                         ACT.Identity, bias=cols[:, 0:1]).then_inc(lin, 1)
                act.wait_ge(bs, 3)
                nc.scalar.activation(sq, x1[:, 0:N], ACT.Square, accum_out=cols[:, 4:5]).then_inc(bact, 1)
                act.wait_ge(bs, 5)
                nc.scalar.activation(cols[:, 6:7], cols[:, 5:6], ACT.Ln).then_inc(bact, 1)
                nc.scalar.activation(dinv[:, :], deg, ACT.Ln).then_inc(bact, 1)
                act.wait_ge(bact, 3)
                nc.scalar.activation(cols[:, 6:7], cols[:, 6:7], ACT.Exp, scale=-0.5).then_inc(bact, 1)
                nc.scalar.activation(dinv[:, :], dinv[:, :], ACT.Exp, scale=-0.5).then_inc(bact, 1)
                act.wait_ge(bs, 16)
                with act.Fori(0, NC) as c:
                    act.wait_ge(mm, NC + c)
                    met(act)
                    nc.scalar.copy(ys, x1[:, bass.ds(c * CN, CN)]).then_inc(staged, 1)

            @block.vector
            def _(dve):
                s = Steps(dve, bs)
                dve.wait_ge(lin, NC + 1)
                s.link(dve.tensor_reduce(cols[:, 3:4], x1[:, 0:N], AX.X, ALU.add))
                s.link(dve.tensor_scalar(cols[:, 3:4], cols[:, 3:4], -1.0 / N, None, ALU.mult))
                s.link(dve.tensor_scalar(x1, x1, cols[:, 3:4], None, ALU.add))
                dve.wait_ge(bact, 1)
                s.link(dve.tensor_scalar(cols[:, 5:6], cols[:, 4:5], 1.0 / N, BN_EPS, ALU.mult, ALU.add))
                s.link(dve.tensor_copy(dgc, deg))
                dve.wait_ge(bact, 5)
                newton(dve, s, cols[:, 6:7], cols[:, 5:6], cols[:, 7:8])
                newton(dve, s, dinv[:, :], dgc, dgw)
                s.link(dve.tensor_tensor(cols[:, 6:7], cols[:, 6:7], cols[:, 1:2], ALU.mult))
                s.link(dve.tensor_scalar(x1, x1, cols[:, 6:7], cols[:, 2:3], ALU.mult, ALU.add))
                s.link(dve.scalar_tensor_tensor(x1, x1, 0.01, x1, ALU.mult, ALU.max))
                assert s.n == 16
                dve.sem_inc(used, 1)
                with dve.Fori(0, NC) as c:
                    s = Steps(dve, bs, c + 16)
                    dve.wait_ge(mm, NC + c + 1)
                    dve.wait_ge(row_free, c + 1)
                    s.link(dve.tensor_tensor(hrow, psv(1, CT, P), over(dinv[:, bass.ds(c * CT, CT)], P, CT, P), ALU.mult))
                    met(dve)
                    dve.tensor_copy(hkeep[:, bass.ds(c * CT, CT), :], hrow).then_inc(used, 1)

        def gather_engines(block, tag, table, width, idx, g, idx_ready, gath, agg):
            @block.sync
            def _(sp):
                def load_idx(i, b):
                    sp.dma_start(idx[:, b, :], a["src_et"][:, bass.ds((i * SLOTS + b) * KT, KT)]).then_inc(idx_ready[b], 16)
                for b in range(SLOTS):
                    load_idx(0, b)
                with sp.Fori(0, NR - 1) as i:
                    for b in range(SLOTS):
                        sp.wait_ge(gath[b], 16 * KT * (i + 1))
                        met(sp)
                        load_idx(i + 1, b)

            @block.gpsimd
            def _(pool):
                with pool.Fori(0, NR) as i:
                    for b in range(SLOTS):
                        pool.wait_ge(idx_ready[b], 16 * (i + 1))
                        pool.wait_ge(agg, i * SLOTS + b + 1)
                        met(pool)
                        for k in range(KT):
                            pool.indirect_dma_start(
                                out=g[:, b, k, :], out_offset=None, in_=table,
                                in_offset=bass.IndirectOffsetOnAxis(ap=idx[:, b, k:k + 1], axis=0)).then_inc(gath[b], 16)

        idx_ready, gath, oh_done, agg, acc_step = sems("gcn_idx"), sems("gcn_gathered"), sem("gcn_onehot"), sem("gcn_sums"), sem("gcn_added")
        A = Arena(TMP, 0, TW)
        idx = A.take(SLOTS, KT, dtype=U32)
        g = A.take(SLOTS, KT, P)
        oh = A.take(2, KT, P)
        with nc.Block() as block:
            gather_engines(block, "gcn", tab1_d, P, idx, g, idx_ready, gath, agg)

            @block.tensor
            def _(pe):
                pe.sem_inc(agg, SLOTS)
                with pe.Fori(0, NR) as i:
                    for b in range(SLOTS):
                        n = i * SLOTS + b
                        pe.wait_ge(oh_done, n + 1)
                        pe.wait_ge(gath[b], 16 * KT * (i + 1))
                        pe.wait_ge(acc_step, n * KT + 4)
                        for k in range(KT):
                            m = nc.tensor.matmul(PS[b % 2][:, 0, k * P:(k + 1) * P], g[:, b, k, :], oh[:, b % 2, k, :], start=True, stop=True)
                        m.then_inc(agg, 1)

            @block.vector
            def _(dve):
                def prepare(n, b):
                    dve.wait_ge(agg, n + 3)
                    onehot(dve, oh[:, b % 2, :, :], n).then_inc(oh_done, 1)

                def round_(i, last):
                    for b in range(SLOTS):
                        n = i * SLOTS + b
                        if b < SLOTS - 1 or not last:
                            prepare(n + 1, b + 1)
                        dve.wait_ge(agg, n + 5)
                        accumulate(dve, acc_step, n, lambda first: AC[:, bass.ds(first, P)],
                                   lambda k: PS[b % 2][:, 0, k * P:(k + 1) * P])

                dve.memset(acc1, 0.0).then_inc(acc_step, 1)
                dve.sem_inc(acc_step, 7)
                prepare(0, 0)
                with dve.Fori(0, NR - 1) as i:
                    round_(i, False)
                round_(NR - 1, True)

        ld, staged, mm, used, fs, acts, vrdy, rrdy, lnd, xt, xc = (sem("gcn_end_loads"), sem("gcn_end_staged"), sem("gcn_end_products"), sem("gcn_end_used"),
            sem("gcn_end_dve"), sem("gcn_end_exp"), sem("gcn_end_var"), sem("gcn_end_rstd"), sem("gcn_end_ln"), sem("gcn_end_x_t"), sem("gcn_end_x_copied"))
        A = Arena(TMP, 0, TW)
        ac = A.take(CN)
        t = A.take(CT, P)
        q = A.take(CT, P)
        sm, vr, rs, ls = A.take(CT), A.take(CT), A.take(CT), A.take(CT)
        bg = A.take(P)
        with nc.Block() as block:
            @block.sync
            def _(sp):
                sp.dma_start(bg, row_bc("L1_gnn_bg")).then_inc(ld, 16)
                sp.wait_ge(ld, 16)

            @block.scalar
            def _(act):
                with act.Fori(0, NC) as c:
                    act.wait_ge(mm, c + 1)
                    met(act)
                    nc.scalar.copy(ac, AC[:, bass.ds(c * CN, CN)]).then_inc(staged, 1)
                    act.wait_ge(acts, 4 * c + 1)
                    nc.scalar.activation(q, t, ACT.Exp).then_inc(acts, 1)
                    act.wait_ge(acts, 4 * c + 3)
                    nc.scalar.activation(ls, ls, ACT.Ln).then_inc(acts, 1)
                    rstd_act(act, lnd, vr, rs, vrdy, rrdy, c)
                    act.wait_ge(xt, c + 1)
                    met(act)
                    nc.scalar.copy(xT[:, bass.ds(c * CN, CN)], psv(1, CN)).then_inc(xc, 1)

            @block.tensor
            def _(pe):
                pe.sem_inc(mm, 1)
                pe.sem_inc(xc, 1)
                with pe.Fori(0, NC) as c:
                    pe.wait_ge(staged, c + 1)
                    for k in range(CT):
                        m = nc.tensor.transpose(psv(0, CT, P)[:, k, :], ac[:, k * P:(k + 1) * P], ident[:, :])
                    m.then_inc(mm, 1)
                    pe.wait_ge(used, c + 1)
                    pe.wait_ge(xc, c + 1)
                    for k in range(CT):
                        m = nc.tensor.transpose(psv(1, CT, P)[:, k, :], t[:, k, :], ident[:, :])
                    m.then_inc(xt, 1)

            @block.vector
            def _(dve):
                dve.wait_ge(ld, 16)
                per = 30
                with dve.Fori(0, NC) as c:
                    s = Steps(dve, fs, c * per)
                    dve.wait_ge(mm, c + 2)
                    dve.wait_ge(xc, c + 1)
                    s.link(dve.tensor_tensor(t, psv(0, CT, P), hkeep[:, bass.ds(c * CT, CT), :], ALU.add))
                    s.link(dve.tensor_tensor(t, t, over(dinv[:, bass.ds(c * CT, CT)], P, CT, P), ALU.mult))
                    s.link(dve.tensor_tensor(t, t, bg.unsqueeze(1).to_broadcast([P, CT, P]), ALU.add))
                    s.link(dve.tensor_reduce(sm, t, AX.X, ALU.max))
                    s.link(dve.tensor_tensor(t, t, over(sm, P, CT, P), ALU.subtract))
                    dve.sem_inc(acts, 1)
                    dve.wait_ge(acts, 4 * c + 2)
                    s.link(dve.tensor_reduce(ls, q, AX.X, ALU.add))
                    dve.sem_inc(acts, 1)
                    dve.wait_ge(acts, 4 * c + 4)
                    s.link(dve.tensor_tensor(t, t, over(ls, P, CT, P), ALU.subtract))
                    residual_out(dve, s, t, q, sm, vr, rs, vrdy, rrdy, c, 1, 0, xn)
                    dve.sem_inc(fs, per - s.n)
                    dve.sem_inc(used, 1)

        layer_ends()

        ld, ts, td = sem("hgt_prep_loads"), sem("hgt_prep_type"), sem("hgt_prep_dve")
        T8kvq, T8s = WA[0:NTYPE, 0:3 * P], rows[0:NTYPE, 0:P]
        embT = TMP[:, 0:NTYPE]
        rel = cols[0:NREL, 0:H2]
        names = ("L2_gnn_Wk", "L2_gnn_Wv", "L2_gnn_Wq", "L2_gnn_Wskip")
        with nc.Block() as block:
            @block.sync
            def _(sp):
                for j, n_ in enumerate(names):
                    sp.dma_start(WB[:, j * P:(j + 1) * P], a[n_][0:P, :]).then_inc(ld, 16)
                    sp.dma_start(typ[:, j * P:(j + 1) * P], a[n_][P:2 * P, :]).then_inc(ld, 16)
                sp.dma_start(WB[:, 4 * P:5 * P], a["L2_gnn_Wo"]).then_inc(ld, 16)
                sp.dma_start(embT, a["L2_gnn_type_emb_T"]).then_inc(ld, 16)
                sp.dma_start(rel, a["L2_gnn_rel_scale"]).then_inc(ld, 16)
                sp.wait_ge(ld, 16 * 11)

            @block.tensor
            def _(pe):
                pe.wait_ge(ld, 16 * 11)
                nc.tensor.matmul(PS[0][0:NTYPE, 0, :], embT, typ[:, 0:4 * P], start=True, stop=True).then_inc(ts, 1)

            @block.vector
            def _(dve):
                dve.wait_ge(ts, 1)
                s = Steps(dve, td)
                s.link(dve.tensor_copy(T8kvq, PS[0][0:NTYPE, 0, 0:3 * P]))
                s.link(dve.tensor_copy(T8s, PS[0][0:NTYPE, 0, 3 * P:4 * P]))
                s.link(dve.tensor_scalar(rel, rel, 1.0 / float(np.sqrt(C2)), None, ALU.mult))

        tld, staged, mm, evac, ohd, stored, row_free = (sem("hgt_type_loads"), sem("hgt_staged"), sem("hgt_products"), sem("hgt_copied"),
            sem("hgt_type_onehot"), sem("hgt_stored"), sem("hgt_row_free"))
        A = Arena(TMP, 0, TW)
        xs = A.take(CN)
        kvq = A.take(CT, 3 * P)
        nt8 = A.take(CN, parts=NTYPE, dtype=I32)
        oh8 = A.take(CN, parts=NTYPE)

        def load_types(sp, c, tld):
            sp.dma_start(nt8, a["type_row"][0, bass.ds(c * CN, CN)].partition_broadcast(NTYPE)).then_inc(tld, 16)

        with nc.Block() as block:
            @block.sync
            def _(sp):
                sp.sem_inc(row_free, 1)
                with sp.Fori(0, NC) as c:
                    sp.wait_ge(row_free, c + 1)
                    met(sp)
                    load_types(sp, c, tld)
                    sp.wait_ge(evac, 3 * (c + 1))
                    met(sp)
                    sp.dma_start(table_rows(kv_d, c, 2 * P), kvq[:, :, 0:2 * P]).then_inc(stored, 16)
                    sp.dma_start(table_rows(q_d, c, P), kvq[:, :, 2 * P:3 * P]).then_inc(stored, 16)
                    sp.wait_ge(stored, 32 * (c + 1))
                    sp.sem_inc(row_free, 1)

            @block.vector
            def _(dve):
                with dve.Fori(0, NC) as c:
                    dve.wait_ge(tld, 16 * (c + 1))
                    dve.wait_ge(mm, c + 1)
                    dve.tensor_scalar(oh8, nt8, iota_p[0:NTYPE, 0:1], None, ALU.is_equal).then_inc(ohd, 1)

            @block.scalar
            def _(act):
                with act.Fori(0, NC) as c:
                    act.wait_ge(mm, c + 1)
                    met(act)
                    nc.scalar.copy(xs, xT[:, bass.ds(c * CN, CN)]).then_inc(staged, 1)
                    act.wait_ge(mm, c + 2)
                    act.wait_ge(row_free, c + 1)
                    for j in range(2):
                        nc.scalar.copy(kvq[:, 2 * j:2 * j + 2, :], PS[j][:, :, 0:3 * P]).then_inc(evac, 1)
                    nc.scalar.copy(kvq[:, 4, :], PS[2][:, 0, 0:3 * P]).then_inc(evac, 1)

            @block.tensor
            def _(pe):
                pe.sem_inc(mm, 1)
                with pe.Fori(0, NC) as c:
                    pe.wait_ge(staged, c + 1)
                    pe.wait_ge(ohd, c + 1)
                    for k in range(CT):
                        ps = PS[k // 2][:, k % 2, 0:3 * P]
                        nc.tensor.matmul(ps, xs[:, k * P:(k + 1) * P], WB[:, 0:3 * P], start=True, stop=False)
                        m = nc.tensor.matmul(ps, oh8[:, k * P:(k + 1) * P], T8kvq, start=False, stop=True)
                    m.then_inc(mm, 1)

        idx_ready, gath, lr_ready, q_ready, kept, rel_ready = (sems("h1_idx"), sems("h1_gathered"), sems("h1_local_dst"), sems("h1_q_rows"),
                                                               sems("h1_kept"), sems("h1_relations"))
        slot_free, oh_done, q_mm, q_used, scored = sem("h1_slot_free"), sem("h1_onehot"), sem("h1_product"), sem("h1_q_used"), sem("h1_dve")
        A = Arena(AC, 0, T * 2 * H0)
        g = A.take(SLOTS, KT, 2 * P)
        qw = A.take(SLOTS, KT, P)
        lrb = A.take(SLOTS, KT * P)
        relb = A.take(SLOTS, KT * P, parts=NREL, dtype=I32)
        ohT = A.take(2, KT * P)
        A = Arena(TMP, 0, TW)
        idx = A.take(SLOTS, KT, dtype=U32)
        oh16 = A.take(2, KT * P, parts=NREL)
        prod = A.take(KT, P)
        dot = A.take(KT, H2)
        with nc.Block() as block:
            @block.sync
            def _(sp):
                def load_idx(i, b):
                    sp.dma_start(idx[:, b, :], a["src_et"][:, bass.ds((i * SLOTS + b) * KT, KT)]).then_inc(idx_ready[b], 16)

                def load_local(i, b):
                    at = bass.ds((i * SLOTS + b) * KT * P, KT * P)
                    sp.dma_start(lrb[:, b, :], lrow_d[0, at].partition_broadcast(P)).then_inc(lr_ready[b], 16)
                    sp.dma_start(relb[:, b, :], a["rel_row"][0, at].partition_broadcast(NREL)).then_inc(rel_ready[b], 16)

                def load_windows(i, b):
                    for k in range(KT):
                        first = sp.value_load(first_i[0:1, bass.ds((i * SLOTS + b) * KT + k, 1)], min_val=0, max_val=N)
                        sp.dma_start(qw[:, b, k, :], q_d[bass.ds(first, P), :]).then_inc(q_ready[b], 16)

                sp.sem_inc(slot_free, SLOTS)
                for b in range(SLOTS):
                    load_idx(0, b)
                    load_local(0, b)
                    load_windows(0, b)
                with sp.Fori(0, NR - 1) as i:
                    for b in range(SLOTS):
                        n = i * SLOTS + b
                        sp.wait_ge(gath[b], 16 * KT * (i + 1))
                        met(sp)
                        load_idx(i + 1, b)
                        sp.wait_ge(oh_done, n + 1)
                        met(sp)
                        load_local(i + 1, b)
                        sp.wait_ge(q_mm, n + 3)
                        met(sp)
                        load_windows(i + 1, b)
                        sp.wait_ge(kept[b], 16 * (i + 1))
                        met(sp)
                        sp.wait_ge(q_used, n + 3)
                        sp.sem_inc(slot_free, 1)
                for b in range(SLOTS):
                    sp.wait_ge(kept[b], 16 * NR)

            @block.gpsimd
            def _(pool):
                with pool.Fori(0, NR) as i:
                    for b in range(SLOTS):
                        pool.wait_ge(idx_ready[b], 16 * (i + 1))
                        pool.wait_ge(slot_free, i * SLOTS + b + 1)
                        met(pool)
                        for k in range(KT):
                            pool.indirect_dma_start(
                                out=g[:, b, k, :], out_offset=None, in_=kv_d,
                                in_offset=bass.IndirectOffsetOnAxis(ap=idx[:, b, k:k + 1], axis=0)).then_inc(gath[b], 16)

            @block.scalar
            def _(act):
                with act.Fori(0, NR) as i:
                    for b in range(SLOTS):
                        act.wait_ge(gath[b], 16 * KT * (i + 1))
                        met(act)
                        act.dma_start(edge_d[:, bass.ds((i * SLOTS + b) * KT, KT), :], g[:, b, :, P:2 * P]).then_inc(kept[b], 16)

            @block.vector
            def _(dve):
                def prepare(i, b, n):
                    dve.wait_ge(lr_ready[b], 16 * (i + 1))
                    dve.wait_ge(rel_ready[b], 16 * (i + 1))
                    dve.wait_ge(q_mm, n + 1)
                    dve.tensor_scalar(oh16[:, b % 2, :], relb[:, b, :], iota_p[0:NREL, 0:1], None, ALU.is_equal)
                    dve.tensor_scalar(ohT[:, b % 2, :], lrb[:, b, :], iota_p[:, 0:1], None, ALU.is_equal).then_inc(oh_done, 1)

                def score(i, b, n):
                    s = Steps(dve, scored, 2 * n)
                    dve.wait_ge(q_mm, n + 3)
                    dve.wait_ge(gath[b], 16 * KT * (i + 1))
                    s.link(dve.tensor_tensor(prod, psv(b % 2, KT, P), g[:, b, :, 0:P], ALU.mult))
                    s.link(dve.tensor_reduce(dot, prod.rearrange("p k (h c) -> p k h c", c=C2), AX.X, ALU.add))
                    dve.tensor_tensor(pm2[:, bass.ds(n * KT, KT), :], dot, psv(2 + b % 2, KT, H2), ALU.mult).then_inc(q_used, 1)

                dve.sem_inc(q_used, 2)
                prepare(0, 0, 0)

                def round_(i, last):
                    for b in range(SLOTS):
                        n = i * SLOTS + b
                        if b < SLOTS - 1:
                            prepare(i, b + 1, n + 1)
                        elif not last:
                            prepare(i + 1, 0, n + 1)
                        score(i, b, n)

                with dve.Fori(0, NR - 1) as i:
                    round_(i, False)
                round_(NR - 1, True)

            @block.tensor
            def _(pe):
                pe.sem_inc(q_mm, 2)
                with pe.Fori(0, NR) as i:
                    for b in range(SLOTS):
                        n = i * SLOTS + b
                        pe.wait_ge(oh_done, n + 1)
                        pe.wait_ge(q_ready[b], 16 * KT * (i + 1))
                        pe.wait_ge(q_used, n + 1)
                        for k in range(KT):
                            w = slice(k * P, (k + 1) * P)
                            nc.tensor.matmul(psv(2 + b % 2, KT, H2)[:, k, :], oh16[:, b % 2, w], rel, start=True, stop=True)
                            m = nc.tensor.matmul(psv(b % 2, KT, P)[:, k, :], ohT[:, b % 2, w], qw[:, b, k, :], start=True, stop=True)
                        m.then_inc(q_mm, 1)

        ts, td, ta = sem("h_max_t"), sem("h_max_dve"), sem("h_exp")
        top = TMP[:, 0:1]
        top1 = TMP[0:1, 4:5]
        with nc.Block() as block:
            @block.vector
            def _(dve):
                s = Steps(dve, td)
                tail = pm2[:, T - ROUND:T, :]
                s.link(dve.tensor_tensor(tail, tail, over(padneg[:, :], P, ROUND, H2), ALU.add))
                s.link(dve.tensor_reduce(top, PM[:, 0:T * H2], AX.X, ALU.max))
                dve.wait_ge(ts, 1)
                s.link(dve.tensor_reduce(top1, PS[0][0:1, 0, 0:P], AX.X, ALU.max))
                dve.wait_ge(ts, 2)
                s.link(dve.tensor_scalar(top, PS[0][:, 1, 0:1], -1.0, None, ALU.mult))

            @block.tensor
            def _(pe):
                pe.wait_ge(td, 2)
                nc.tensor.transpose(PS[0][0:1, 0, 0:P], top, ident[:, :]).then_inc(ts, 1)
                pe.wait_ge(td, 3)
                nc.tensor.matmul(PS[0][:, 1, 0:1], ones[0:1, :], top1, start=True, stop=True).then_inc(ts, 1)

            @block.scalar
            def _(act):
                act.wait_ge(td, 4)
                nc.scalar.activation(PM[:, 0:T * H2], PM[:, 0:T * H2], ACT.Exp, bias=top).then_inc(ta, 1)

        weighted_pass("hgt_sum", pm2, H2, C2, H2)

        ld, tld, staged, mm, used, fs, acts, vrdy, rrdy, lnd, xt, xc = (sem("hgt_end_loads"), sem("hgt_end_types"), sem("hgt_end_staged"),
            sem("hgt_end_products"), sem("hgt_end_used"), sem("hgt_end_dve"), sem("hgt_end_exp"), sem("hgt_end_var"), sem("hgt_end_rstd"),
            sem("hgt_end_ln"), sem("hgt_end_x_t"), sem("hgt_end_x_copied"))
        A = Arena(TMP, 0, TW)
        xs = A.take(CN)
        ac = A.take(CN)
        zc = A.take(CN, parts=H2)
        t = A.take(CT, P)
        q = A.take(CT, P)
        nt8 = A.take(CN, parts=NTYPE, dtype=I32)
        oh8 = A.take(CN, parts=NTYPE)
        sm, vr, rs = A.take(CT), A.take(CT), A.take(CT)
        rb = PM[:, 0:3 * P].rearrange("p (a b) -> p a b", b=P)
        with nc.Block() as block:
            @block.sync
            def _(sp):
                for j, n_ in enumerate(("L2_gnn_bo", "L2_gnn_gamma", "L2_gnn_beta")):
                    sp.dma_start(rb[:, j, :], row_bc(n_)).then_inc(ld, 16)
                with sp.Fori(0, NC) as c:
                    sp.dma_start(nt8, a["type_row"][0, bass.ds(c * CN, CN)].partition_broadcast(NTYPE)).then_inc(tld, 16)
                    sp.wait_ge(used, c + 1)
                    met(sp)
                sp.wait_ge(ld, 48)

            @block.scalar
            def _(act):
                half = CN // 2
                act.sem_inc(acts, 1)
                with act.Fori(0, NC) as c:
                    act.wait_ge(mm, 2 * c + 1)
                    met(act)
                    nc.scalar.copy(xs, xT[:, bass.ds(c * CN, CN)]).then_inc(staged, 1)
                    nc.scalar.copy(ac, acc2[:, 0, bass.ds(c * CN, CN)]).then_inc(staged, 1)
                    nc.scalar.copy(zc, acc2[0:H2, 1, bass.ds(c * CN, CN)]).then_inc(staged, 1)
                    rstd_act(act, lnd, vr, rs, vrdy, rrdy, 2 * c)
                    act.wait_ge(acts, 2 * c + 2)
                    nc.scalar.activation(q, q, ACT.Exp).then_inc(acts, 1)
                    rstd_act(act, lnd, vr, rs, vrdy, rrdy, 2 * c + 1)
                    act.wait_ge(xt, c + 1)
                    met(act)
                    nc.scalar.copy(xT[:, bass.ds(c * CN, CN)], psv(2, CN)).then_inc(xc, 1)

            @block.tensor
            def _(pe):
                half = CN // 2
                pe.sem_inc(mm, 1)
                with pe.Fori(0, NC) as c:
                    pe.wait_ge(staged, 3 * c + 3)
                    for j in range(2):
                        m = nc.tensor.matmul(PS[0][:, j, 0:half], headmap[:, :], zc[:, j * half:(j + 1) * half], start=True, stop=True)
                    m.then_inc(mm, 1)
                    pe.wait_ge(fs, c * 50 + 4)
                    for k in range(CT):
                        w = slice(k * P, (k + 1) * P)
                        ps = psv(1, CT, P)[:, k, :]
                        nc.tensor.matmul(ps, ac[:, w], WB[:, 4 * P:5 * P], start=True, stop=False)
                        nc.tensor.matmul(ps, xs[:, w], WB[:, 3 * P:4 * P], start=False, stop=False)
                        m = nc.tensor.matmul(ps, oh8[:, w], T8s, start=False, stop=True)
                    m.then_inc(mm, 1)
                    pe.wait_ge(used, c + 1)
                    for k in range(CT):
                        m = nc.tensor.transpose(psv(2, CT, P)[:, k, :], t[:, k, :], ident[:, :])
                    m.then_inc(xt, 1)

            @block.vector
            def _(dve):
                half = CN // 2
                dve.wait_ge(ld, 48)
                dve.sem_inc(xc, 1)
                per = 50
                with dve.Fori(0, NC) as c:
                    s = Steps(dve, fs, c * per)
                    dve.wait_ge(mm, 2 * c + 2)
                    qv = q.rearrange("p a b -> p (a b)")
                    s.link(dve.tensor_scalar(qv.rearrange("p (a b) -> p a b", a=2), PS[0][:, :, 0:half], SM_EPS, None, ALU.add))
                    s.link(dve.reciprocal(qv, qv))
                    s.link(dve.tensor_tensor(ac, ac, qv, ALU.mult))
                    dve.wait_ge(tld, 16 * (c + 1))
                    s.link(dve.tensor_scalar(oh8, nt8, iota_p[0:NTYPE, 0:1], None, ALU.is_equal))
                    dve.wait_ge(mm, 2 * c + 3)
                    dve.wait_ge(xc, c + 1)
                    s.link(dve.tensor_tensor(t, psv(1, CT, P), rb[:, 0, :].unsqueeze(1).to_broadcast([P, CT, P]), ALU.add))
                    layer_norm(dve, s, t, q, sm, vr, rs, vrdy, rrdy, 2 * c)
                    s.link(dve.tensor_tensor(t, t, rb[:, 1, :].unsqueeze(1).to_broadcast([P, CT, P]), ALU.mult))
                    s.link(dve.tensor_tensor(t, t, rb[:, 2, :].unsqueeze(1).to_broadcast([P, CT, P]), ALU.add))
                    s.link(dve.tensor_scalar(q, t, 0.0, None, ALU.min))
                    dve.sem_inc(acts, 1)
                    dve.wait_ge(acts, 2 * c + 3)
                    s.link(dve.tensor_scalar(q, q, -1.0, None, ALU.add))
                    s.link(dve.scalar_tensor_tensor(t, t, 0.0, q, ALU.max, ALU.add))
                    residual_out(dve, s, t, q, sm, vr, rs, vrdy, rrdy, c, 2, 1, xn)
                    dve.sem_inc(fs, per - s.n)
                    dve.sem_inc(used, 1)

        layer_ends()

        ld, cd, ca, bt = sem("sch_loads"), sem("sch_dve"), sem("sch_sin"), sem("sch_bias")
        A = Arena(PM, 0, T * Z0)
        cw = A.take(T)
        after_cw = A.at
        wq = A.take(T)
        wk = A.take(T, dtype=I32)
        brow = typ[0:1, 0:P]
        bres = typ[0:1, P:2 * P]
        bsplit = typ[0:96, 2 * P:4 * P].bitcast(BF16)
        ones_b = typ[0:96, 4 * P:5 * P].bitcast(BF16)[:, 0:P]
        b1, cap1, l2b, cap2, capc = (cols[:, j:j + 1] for j in range(5))
        lin1, w1, w2, lin2, linw = WA[:, 0:P], WA[0:NG, P:2 * P], WA[:, 2 * P:3 * P], WB[:, 0:P], WB[:, P:2 * P]
        with nc.Block() as block:
            @block.sync
            def _(sp):
                for dst_, src_ in ((lin1, a["L3_gnn_lin1_w_T"]), (w1, a["L3_gnn_mlp_w1_T"]), (w2, a["L3_gnn_mlp_w2_T"]), (lin2, a["L3_gnn_lin2_w_T"]),
                                   (linw, a["L3_gnn_lin_w_T"]), (cw, a["w_et"]), (b1, col_in("L3_gnn_mlp_b1")), (l2b, col_in("L3_gnn_lin2_b")),
                                   (brow, a["L3_gnn_mlp_b2"].rearrange("(o f) -> o f", o=1))):
                    sp.dma_start(dst_, src_).then_inc(ld, 16)
                sp.wait_ge(ld, 144)

            @block.tensor
            def _(pe):
                pe.wait_ge(ld, 144)
                nc.tensor.matmul(PS[0][0:1, 0, 0:P], ones[:, 0:1], w2, start=True, stop=True).then_inc(bt, 1)

            @block.vector
            def _(dve):
                s = Steps(dve, cd)
                dve.wait_ge(ld, 144)
                s.link(dve.tensor_scalar(wk, cw, 0.05, None, ALU.mult))
                s.link(dve.tensor_copy(wq, wk))
                s.link(dve.scalar_tensor_tensor(wq, wq, -20.0, cw, ALU.mult, ALU.add))
                s.link(dve.scalar_tensor_tensor(wq, wq, -1.0, wq, ALU.mult, ALU.max))
                s.link(dve.tensor_scalar(cw, wq, -1.0, 20.0, ALU.mult, ALU.add))
                s.link(dve.tensor_tensor(wq, wq, cw, ALU.min))
                s.link(dve.tensor_scalar(wq, wq, -float(np.pi) / 10, float(np.pi) / 2, ALU.mult, ALU.add))
                s.link(dve.memset(capc, SP_CAP))
                s.link(dve.tensor_scalar(cap1, b1, -1.0, SP_CAP, ALU.mult, ALU.add))
                s.link(dve.tensor_scalar(cap2, l2b, -1.0, SP_CAP, ALU.mult, ALU.add))
                dve.wait_ge(ca, 1)
                s.link(dve.tensor_scalar(cw, wq, 0.5, 0.5, ALU.mult, ALU.add))
                dve.wait_ge(bt, 1)
                s.link(dve.scalar_tensor_tensor(brow, PS[0][0:1, 0, 0:P], -LN2, brow, ALU.mult, ALU.add))
                s.link(dve.memset(bsplit, 0.0))
                s.link(dve.memset(ones_b, 1.0))
                for j in range(3):
                    part = bsplit[32 * j:32 * j + 1, :].rearrange("p (k f) -> p k f", f=P)
                    s.link(dve.tensor_copy(part, brow.unsqueeze(1).to_broadcast([1, KT, P])))
                    s.link(dve.tensor_copy(bres, part[:, 0, :]))
                    s.link(dve.tensor_tensor(brow, brow, bres, ALU.subtract))

            @block.scalar
            def _(act):
                act.wait_ge(cd, 7)
                nc.scalar.activation(wq, wq, ACT.Sin).then_inc(ca, 1)

        staged, mm, evac, stored, row_free = sem("sch_staged"), sem("sch_products"), sem("sch_copied"), sem("sch_stored"), sem("sch_row_free")
        A = Arena(TMP, 0, TW)
        xs = A.take(CN)
        hrow = A.take(CT, P)
        with nc.Block() as block:
            @block.sync
            def _(sp):
                sp.sem_inc(row_free, 1)
                with sp.Fori(0, NC) as c:
                    sp.wait_ge(evac, c + 1)
                    met(sp)
                    sp.dma_start(table_rows(tab3_d, c, P), hrow).then_inc(stored, 16)
                    sp.wait_ge(stored, 16 * (c + 1))
                    sp.sem_inc(row_free, 1)

            @block.scalar
            def _(act):
                with act.Fori(0, NC) as c:
                    act.wait_ge(mm, c + 1)
                    met(act)
                    nc.scalar.copy(xs, xT[:, bass.ds(c * CN, CN)]).then_inc(staged, 1)
                    act.wait_ge(mm, c + 2)
                    act.wait_ge(row_free, c + 1)
                    nc.scalar.copy(hrow, psv(0, CT, P)).then_inc(evac, 1)

            @block.tensor
            def _(pe):
                pe.sem_inc(mm, 1)
                with pe.Fori(0, NC) as c:
                    pe.wait_ge(staged, c + 1)
                    for k in range(CT):
                        m = nc.tensor.matmul(psv(0, CT, P)[:, k, :], xs[:, k * P:(k + 1) * P], lin1, start=True, stop=True)
                    m.then_inc(mm, 1)

        idx_ready, gath, attr_ready = sems("sch_idx"), sems("sch_gathered"), sems("sch_attr")
        z_mm, sp_act, sp_done, w_mm, msg_done, oh_done, agg, acc_step, softs = (sem("sch_z"), sem("sch_log"), sem("sch_softplus"), sem("sch_filters"),
            sem("sch_messages"), sem("sch_onehot"), sem("sch_sums"), sem("sch_added"), sem("sch_act"))
        A = Arena(PM, after_cw, T * Z0)
        attr = A.take(SLOTS, KT * P, parts=NG)
        ex = A.take(2, KT * P)
        soft = A.take(2, KT * P)
        msg = A.take(2, KT, P)
        oh = A.take(2, KT, P)
        A = Arena(TMP, 0, TW)
        idx = A.take(SLOTS, KT, dtype=U32)
        g = A.take(SLOTS, KT, P)
        zb = [PS[0][:, j, :] for j in range(2)]
        wb = [PS[1][:, j, :].rearrange("p (k f) -> p k f", f=P) for j in range(2)]
        sb_ = [PS[2][:, j, :] for j in range(2)]
        with nc.Block() as block:
            @block.sync
            def _(sp):
                def load_idx(i, b):
                    sp.dma_start(idx[:, b, :], a["src_et"][:, bass.ds((i * SLOTS + b) * KT, KT)]).then_inc(idx_ready[b], 16)

                def load_attr(i, b):
                    sp.dma_start(attr[:, b, :], a["attrT"][:, bass.ds((i * SLOTS + b) * KT * P, KT * P)]).then_inc(attr_ready[b], 16)

                for b in range(SLOTS):
                    load_idx(0, b)
                    load_attr(0, b)
                with sp.Fori(0, NR - 1) as i:
                    for b in range(SLOTS):
                        sp.wait_ge(z_mm, i * SLOTS + b + 1)
                        met(sp)
                        load_attr(i + 1, b)
                        sp.wait_ge(gath[b], 16 * KT * (i + 1))
                        met(sp)
                        load_idx(i + 1, b)

            @block.gpsimd
            def _(pool):
                with pool.Fori(0, NR) as i:
                    for b in range(SLOTS):
                        pool.wait_ge(idx_ready[b], 16 * (i + 1))
                        pool.wait_ge(msg_done, i * SLOTS + b + 1)
                        met(pool)
                        for k in range(KT):
                            pool.indirect_dma_start(
                                out=g[:, b, k, :], out_offset=None, in_=tab3_d,
                                in_offset=bass.IndirectOffsetOnAxis(ap=idx[:, b, k:k + 1], axis=0)).then_inc(gath[b], 16)

            def ahead(i, b, d):
                return (i + 1 if b + d >= SLOTS else i), (b + d) % SLOTS

            @block.tensor
            def _(pe):
                def filters_in(i, b, n):
                    pe.wait_ge(attr_ready[b], 16 * (i + 1))
                    pe.wait_ge(sp_done, n + 1)
                    nc.tensor.matmul(zb[b % 2], w1, attr[:, b, :], start=True, stop=True).then_inc(z_mm, 1)

                def filters_out(b, n):
                    pe.wait_ge(sp_done, n + 3)
                    pe.wait_ge(msg_done, n + 3)
                    nc.tensor.matmul(PS[1][:, b % 2, :], ones_b, bsplit, start=True, stop=False, skip_group_check=True)
                    for k in range(KT):
                        m = nc.tensor.matmul(wb[b % 2][:, k, :], soft[:, b % 2, k * P:(k + 1) * P], w2, start=False, stop=(k == KT - 1),
                                             skip_group_check=True)
                    m.then_inc(w_mm, 1)

                def sums(b, n):
                    pe.wait_ge(msg_done, n + SLOTS + 1)
                    pe.wait_ge(oh_done, n + 1)
                    pe.wait_ge(acc_step, n * KT + 4)
                    for k in range(KT):
                        m = nc.tensor.matmul(sb_[b % 2][:, k * P:(k + 1) * P], msg[:, b % 2, k, :], oh[:, b % 2, k, :], start=True, stop=True)
                    m.then_inc(agg, 1)

                def round_(i, last):
                    for b in range(SLOTS):
                        n = i * SLOTS + b
                        if b + 2 < SLOTS or not last:
                            filters_in(*ahead(i, b, 2), n + 2)
                        if b + 1 < SLOTS or not last:
                            filters_out((b + 1) % SLOTS, n + 1)
                        sums(b, n)

                filters_in(0, 0, 0)
                filters_in(0, 1, 1)
                filters_out(0, 0)
                with pe.Fori(0, NR - 1) as i:
                    round_(i, False)
                round_(NR - 1, True)

            @block.scalar
            def _(act):
                with act.Fori(0, NR) as i:
                    for b in range(SLOTS):
                        n = i * SLOTS + b
                        s = Steps(act, softs, 2 * n)
                        act.wait_ge(z_mm, n + 1)
                        act.wait_ge(sp_done, n + 1)
                        e = ex[:, b % 2, :]
                        s.link(nc.scalar.activation(e, zb[b % 2], ACT.Relu, bias=cap1, scale=-1.0))
                        s.link(nc.scalar.activation(e, e, ACT.Exp, bias=capc, scale=-1.0))
                        nc.scalar.activation(e, e, ACT.Ln, bias=1.0).then_inc(sp_act, 1)

            @block.vector
            def _(dve):
                def softplus(b, n):
                    dve.wait_ge(sp_act, n + 1)
                    dve.wait_ge(w_mm, n + 1)
                    dve.scalar_tensor_tensor(soft[:, b % 2, :], zb[b % 2], b1, ex[:, b % 2, :], ALU.add, ALU.max).then_inc(sp_done, 1)

                def messages(i, b, n):
                    dve.wait_ge(w_mm, n + 3)
                    dve.wait_ge(gath[b], 16 * KT * (i + 1))
                    dve.wait_ge(agg, n + 1)
                    dve.tensor_tensor(msg[:, b % 2, :, :], wb[b % 2], g[:, b, :, :], ALU.mult).then_inc(msg_done, 1)
                    for k in range(KT):
                        t_ = bass.ds(n * KT + k, 1)
                        m = dve.scalar_tensor_tensor(oh[:, b % 2, k, :], iota_f[:, :], lr[:, t_], cw[:, t_].to_broadcast([P, P]), ALU.is_equal, ALU.mult)
                    m.then_inc(oh_done, 1)

                def round_(i, last):
                    for b in range(SLOTS):
                        n = i * SLOTS + b
                        messages(i, b, n)
                        if b + 1 < SLOTS or not last:
                            softplus((b + 1) % SLOTS, n + 1)
                        dve.wait_ge(agg, n + 3)
                        accumulate(dve, acc_step, n, lambda first: AC[:, bass.ds(first, P)],
                                   lambda k: sb_[b % 2][:, k * P:(k + 1) * P])

                dve.memset(acc1, 0.0).then_inc(acc_step, 1)
                dve.sem_inc(acc_step, 7)
                dve.sem_inc(sp_done, 2)
                dve.sem_inc(msg_done, SLOTS)
                dve.sem_inc(w_mm, 2)
                dve.sem_inc(agg, 2)
                softplus(0, 0)
                with dve.Fori(0, NR - 1) as i:
                    round_(i, False)
                round_(NR - 1, True)

        ld, mm, used, fs, acts, vrdy, rrdy, lnd, z_act, st = (sem("sch_end_loads"), sem("sch_end_products"), sem("sch_end_used"), sem("sch_end_dve"),
            sem("sch_end_soft"), sem("sch_end_var"), sem("sch_end_rstd"), sem("sch_end_ln"), sem("sch_end_log"), sem("sch_end_stored"))
        A = Arena(TMP, 0, TW)
        e_ = A.take(2, CN // 2)
        so = A.take(2, CN // 2)
        t = A.take(CT, P)
        q = A.take(CT, P)
        sm, vr, rs = A.take(CT), A.take(CT), A.take(CT)
        lb = A.take(P)
        with nc.Block() as block:
            @block.sync
            def _(sp):
                sp.dma_start(lb, row_bc("L3_gnn_lin_b")).then_inc(ld, 16)
                with sp.Fori(0, NC) as c:
                    sp.wait_ge(used, c + 1)
                    met(sp)
                    sp.dma_start(table_rows(out, c, P), xn[:, bass.ds(c * CT, CT), :]).then_inc(st, 16)
                sp.wait_ge(st, 16 * NC)

            @block.tensor
            def _(pe):
                half = CN // 2
                with pe.Fori(0, NC) as c:
                    pe.wait_ge(acts, c + 1)
                    for j in range(2):
                        m = nc.tensor.matmul(PS[0][:, j, 0:half], lin2, AC[:, bass.ds(c * CN + j * half, half)], start=True, stop=True)
                    m.then_inc(mm, 1)
                    pe.wait_ge(fs, c * 40 + 2)
                    sv_ = so.rearrange("p a b -> p (a b)")
                    for k in range(CT):
                        m = nc.tensor.matmul(psv(1, CT, P)[:, k, :], sv_[:, k * P:(k + 1) * P], linw, start=True, stop=True)
                    m.then_inc(mm, 1)

            @block.scalar
            def _(act):
                half = CN // 2
                with act.Fori(0, NC) as c:
                    s = Steps(act, z_act, 3 * c)
                    act.wait_ge(mm, 2 * c + 1)
                    s.link(nc.scalar.activation(e_, PS[0][:, :, 0:half], ACT.Relu, bias=cap2, scale=-1.0))
                    s.link(nc.scalar.activation(e_, e_, ACT.Exp, bias=capc, scale=-1.0))
                    s.link(nc.scalar.activation(e_, e_, ACT.Ln, bias=1.0))
                    rstd_act(act, lnd, vr, rs, vrdy, rrdy, c)

            @block.vector
            def _(dve):
                half = CN // 2
                dve.wait_ge(ld, 16)
                dve.sem_inc(acts, 1)
                per = 40
                with dve.Fori(0, NC) as c:
                    s = Steps(dve, fs, c * per)
                    dve.wait_ge(z_act, 3 * c + 3)
                    s.link(dve.scalar_tensor_tensor(so, PS[0][:, :, 0:half], l2b, e_, ALU.add, ALU.max))
                    s.link(dve.tensor_scalar(so, so, -LN2, None, ALU.add))
                    dve.wait_ge(mm, 2 * c + 2)
                    s.link(dve.tensor_tensor(t, psv(1, CT, P), lb.unsqueeze(1).to_broadcast([P, CT, P]), ALU.add))
                    dve.sem_inc(acts, 1)
                    residual_out(dve, s, t, q, sm, vr, rs, vrdy, rrdy, c, 1, 0, xn)
                    dve.sem_inc(fs, per - s.n)
                    dve.sem_inc(used, 1)


_WEIGHTS = ["L0_gnn_W", "L0_gnn_skip_W", "L0_gnn_gat_bias", "L0_gnn_skip_b", "L0_gnn_ln_g", "L0_gnn_ln_b", "L1_gnn_blin", "L1_gnn_gamma",
            "L1_gnn_beta", "L1_gnn_bg", "L2_gnn_type_emb", "L2_gnn_Wk", "L2_gnn_Wq", "L2_gnn_Wv", "L2_gnn_rel_scale", "L2_gnn_Wo",
            "L2_gnn_bo", "L2_gnn_Wskip", "L2_gnn_gamma", "L2_gnn_beta", "L3_gnn_mlp_b1", "L3_gnn_mlp_b2", "L3_gnn_lin2_b", "L3_gnn_lin_b"]
_TRANSPOSED = ["L1_gnn_Wlin", "L1_gnn_Wg", "L2_gnn_type_emb", "L3_gnn_mlp_w1", "L3_gnn_mlp_w2", "L3_gnn_lin1_w", "L3_gnn_lin2_w", "L3_gnn_lin_w"]


def kernel(**inputs):
    import numpy as _np
    import concourse.bacc as _bacc
    from concourse import mybir as _mybir
    from concourse.bass_utils import run_bass_kernel_spmd as _run

    i = {k: _np.asarray(v) for k, v in inputs.items()}

    def edges(v, fill, shift=0):
        v = _np.concatenate([v, _np.full((EP - E,) + v.shape[1:], fill, v.dtype)])
        if shift:
            v = _np.concatenate([_np.full(1, -1, v.dtype), v[:-1]]) if shift < 0 else _np.concatenate([v[1:], _np.full(1, -1, v.dtype)])
        return v

    def by_tile(v):
        return v.reshape(T, P).T

    def nodes(v):
        return _np.concatenate([v, _np.zeros((NP - N,) + v.shape[1:], v.dtype)])

    arrays = {k: i[k] for k in _WEIGHTS}
    arrays |= {k + "_T": i[k].T for k in _TRANSPOSED}
    dst = edges(i["dst"], N)
    arrays |= {
        "x": nodes(i["x"]), "xT": nodes(i["x"]).T,
        "src_et": by_tile(edges(i["src"], 0)).view(_np.uint32) if False else _np.ascontiguousarray(by_tile(edges(i["src"], 0))).view(_np.uint32),
        "dst_et": by_tile(dst), "dst_prev_et": by_tile(edges(i["dst"], N, -1)),
        "dst_first": dst[::P].reshape(1, T),
        "dst_rows": dst.reshape(NR, RW), "dst_prev_rows": edges(i["dst"], N, -1).reshape(NR, RW),
        "dst_next_rows": edges(i["dst"], N, 1).reshape(NR, RW),
        "w_et": by_tile(edges(i["edge_weight"], 0)), "rel_row": edges(i["edge_type_16"], 0).reshape(1, EP),
        "attrT": edges(i["edge_attr_50"], 0).T, "type_row": nodes(i["node_type_8"]).reshape(1, NP),
        "att_src": i["L0_gnn_att_src"].reshape(P), "att_dst": i["L0_gnn_att_dst"].reshape(P),
    }
    nc = _bacc.Bacc("TRN2", target_bir_lowering=False, num_devices=1)
    args, fed = {}, {}
    for name, v in arrays.items():
        v = _np.ascontiguousarray(v)
        fed[f"in_{name}"] = v
        args[name] = nc.dram_tensor(f"in_{name}", v.shape, _mybir.dt.from_np(v.dtype), kind="ExternalInput").ap()
    out = nc.dram_tensor("out_0", (NP, P), _mybir.dt.float32, kind="ExternalOutput").ap()
    build(nc, args, out)
    r = _run(nc, [fed], core_ids=[0])
    return r.results[0]["out_0"][:N]
```

```python
from contextlib import ExitStack

import numpy as np

import concourse.bass as bass
from concourse import mybir

F32 = mybir.dt.float32
BF16 = mybir.dt.bfloat16
I32 = mybir.dt.int32
U32 = mybir.dt.uint32
ALU = mybir.AluOpType
ACT = mybir.ActivationFunctionType
AX = mybir.AxisListType

P = 128
N = 6250
E = 206250
KT = 4
SLOTS = 4
ROUND = KT * SLOTS
NR = -(-E // (P * ROUND))
T = NR * ROUND
EP = T * P
CT = 10
PARTS = 2
PT = CT // PARTS
PN = PT * P
QN = PN // 2
CN = CT * P
NC = -(-(N + P) // CN)
NP = NC * CN
NT = NP // P
HALF = ROUND // 2
RW = ROUND * P
H0, C0 = 4, 32
H2, C2 = 8, 16
ROW0 = P + H0
Z0 = 2 * H0 + 1
NTYPE, NREL, NG = 8, 16, 50
BIG = 1e30
LN_EPS, BN_EPS, SM_EPS = 1e-5, 1e-5, 1e-16
LN2 = float(np.log(2.0))
SP_CAP = 20.0
TW = 6470


class Steps:

    def __init__(self, engine, sem, base=0):
        self.engine, self.sem, self.base, self.n = engine, sem, base, 0

    def link(self, ins):
        ins.then_inc(self.sem, 1)
        self.n += 1
        self.engine.wait_ge(self.sem, self.base + self.n)


class Arena:

    def __init__(self, tensor, lo, hi):
        self.t, self.at, self.hi = tensor, lo, hi

    def take(self, *dims, parts=P, dtype=F32):
        n = int(np.prod(dims))
        words = n if dtype in (F32, I32, U32) else -(-n // 2)
        v = self.t[0:parts, self.at:self.at + words]
        self.at += words
        assert self.at <= self.hi, (self.at, self.hi)
        if dtype != F32:
            v = v.bitcast(dtype)
        names = "abcd"[:len(dims)]
        if len(dims) == 1:
            return v
        return v.rearrange(f"p ({' '.join(names)}) -> p {' '.join(names)}", **dict(zip(names, dims)))


def over(ap, *shape):
    while len(ap.shape) < len(shape):
        ap = ap.unsqueeze(len(ap.shape))
    return ap.to_broadcast(list(shape))


def build(nc, a, out):
    ctx = ExitStack()
    with ctx:
        def sb(name, shape, dt=F32):
            return ctx.enter_context(nc.sbuf_tensor(name, shape, dt))

        layer_sems = []

        def sem(name):
            layer_sems.append(nc.alloc_semaphore(name=name))
            return layer_sems[-1]

        passed = {e: nc.alloc_semaphore(name=f"passed_{e}") for e in ("sync", "gpsimd", "scalar", "vector")}

        def met(engine):
            name = {nc.sync: "sync", nc.gpsimd: "gpsimd", nc.scalar: "scalar", nc.vector: "vector"}[engine]
            engine.sem_inc(passed[name], 1)

        def layer_ends():
            nc.clear_and_free_semaphores(layer_sems)
            layer_sems.clear()
            nc.all_engine_barrier()

        def sems(name, n=SLOTS):
            return [sem(f"{name}{b}") for b in range(n)]

        def scratch(name, shape, dt=F32):
            return nc.dram_tensor(name, shape, dt, kind="Internal").ap()

        lrow_d = scratch("local_dst_row", (1, EP))
        tab0_d = scratch("gat_table", (NP, ROW0))
        adt_d = scratch("gat_dst_scores", (NP, H0))
        tab1_d = scratch("gcn_table", (NP, P))
        kv_d = scratch("hgt_kv_table", (NP, 2 * P))
        q_d = scratch("hgt_q_table", (NP, P))
        tab3_d = scratch("schnet_table", (NP, P))
        edge_d = scratch("edge_rows", (P, T, P))

        xT = sb("xT", [P, NP])
        xn = sb("xn", [P, NT, P])
        AC = sb("AC", [P, T * 2 * H0])
        PM = sb("PM", [P, T * Z0])
        TMP = sb("TMP", [P, TW])
        lr = sb("lr", [P, T])
        first_i = sb("first_i", [1, T], I32)
        narrow_i = sb("narrow_i", [1, 1], I32)
        iota_f = sb("iota_f", [P, P])
        iota_p = sb("iota_p", [P, 1])
        ident = sb("ident", [P, P])
        ones = sb("ones", [P, P])
        padneg = sb("padneg", [P, ROUND])
        asd = sb("asd", [P, NT, 2 * H0])
        dinv = sb("dinv", [P, NT])
        degs = sb("degs", [P, 3, NT])
        deg, dgc, dgw = degs[:, 0, :], degs[:, 1, :], degs[:, 2, :]
        WA = sb("WA", [P, 3 * P])
        WB = sb("WB", [P, 5 * P])
        rows = sb("rows", [P, 3 * P])
        cols = sb("cols", [P, 16])
        typ = sb("typ", [P, 5 * P])
        headmap = sb("headmap", [H2, P])

        PS = [ctx.enter_context(nc.psum_tensor(f"ps{i}", [P, 2, 512], F32)) for i in range(4)]

        def psv(i, *dims, parts=P):
            v = PS[i][0:parts, :, :].rearrange("p a b -> p (a b)")
            n = int(np.prod(dims))
            names = "abcd"[:len(dims)]
            v = v[:, 0:n]
            return v if len(dims) == 1 else v.rearrange(
                f"p ({' '.join(names)}) -> p {' '.join(names)}", **dict(zip(names, dims)))

        as_e = AC[:, 0:T * H0].rearrange("p (t h) -> p t h", h=H0)
        ad_e = AC[:, T * H0:2 * T * H0].rearrange("p (t h) -> p t h", h=H0)
        pm0 = PM[:, :].rearrange("p (t z) -> p t z", z=Z0)
        pm2 = PM[:, 0:T * H2].rearrange("p (t z) -> p t z", z=H2)
        acc2 = AC[:, 0:2 * NP].rearrange("p (a n) -> p a n", a=2)
        acc1 = AC[:, 0:NP]
        hkeep = AC[:, NP:2 * NP].rearrange("p (t f) -> p t f", f=P)

        def table_rows(d, c, width):
            return d[bass.ds(c * CN, CN), 0:width].rearrange("(t p) f -> p t f", p=P)

        def row_bc(name, n=P, parts=P):
            return a[name].partition_broadcast(parts)

        def col_in(name):
            return a[name].rearrange("(f o) -> f o", o=1)

        load0, c0, v0, st0 = sem("start_loads"), sem("start_consts"), sem("start_dve"), sem("start_stores")
        A = Arena(TMP, 0, TW)
        B = Arena(PM, 0, T * Z0)
        dst_i = B.take(T, dtype=I32)
        dstf = B.take(T)
        firstb = B.take(T, dtype=I32)
        firstf = B.take(T)
        rfirstb = B.take(T, dtype=I32)
        rfirstf = B.take(T)
        rlastb = B.take(NR, dtype=I32)
        span = B.take(NR)
        nar = B.take(1)
        rows_i = A.take(ROUND, P, parts=NR, dtype=I32)
        rows_l = A.take(ROUND, P, parts=NR)
        base_r = A.take(ROUND, parts=NR)
        step_r = A.take(ROUND, parts=NR)
        iw = A.take(P, dtype=I32)
        ip = A.take(1, dtype=I32)
        with nc.Block() as block:
            @block.sync
            def _(sp):
                for dst, src in ((xT[:, :], a["xT"]), (dst_i, a["dst_et"]), (firstb, a["dst_first"][0].partition_broadcast(P)),
                                 (rfirstb, a["dst_round_first"][0].partition_broadcast(P)), (rlastb, a["dst_round_last"][0].partition_broadcast(P)), (rows_i, a["dst_rows"].rearrange("p (a b) -> p a b", b=P))):
                    sp.dma_start(dst, src).then_inc(load0, 16)
                sp.wait_ge(v0, 100)
                met(sp)
                sp.dma_start(lrow_d.rearrange("o (p a b) -> (o p) a b", a=ROUND, b=P), rows_l).then_inc(st0, 16)
                sp.wait_ge(st0, 16)

            @block.gpsimd
            def _(pool):
                pool.memset(ident[:, :], 0.0).then_inc(c0, 1)
                pool.memset(ones[:, :], 1.0).then_inc(c0, 1)
                pool.memset(headmap[:, :], 1.0).then_inc(c0, 1)
                pool.iota(iw, [[1, P]], base=0, channel_multiplier=0).then_inc(c0, 1)
                pool.iota(ip, [[1, 1]], base=0, channel_multiplier=1).then_inc(c0, 1)
                pool.wait_ge(c0, 5)
                pool.affine_select(out=ident[:, :], in_=ident[:, :], compare_op=ALU.not_equal, fill=1.0, base=0,
                                   pattern=[[-1, P]], channel_multiplier=1).then_inc(c0, 1)
                pool.affine_select(out=headmap[:, :], in_=headmap[:, :], compare_op=ALU.is_ge, fill=0.0, base=0,
                                   pattern=[[1, P]], channel_multiplier=-C2).then_inc(c0, 1)
                pool.wait_ge(c0, 7)
                pool.affine_select(out=headmap[:, :], in_=headmap[:, :], compare_op=ALU.is_ge, fill=0.0, base=C2 - 1,
                                   pattern=[[-1, P]], channel_multiplier=C2).then_inc(c0, 1)

            @block.vector
            def _(dve):
                s = Steps(dve, v0)
                dve.wait_ge(load0, 96)
                dve.wait_ge(c0, 8)
                s.link(dve.tensor_copy(iota_f[:, :], iw))
                s.link(dve.tensor_copy(iota_p[:, :], ip))
                s.link(dve.tensor_copy(dstf, dst_i))
                s.link(dve.tensor_copy(firstf, firstb))
                s.link(dve.tensor_copy(rfirstf, rfirstb))
                s.link(dve.tensor_tensor(span, rlastb, rfirstb[:, ::ROUND], ALU.subtract))
                s.link(dve.tensor_reduce(nar, span, AX.X, ALU.max))
                s.link(dve.tensor_scalar(nar, nar, float(P), None, ALU.is_lt))
                s.link(dve.tensor_copy(narrow_i[:, :], nar[0:1, :]))
                s.link(dve.tensor_tensor(rfirstf, rfirstf, firstf, ALU.subtract))
                s.link(dve.scalar_tensor_tensor(firstf, rfirstf, nar, firstf, ALU.mult, ALU.add))
                s.link(dve.tensor_copy(first_i[:, :], firstf[0:1, :]))
                s.link(dve.tensor_tensor(lr[:, :], dstf, firstf, ALU.subtract))
                s.link(dve.tensor_scalar(padneg[:, :], dstf[:, T - ROUND:T], float(N), -BIG, ALU.is_ge, ALU.mult))
                s.link(dve.tensor_copy(base_r, rows_i[:, :, 0]))
                s.link(dve.tensor_tensor(step_r, base_r[:, 0:1].to_broadcast([NR, ROUND]), base_r, ALU.subtract))
                s.link(dve.scalar_tensor_tensor(base_r, step_r, nar[0:NR, :], base_r, ALU.mult, ALU.add))
                s.link(dve.tensor_tensor(rows_l, rows_i, over(base_r, NR, ROUND, P), ALU.subtract))
                dve.sem_inc(v0, 100 - s.n)
                s.n = 100

        def layer_norm(dve, s, t, q, sm, vr, rs, var_ready, rstd_ready, count):
            s.link(dve.tensor_reduce(sm, t, AX.X, ALU.add))
            s.link(dve.tensor_scalar(sm, sm, -1.0 / P, None, ALU.mult))
            s.link(dve.tensor_tensor(t, t, over(sm, P, CT, P), ALU.add))
            s.link(dve.tensor_tensor(q, t, t, ALU.mult))
            s.link(dve.tensor_reduce(vr, q, AX.X, ALU.add))
            s.link(dve.tensor_scalar(vr, vr, 1.0 / P, LN_EPS, ALU.mult, ALU.add))
            dve.sem_inc(var_ready, 1)
            dve.wait_ge(rstd_ready, count + 1)
            newton(dve, s, rs, vr, sm)
            s.link(dve.tensor_tensor(t, t, over(rs, P, CT, P), ALU.mult))

        def newton(dve, s, r, v, w):
            s.link(dve.tensor_tensor(w, r, r, ALU.mult))
            s.link(dve.tensor_tensor(w, w, v, ALU.mult))
            s.link(dve.tensor_scalar(w, w, -0.5, 1.5, ALU.mult, ALU.add))
            s.link(dve.tensor_tensor(r, r, w, ALU.mult))

        def rstd_act(act, ln_done, vr, rs, var_ready, rstd_ready, count, extra=0):
            act.wait_ge(var_ready, count + 1)
            nc.scalar.activation(rs, vr, ACT.Ln).then_inc(ln_done, 1)
            act.wait_ge(ln_done, count + 1 + extra)
            nc.scalar.activation(rs, rs, ACT.Exp, scale=-0.5).then_inc(rstd_ready, 1)

        def either(engine, program):
            narrow = engine.value_load(narrow_i[0:1, 0:1], min_val=0, max_val=1)
            with engine.If(narrow > 0):
                program(True)
            with engine.Else():
                program(False)

        def first_node(engine, tile):
            return engine.value_load(first_i[0:1, bass.ds(tile, 1)], min_val=0, max_val=N)

        def sum_place(narrow, b, k):
            if narrow:
                return b // 2, 0, b % 2 == 0 and k == 0, b % 2 == 1 and k == KT - 1
            return b % 2, k * P, True, True

        def sum_bank_free(pe, acc_step, i, b, narrow):
            if not narrow:
                pe.wait_ge(acc_step, (i * SLOTS + b) * KT + 4)
            elif b % 2 == 0:
                pe.wait_ge(acc_step, 2 * i + b // 2 + 7)

        def accumulate(dve, acc_step, agg, before, i, b, narrow, window, part):
            n = i * SLOTS + b
            if narrow:
                if b >= 2:
                    h = b - 2
                    w = window(first_node(dve, i * ROUND))
                    dve.wait_ge(agg, i * SLOTS + 2 * h + 2 + before)
                    dve.wait_ge(acc_step, 2 * i + h + 8)
                    dve.tensor_tensor(w, w, part(h, 0), ALU.add).then_inc(acc_step, 1)
                return
            dve.wait_ge(agg, n + 1 + before)
            for k in range(KT):
                w = window(first_node(dve, n * KT + k))
                dve.wait_ge(acc_step, n * KT + 8 + k)
                dve.tensor_tensor(w, w, part(b % 2, k * P), ALU.add).then_inc(acc_step, 1)

        def onehot(dve, dst, n):
            return dve.tensor_tensor(
                dst, iota_f[:, :].unsqueeze(1).to_broadcast([P, KT, P]),
                over(lr[:, bass.ds(n * KT, KT)], P, KT, P), ALU.is_equal)

        ld = sem("gat_tables_loads")
        staged, mm, evac, used, hs = sem("gat_x_staged"), sem("gat_h_ready"), sem("gat_h_copied"), sem("gat_scores_ready"), sem("gat_dve")
        stored, row_free = sem("gat_rows_stored"), sem("gat_row_free")
        A = Arena(TMP, 0, TW)
        xs = A.take(CN)
        row = A.take(CT, ROW0)
        prod = A.take(CT, P)
        adb = A.take(CT, H0)
        W_gat = WA[:, 0:2 * P]
        with nc.Block() as block:
            @block.sync
            def _(sp):
                sp.dma_start(WA[:, 0:P], a["L0_gnn_W"]).then_inc(ld, 16)
                sp.dma_start(WA[:, P:2 * P], a["L0_gnn_skip_W"]).then_inc(ld, 16)
                sp.dma_start(rows[:, 0:P], row_bc("att_src")).then_inc(ld, 16)
                sp.dma_start(rows[:, P:2 * P], row_bc("att_dst")).then_inc(ld, 16)
                sp.sem_inc(row_free, 1)
                with sp.Fori(0, NC) as c:
                    sp.wait_ge(evac, PARTS * (c + 1))
                    met(sp)
                    sp.wait_ge(used, c + 2)
                    met(sp)
                    sp.dma_start(table_rows(tab0_d, c, ROW0), row).then_inc(stored, 16)
                    sp.dma_start(table_rows(adt_d, c, H0), adb).then_inc(stored, 16)
                    sp.wait_ge(stored, 32 * (c + 1))
                    sp.sem_inc(row_free, 1)

            @block.tensor
            def _(pe):
                pe.wait_ge(ld, 64)
                pe.sem_inc(mm, 1)
                with pe.Fori(0, NC) as c:
                    pe.wait_ge(staged, c + 1)
                    pe.wait_ge(used, c + 1)
                    for k in range(CT):
                        i = nc.tensor.matmul(psv(k // PT, PT, P)[:, k % PT, :], xs[:, k * P:(k + 1) * P], WA[:, 0:P], start=True, stop=True)
                    i.then_inc(mm, 1)

            @block.scalar
            def _(act):
                with act.Fori(0, NC) as c:
                    act.wait_ge(mm, c + 1)
                    met(act)
                    nc.scalar.copy(xs, xT[:, bass.ds(c * CN, CN)]).then_inc(staged, 1)
                    act.wait_ge(mm, c + 2)
                    act.wait_ge(row_free, c + 1)
                    for j in range(PARTS):
                        nc.scalar.copy(row[:, j * PT:(j + 1) * PT, 0:P], psv(j, PT, P)).then_inc(evac, 1)

            @block.vector
            def _(dve):
                dve.wait_ge(ld, 64)
                dve.sem_inc(used, 1)
                with dve.Fori(0, NC) as c:
                    s = Steps(dve, hs, c * 5)
                    dve.wait_ge(mm, c + 2)
                    dve.wait_ge(row_free, c + 1)
                    dve.wait_ge(evac, PARTS * (c + 1))
                    h = row[:, :, 0:P]
                    sc = asd[:, bass.ds(c * CT, CT), :]
                    for j, dstv in enumerate((row[:, :, P:ROW0], adb)):
                        s.link(dve.tensor_tensor(prod, h, rows[:, j * P:(j + 1) * P].unsqueeze(1).to_broadcast([P, CT, P]), ALU.mult))
                        s.link(dve.tensor_reduce(dstv, prod.rearrange("p t (h c) -> p t h c", c=C0), AX.X, ALU.add))
                    met(dve)
                    s.link(dve.tensor_copy(sc[:, :, 0:H0], row[:, :, P:ROW0]))
                    met(dve)
                    dve.tensor_copy(sc[:, :, H0:2 * H0], adb).then_inc(used, 1)

        idx_ready, lr_ready, ad_ready = sems("g1_idx", 2), sems("g1_local_dst", 2), sems("g1_dst_rows", 2)
        gath, kept = sems("g1_gathered"), sems("g1_kept")
        as_copied, oh_done, ad_mm, ad_copied = sem("g1_src_scores"), sem("g1_onehot"), sem("g1_product"), sem("g1_dst_scores")
        A = Arena(TMP, 0, TW)
        idx = A.take(2, HALF, dtype=U32)
        g = A.take(SLOTS, KT, ROW0)
        lrb = A.take(SLOTS, KT * P)
        ohT = A.take(2, KT * P)
        adw = A.take(2, HALF, H0)

        def first_pass_loads(sp, narrow, load_windows, load_rows, gath, oh_done, products):
            def load_idx(i, h):
                sp.dma_start(idx[:, h, :], a["src_et"][:, bass.ds((i * 2 + h) * HALF, HALF)]).then_inc(idx_ready[h], 16)

            for h in range(2):
                load_idx(0, h)
                load_rows(0, h)
                load_windows(0, h)
            with sp.Fori(0, NR - 1) as i:
                for h in range(2):
                    last = i * SLOTS + 2 * h + 1
                    for b in (2 * h, 2 * h + 1):
                        sp.wait_ge(gath[b], 16 * KT * (i + 1))
                    met(sp)
                    load_idx(i + 1, h)
                    sp.wait_ge(oh_done, last + 1)
                    met(sp)
                    load_rows(i + 1, h)
                    sp.wait_ge(products, last + 3)
                    met(sp)
                    load_windows(i + 1, h)

        def load_node_windows(sp, narrow, i, h, windows, table, ready):
            for k in range(1 if narrow else HALF):
                first = first_node(sp, (i * 2 + h) * HALF + k)
                sp.dma_start(windows[:, h, k, :], table[bass.ds(first, P), :]).then_inc(ready[h], 16)

        def window_of(narrow, b, k):
            return 0 if narrow else (b % 2) * KT + k

        def windows_loaded(narrow, i):
            return 16 * (1 if narrow else HALF) * (i + 1)

        with nc.Block() as block:
            @block.sync
            def _(sp):
                def program(narrow):
                    def load_rows(i, h):
                        sp.dma_start(lrb[:, 2 * h:2 * h + 2, :].rearrange("p b e -> p (b e)"),
                                     lrow_d[0, bass.ds((i * 2 + h) * HALF * P, HALF * P)].partition_broadcast(P)).then_inc(lr_ready[h], 16)

                    first_pass_loads(sp, narrow, lambda i, h: load_node_windows(sp, narrow, i, h, adw, adt_d, ad_ready),
                                     load_rows, gath, oh_done, ad_mm)
                either(sp, program)
                for b in range(SLOTS):
                    sp.wait_ge(kept[b], 16 * (NR + 1))

            @block.gpsimd
            def _(pool):
                with pool.Fori(0, NR) as i:
                    for b in range(SLOTS):
                        pool.wait_ge(idx_ready[b // 2], 16 * (i + 1))
                        pool.wait_ge(kept[b], 16 * (i + 1))
                        pool.wait_ge(as_copied, i * SLOTS + b + 1)
                        met(pool)
                        for k in range(KT):
                            pool.indirect_dma_start(
                                out=g[:, b, k, :], out_offset=None, in_=tab0_d,
                                in_offset=bass.IndirectOffsetOnAxis(ap=idx[:, b // 2, (b % 2) * KT + k:(b % 2) * KT + k + 1], axis=0)).then_inc(gath[b], 16)

            @block.scalar
            def _(act):
                for b in range(SLOTS):
                    act.sem_inc(kept[b], 16)
                act.sem_inc(as_copied, SLOTS)
                with act.Fori(0, NR) as i:
                    for b in range(SLOTS):
                        t = (i * SLOTS + b) * KT
                        act.wait_ge(gath[b], 16 * KT * (i + 1))
                        met(act)
                        act.dma_start(edge_d[:, bass.ds(t, KT), :], g[:, b, :, 0:P]).then_inc(kept[b], 16)
                        nc.scalar.copy(as_e[:, bass.ds(t, KT), :], g[:, b, :, P:ROW0]).then_inc(as_copied, 1)

            @block.vector
            def _(dve):
                dve.sem_inc(ad_copied, 2)
                with dve.Fori(0, NR) as i:
                    for b in range(SLOTS):
                        n = i * SLOTS + b
                        dve.wait_ge(lr_ready[b // 2], 16 * (i + 1))
                        dve.wait_ge(ad_mm, n + 1)
                        dve.tensor_scalar(ohT[:, b % 2, :], lrb[:, b, :], iota_p[:, 0:1], None, ALU.is_equal).then_inc(oh_done, 1)
                        dve.wait_ge(ad_mm, n + 3)
                        met(dve)
                        dve.tensor_copy(ad_e[:, bass.ds(n * KT, KT), :], psv(b % 2, KT, H0)).then_inc(ad_copied, 1)

            @block.tensor
            def _(pe):
                pe.sem_inc(ad_mm, 2)

                def program(narrow):
                    with pe.Fori(0, NR) as i:
                        for b in range(SLOTS):
                            n = i * SLOTS + b
                            pe.wait_ge(oh_done, n + 1)
                            pe.wait_ge(ad_ready[b // 2], windows_loaded(narrow, i))
                            pe.wait_ge(ad_copied, n + 1)
                            ps = psv(b % 2, KT, H0)
                            for k in range(KT):
                                m = nc.tensor.matmul(ps[:, k, :], ohT[:, b % 2, k * P:(k + 1) * P], adw[:, b // 2, window_of(narrow, b, k), :],
                                                     start=True, stop=True)
                            m.then_inc(ad_mm, 1)
                either(pe, program)

        ld, sd, rt, rc, bt, mt = (sem("seg_loads"), sem("seg_dve"), sem("seg_rows_t"), sem("seg_rows_copied"), sem("seg_carry_t"), sem("seg_max_t"))
        mused, madd = sem("seg_max_used"), sem("seg_carry_ready")
        xn_flat = xn[:, :, :].rearrange("p t f -> p (t f)")
        A = Arena(xn_flat, 0, NP)
        negF = A.take(RW, parts=NR)
        negB = A.take(RW, parts=NR)
        R = A.take(RW, parts=NR)
        A = Arena(TMP, 0, TW)
        F = A.take(RW, parts=NR)
        Bk = A.take(RW, parts=NR)
        rowi = A.take(RW, parts=NR, dtype=I32)
        ends = A.take(4, parts=NR)
        carry = A.take(2, parts=NR)
        A = Arena(WB, 0, 5 * P)
        carry_r = A.take(2, NR + 1, parts=1)
        resets_r = A.take(2, NR, parts=1)
        ends_r = A.take(2, NR, parts=1)
        with nc.Block() as block:
            @block.sync
            def _(sp):
                sp.dma_start(rowi, a["dst_rows"]).then_inc(ld, 16)
                sp.dma_start(F.bitcast(I32), a["dst_prev_rows"]).then_inc(ld, 16)
                sp.dma_start(Bk.bitcast(I32), a["dst_next_rows"]).then_inc(ld, 16)

            @block.tensor
            def _(pe):
                for h in range(H0):
                    for q in range(ROUND // KT):
                        n = h * (ROUND // KT) + q
                        if n >= 2:
                            pe.wait_ge(rc, n - 1)
                        for k in range(KT):
                            m = nc.tensor.transpose(psv(n % 2, KT, P, parts=NR)[:, k, :], as_e[:, q * KT + k::ROUND, h], ident[:, :])
                        m.then_inc(rt, 1)
                    pe.wait_ge(madd, 3 * h + 1)
                    for j in range(2):
                        nc.tensor.matmul(PS[2][0:1, 0, j * P:j * P + NR], ends[:, j:j + 1], ident[0:NR, 0:NR], start=True, stop=True)
                        m = nc.tensor.matmul(PS[2][0:1, 1, j * P:j * P + NR], ends[:, 2 + j:3 + j], ident[0:NR, 0:NR], start=True, stop=True)
                    m.then_inc(bt, 1)
                    pe.wait_ge(madd, 3 * h + 2)
                    nc.tensor.matmul(PS[2][0:NR, 0, 256:257], carry_r[:, 0, 0:NR], ones[0:1, 0:1], start=True, stop=True)
                    nc.tensor.matmul(PS[2][0:NR, 0, 257:258], carry_r[:, 1, 1:NR + 1], ones[0:1, 0:1], start=True, stop=True).then_inc(bt, 1)
                    pe.wait_ge(madd, 3 * h + 3)
                    for q in range(ROUND // KT):
                        n = h * (ROUND // KT) + q
                        if n >= 1:
                            pe.wait_ge(mused, n)
                        for k in range(KT):
                            m = nc.tensor.transpose(PS[3][:, 0, k * NR:(k + 1) * NR], F[:, (q * KT + k) * P:(q * KT + k + 1) * P], ident[0:NR, 0:NR])
                        m.then_inc(mt, 1)

            @block.scalar
            def _(act):
                for h in range(H0):
                    for q in range(ROUND // KT):
                        n = h * (ROUND // KT) + q
                        act.wait_ge(rt, n + 1)
                        if q == 0 and h:
                            act.wait_ge(madd, 3 * h)
                        nc.scalar.copy(R[:, q * KT * P:(q + 1) * KT * P], psv(n % 2, KT * P, parts=NR)).then_inc(rc, 1)

            @block.vector
            def _(dve):
                s = Steps(dve, sd)
                dve.wait_ge(ld, 48)
                s.link(dve.tensor_tensor(negF, rowi, F.bitcast(I32), ALU.not_equal))
                s.link(dve.tensor_tensor(negB, rowi, Bk.bitcast(I32), ALU.not_equal))
                s.link(dve.tensor_scalar(negF, negF, -BIG, None, ALU.mult))
                s.link(dve.tensor_scalar(negB, negB, -BIG, None, ALU.mult))
                s.link(dve.tensor_reduce(ends[:, 2:3], negF, AX.X, ALU.min))
                s.link(dve.tensor_reduce(ends[:, 3:4], negB, AX.X, ALU.min))
                for h in range(H0):
                    dve.wait_ge(rc, (h + 1) * (ROUND // KT))
                    for final in range(2):
                        f0 = carry[:, 0:1] if final else -BIG
                        b0 = carry[:, 1:2] if final else -BIG
                        s.link(dve.tensor_tensor_scan(F, negF, R, f0, ALU.add, ALU.max))
                        s.link(dve.tensor_tensor_scan(Bk[:, ::-1], negB[:, ::-1], R[:, ::-1], b0, ALU.add, ALU.max))
                        if not final:
                            s.link(dve.tensor_copy(ends[:, 0:1], F[:, RW - 1:RW]))
                            s.link(dve.tensor_copy(ends[:, 1:2], Bk[:, 0:1]))
                            dve.sem_inc(madd, 1)
                            dve.wait_ge(bt, 2 * h + 1)
                            s.link(dve.tensor_copy(ends_r[:, :, 0:NR], PS[2][0:1, 0, 0:2 * P].rearrange("p (a b) -> p a b", a=2)[:, :, 0:NR]))
                            s.link(dve.tensor_copy(resets_r, PS[2][0:1, 1, 0:2 * P].rearrange("p (a b) -> p a b", a=2)[:, :, 0:NR]))
                            s.link(dve.memset(carry_r, -BIG))
                            s.link(dve.tensor_tensor_scan(carry_r[:, 0, 1:NR + 1], resets_r[:, 0, :], ends_r[:, 0, 0:NR], -BIG, ALU.add, ALU.max))
                            s.link(dve.tensor_tensor_scan(carry_r[:, 1, 0:NR][:, ::-1], resets_r[:, 1, :][:, ::-1], ends_r[:, 1, 0:NR][:, ::-1], -BIG, ALU.add, ALU.max))
                            dve.sem_inc(madd, 1)
                            dve.wait_ge(bt, 2 * h + 2)
                            s.link(dve.tensor_copy(carry, PS[2][0:NR, 0, 256:258]))
                    s.link(dve.tensor_tensor(F, F, Bk, ALU.max))
                    dve.sem_inc(madd, 1)
                    for q in range(ROUND // KT):
                        n = h * (ROUND // KT) + q
                        dve.wait_ge(mt, n + 1)
                        m = pm0[:, :, H0 + h].rearrange("p (r q) -> p q r", q=ROUND)[:, q * KT:(q + 1) * KT, :]
                        dve.tensor_copy(m, PS[3][:, 0, 0:KT * NR].rearrange("p (k r) -> p k r", r=NR)).then_inc(mused, 1)

        ld, sd, pa = sem("w_loads"), sem("w_dve"), sem("w_exp")
        A = Arena(TMP, 0, TW)
        di = A.take(T, dtype=I32)
        dp = A.take(T, dtype=I32)
        st = A.take(T)
        with nc.Block() as block:
            @block.sync
            def _(sp):
                sp.dma_start(di, a["dst_et"]).then_inc(ld, 16)
                sp.dma_start(dp, a["dst_prev_et"]).then_inc(ld, 16)
                sp.dma_start(xn[:, :, :], a["x"].rearrange("(t p) f -> p t f", p=P)).then_inc(ld, 16)
                sp.wait_ge(ld, 48)

            @block.vector
            def _(dve):
                s = Steps(dve, sd)
                pe_, me_ = pm0[:, :, 0:H0], pm0[:, :, H0:2 * H0]
                s.link(dve.tensor_tensor(as_e, as_e, ad_e, ALU.add))
                s.link(dve.scalar_tensor_tensor(pe_, as_e, 0.2, as_e, ALU.mult, ALU.max))
                s.link(dve.tensor_tensor(me_, me_, ad_e, ALU.add))
                s.link(dve.scalar_tensor_tensor(me_, me_, 0.2, me_, ALU.mult, ALU.max))
                s.link(dve.tensor_tensor(pe_, pe_, me_, ALU.subtract))
                dve.sem_inc(pa, 1)
                dve.wait_ge(ld, 48)
                s.link(dve.tensor_tensor(st, di, dp, ALU.not_equal))
                s.link(dve.tensor_tensor(me_, me_, over(st, P, T, H0), ALU.mult))
                s.link(dve.memset(pm0[:, :, 2 * H0:Z0], 1.0))

            @block.scalar
            def _(act):
                act.wait_ge(pa, 1)
                nc.scalar.activation(pm0[:, :, 0:H0], pm0[:, :, 0:H0], ACT.Exp).then_inc(pa, 1)

        def weighted_pass(tag, pm, heads, width, side):
            loaded, oh_done, msg_done, side_done, agg, acc_step = (sems(tag + "_rows"), sem(tag + "_onehot"), sem(tag + "_messages"),
                                                                   sem(tag + "_side"), sem(tag + "_sums"), sem(tag + "_added"))
            A = Arena(TMP, 0, TW)
            msg = A.take(SLOTS, KT, P + side)
            oh = A.take(SLOTS, KT, P)
            by_node = A.take(2, P + side)
            node_copied, turned = sem(tag + "_by_node"), sem(tag + "_turned")
            with nc.Block() as block:
                @block.sync
                def _(sp):
                    def load(i, b):
                        sp.dma_start(msg[:, b, :, 0:P], edge_d[:, bass.ds((i * SLOTS + b) * KT, KT), :]).then_inc(loaded[b], 16)
                    for b in range(SLOTS):
                        load(0, b)
                    with sp.Fori(0, NR - 1) as i:
                        for b in range(SLOTS):
                            sp.wait_ge(agg, i * SLOTS + b + 1 + SLOTS)
                            met(sp)
                            load(i + 1, b)

                @block.scalar
                def _(act):
                    def weights(n, b):
                        act.wait_ge(agg, n + 1)
                        met(act)
                        nc.scalar.copy(msg[:, b, :, P:P + side], pm[:, bass.ds(n * KT, KT), :]).then_inc(side_done, 1)

                    def program(narrow):
                        def round_(i, last):
                            for b in range(SLOTS):
                                if b + 2 < SLOTS or not last:
                                    weights(i * SLOTS + b + 2, (b + 2) % SLOTS)
                                if narrow and b % 2 == 1:
                                    act.wait_ge(agg, i * SLOTS + b + 1 + SLOTS)
                                    nc.scalar.copy(by_node[:, b // 2, :], PS[2][:, b // 2, 0:P + side]).then_inc(node_copied, 1)

                        weights(0, 0)
                        weights(1, 1)
                        with act.Fori(0, NR - 1) as i:
                            round_(i, False)
                        round_(NR - 1, True)
                    either(act, program)

                @block.tensor
                def _(pe):
                    pe.sem_inc(agg, SLOTS)

                    def turn(i, h):
                        pe.wait_ge(node_copied, 2 * i + h + 1)
                        sum_bank_free(pe, acc_step, i, 2 * h, True)
                        nc.tensor.transpose(PS[h][:, 0, 0:P], by_node[:, h, 0:P], ident[:, :])
                        nc.tensor.transpose(PS[h][0:side, 1, 0:P], by_node[:, h, P:P + side], ident[:, :]).then_inc(turned, 1)

                    def program(narrow):
                        def round_(i, first):
                            for b in range(SLOTS):
                                n = i * SLOTS + b
                                pe.wait_ge(oh_done, n + 1)
                                pe.wait_ge(msg_done, n + 1)
                                pe.wait_ge(side_done, n + 1)
                                if not narrow:
                                    sum_bank_free(pe, acc_step, i, b, narrow)
                                for k in range(KT):
                                    o = oh[:, b, k, :]
                                    bank, c, start, stop = sum_place(narrow, b, k)
                                    if narrow:
                                        m = nc.tensor.matmul(PS[2][:, bank, 0:P + side], o, msg[:, b, k, :], start=start, stop=stop)
                                    else:
                                        nc.tensor.matmul(PS[bank][:, 0, c:c + P], msg[:, b, k, 0:P], o, start=start, stop=stop)
                                        m = nc.tensor.matmul(PS[bank][0:side, 1, c:c + P], msg[:, b, k, P:P + side], o, start=start, stop=stop)
                                m.then_inc(agg, 1)
                                if narrow and b == 0 and not first:
                                    turn(i - 1, 1)
                                if narrow and b == 2:
                                    turn(i, 0)

                        round_(0, True)
                        with pe.Fori(1, NR) as i:
                            round_(i, False)
                        if narrow:
                            turn(NR - 1, 1)
                    either(pe, program)

                @block.vector
                def _(dve):
                    def messages(i, b):
                        n = i * SLOTS + b
                        dve.wait_ge(agg, n + 1)
                        onehot(dve, oh[:, b, :, :], n).then_inc(oh_done, 1)
                        dve.wait_ge(loaded[b], 16 * (i + 1))
                        dve.tensor_tensor(
                            msg[:, b, :, 0:P].rearrange("p k (h c) -> p k h c", c=width),
                            msg[:, b, :, 0:P].rearrange("p k (h c) -> p k h c", c=width),
                            over(pm[:, bass.ds(n * KT, KT), 0:heads], P, KT, heads, width), ALU.mult).then_inc(msg_done, 1)

                    def add_half(i, h):
                        at = acc2[:, :, bass.ds(first_node(dve, i * ROUND), P)]
                        dve.wait_ge(turned, 2 * i + h + 1)
                        dve.wait_ge(acc_step, 2 * i + h + 8)
                        dve.tensor_tensor(at, at, PS[h][:, :, 0:P], ALU.add).then_inc(acc_step, 1)

                    def program(narrow):
                        def round_(i, first, last):
                            for b in range(SLOTS):
                                if b < SLOTS - 1:
                                    messages(i, b + 1)
                                elif not last:
                                    messages(i + 1, 0)
                                if not narrow:
                                    accumulate(dve, acc_step, agg, SLOTS, i, b, narrow, lambda first: acc2[:, :, bass.ds(first, P)],
                                               lambda bank, c: PS[bank][:, :, c:c + P])
                                elif b == 1 and not first:
                                    add_half(i - 1, 1)
                                elif b == 3:
                                    add_half(i, 0)

                        messages(0, 0)
                        round_(0, True, False)
                        with dve.Fori(1, NR - 1) as i:
                            round_(i, False, False)
                        round_(NR - 1, False, True)
                        if narrow:
                            add_half(NR - 1, 1)

                    dve.memset(AC[:, 0:2 * NP], 0.0).then_inc(acc_step, 1)
                    for j in range(2):
                        dve.memset(PS[j][:, 1, :], 0.0).then_inc(acc_step, 1)
                    dve.sem_inc(acc_step, 5)
                    either(dve, program)

        weighted_pass("gat_sum", pm0, H0, C0, Z0)

        ld, staged, mm, read, used, fs, acts, vrdy, rrdy, lnd, xt, xc = (sem("gat_end_loads"), sem("gat_end_staged"), sem("gat_end_products"),
            sem("gat_end_read"), sem("gat_end_used"), sem("gat_end_dve"), sem("gat_end_exp"), sem("gat_end_var"), sem("gat_end_rstd"),
            sem("gat_end_ln"), sem("gat_end_x_t"), sem("gat_end_x_copied"))
        A = Arena(PM, 0, T * Z0)
        rb = A.take(4, P)
        bsum = A.take(P)
        xs = A.take(CN)
        ac = A.take(CN)
        zc = A.take(CN)
        t = A.take(CT, P)
        q = A.take(CT, P)
        z = A.take(CT, Z0)
        sv = A.take(CT, H0)
        sm, vr, rs = A.take(CT), A.take(CT), A.take(CT)

        def residual_out(dve, s, t, q, sm, vr, rs, vrdy, rrdy, c, per, j):
            s.link(dve.tensor_tensor(t, t, xn[:, bass.ds(c * CT, CT), :], ALU.add))
            layer_norm(dve, s, t, q, sm, vr, rs, vrdy, rrdy, c * per + j)
            met(dve)
            s.link(dve.tensor_copy(xn[:, bass.ds(c * CT, CT), :], t))

        def part(j):
            return slice(j * PT, (j + 1) * PT)

        def transpose_x(pe, t, banks, xt):
            for j in range(PARTS):
                for k in range(PT):
                    m = nc.tensor.transpose(psv(banks[j], PT, P)[:, k, :], t[:, j * PT + k, :], ident[:, :])
                m.then_inc(xt, 1)

        def keep_x(act, c, banks, xt, xc):
            for j in range(PARTS):
                act.wait_ge(xt, PARTS * c + j + 1)
                met(act)
                nc.scalar.copy(xT[:, bass.ds(c * CN + j * PN, PN)], psv(banks[j], PN)).then_inc(xc, 1)

        with nc.Block() as block:
            @block.sync
            def _(sp):
                for j, n_ in enumerate(("L0_gnn_gat_bias", "L0_gnn_skip_b", "L0_gnn_ln_g", "L0_gnn_ln_b")):
                    sp.dma_start(rb[:, j, :], row_bc(n_)).then_inc(ld, 16)
                sp.wait_ge(ld, 64)

            @block.scalar
            def _(act):
                with act.Fori(0, NC) as c:
                    act.wait_ge(mm, 7 * c + 1)
                    met(act)
                    nc.scalar.copy(zc[0:Z0, :], acc2[0:Z0, 1, bass.ds(c * CN, CN)]).then_inc(staged, 1)
                    nc.scalar.copy(xs, xT[:, bass.ds(c * CN, CN)]).then_inc(staged, 1)
                    nc.scalar.copy(ac, acc2[:, 0, bass.ds(c * CN, CN)]).then_inc(staged, 1)
                    act.wait_ge(acts, 2 * c + 1)
                    nc.scalar.activation(sv, sv, ACT.Exp).then_inc(acts, 1)
                    for j in range(2):
                        rstd_act(act, lnd, vr, rs, vrdy, rrdy, 2 * c + j)
                    keep_x(act, c, (3, 0), xt, xc)

            @block.tensor
            def _(pe):
                pe.sem_inc(mm, 1)
                pe.sem_inc(xc, PARTS)
                with pe.Fori(0, NC) as c:
                    pe.wait_ge(staged, 3 * c + 2)
                    pe.wait_ge(xc, PARTS * (c + 1))
                    for j in range(PARTS):
                        w = [slice((j * PT + k) * P, (j * PT + k + 1) * P) for k in range(PT)]
                        if j:
                            pe.wait_ge(read, 6 * c + 1)
                        for k in range(PT):
                            m = nc.tensor.matmul(psv(1, PT, P)[:, k, :], xs[:, w[k]], WA[:, 0:P], start=True, stop=True)
                        m.then_inc(mm, 1)
                        if j == 0:
                            for k in range(CT):
                                m = nc.tensor.transpose(psv(3, CT, Z0)[:, k, :], zc[0:Z0, k * P:(k + 1) * P], ident[0:Z0, 0:Z0])
                            m.then_inc(mm, 1)
                            pe.wait_ge(staged, 3 * c + 3)
                        else:
                            pe.wait_ge(read, 6 * c + 2)
                        for k in range(PT):
                            m = nc.tensor.transpose(psv(0, PT, P)[:, k, :], ac[:, w[k]], ident[:, :])
                        m.then_inc(mm, 1)
                        if j:
                            pe.wait_ge(read, 6 * c + 3)
                        for k in range(PT):
                            m = nc.tensor.matmul(psv(2, PT, P)[:, k, :], xs[:, w[k]], WA[:, P:2 * P], start=True, stop=True)
                        m.then_inc(mm, 1)
                    pe.wait_ge(used, c + 1)
                    transpose_x(pe, t, (3, 0), xt)

            @block.vector
            def _(dve):
                s = Steps(dve, fs)
                dve.wait_ge(ld, 64)
                s.link(dve.tensor_tensor(bsum, rb[:, 0, :], rb[:, 1, :], ALU.add))
                per = 60
                with dve.Fori(0, NC) as c:
                    s = Steps(dve, fs, c * per + 1)
                    heads = "p t (h c) -> p t h c"
                    a_s, a_d = asd[:, bass.ds(c * CT, CT), 0:H0], asd[:, bass.ds(c * CT, CT), H0:2 * H0]
                    s.link(dve.tensor_tensor(sv, a_s, a_d, ALU.add))
                    s.link(dve.scalar_tensor_tensor(sv, sv, 0.2, sv, ALU.mult, ALU.max))
                    dve.wait_ge(mm, 7 * c + 3)
                    s.link(dve.tensor_copy(z, psv(3, CT, Z0)))
                    s.link(dve.tensor_scalar(deg[:, bass.ds(c * CT, CT)], z[:, :, 2 * H0], 1.0, None, ALU.add))
                    s.link(dve.tensor_tensor(sv, sv, z[:, :, H0:2 * H0], ALU.subtract))
                    dve.sem_inc(acts, 1)
                    dve.wait_ge(acts, 2 * c + 2)
                    s.link(dve.tensor_tensor(z[:, :, 0:H0], z[:, :, 0:H0], sv, ALU.add))
                    s.link(dve.tensor_scalar(z[:, :, 0:H0], z[:, :, 0:H0], SM_EPS, None, ALU.add))
                    s.link(dve.reciprocal(z[:, :, 0:H0], z[:, :, 0:H0]))
                    for j in range(PARTS):
                        tj = t[:, part(j), :]
                        dve.wait_ge(mm, 7 * c + 3 + 3 * j)
                        if j == 0:
                            dve.wait_ge(xc, PARTS * (c + 1))
                        s.link(dve.tensor_tensor(tj.rearrange(heads, c=C0), psv(1, PT, P).rearrange(heads, c=C0), over(sv[:, part(j), :], P, PT, H0, C0), ALU.mult))
                        dve.sem_inc(read, 1)
                        dve.wait_ge(mm, 7 * c + 4 + 3 * j)
                        s.link(dve.tensor_tensor(tj, tj, psv(0, PT, P), ALU.add))
                        dve.sem_inc(read, 1)
                        s.link(dve.tensor_tensor(tj.rearrange(heads, c=C0), tj.rearrange(heads, c=C0), over(z[:, part(j), 0:H0], P, PT, H0, C0), ALU.mult))
                        dve.wait_ge(mm, 7 * c + 5 + 3 * j)
                        s.link(dve.tensor_tensor(tj, tj, psv(2, PT, P), ALU.add))
                        dve.sem_inc(read, 1)
                    s.link(dve.tensor_tensor(t, t, bsum.unsqueeze(1).to_broadcast([P, CT, P]), ALU.add))
                    layer_norm(dve, s, t, q, sm, vr, rs, vrdy, rrdy, 2 * c)
                    s.link(dve.tensor_tensor(t, t, rb[:, 2, :].unsqueeze(1).to_broadcast([P, CT, P]), ALU.mult))
                    s.link(dve.tensor_tensor(t, t, rb[:, 3, :].unsqueeze(1).to_broadcast([P, CT, P]), ALU.add))
                    residual_out(dve, s, t, q, sm, vr, rs, vrdy, rrdy, c, 2, 1)
                    dve.sem_inc(fs, per - s.n)
                    dve.sem_inc(used, 1)


        layer_ends()

        ld, staged, mm, lin, bs, bact, used, stored, row_free = (sem("gcn_loads"), sem("gcn_staged"), sem("gcn_products"), sem("gcn_linear"),
            sem("gcn_dve"), sem("gcn_act"), sem("gcn_used"), sem("gcn_stored"), sem("gcn_row_free"))
        A = Arena(TMP, 0, TW)
        ys = A.take(CN)
        hrow = A.take(CT, P)
        A = Arena(PM, 0, T * Z0)
        x1 = A.take(NP)
        sq = A.take(N)
        with nc.Block() as block:
            @block.sync
            def _(sp):
                for j, n_ in enumerate(("L1_gnn_Wlin_T", "L1_gnn_Wg_T")):
                    sp.dma_start(WA[:, j * P:(j + 1) * P], a[n_]).then_inc(ld, 16)
                for j, n_ in enumerate(("L1_gnn_blin", "L1_gnn_gamma", "L1_gnn_beta")):
                    sp.dma_start(cols[:, j:j + 1], col_in(n_)).then_inc(ld, 16)
                sp.sem_inc(row_free, 1)
                with sp.Fori(0, NC) as c:
                    sp.wait_ge(used, c + 2)
                    met(sp)
                    sp.dma_start(table_rows(tab1_d, c, P), hrow).then_inc(stored, 16)
                    sp.wait_ge(stored, 16 * (c + 1))
                    sp.sem_inc(row_free, 1)

            @block.tensor
            def _(pe):
                pe.wait_ge(ld, 80)
                with pe.Fori(0, NC) as c:
                    for j in range(PARTS):
                        pe.wait_ge(lin, PARTS * c + j + 1)
                        for k in range(2):
                            m = nc.tensor.matmul(PS[j][:, k, 0:QN], WA[:, 0:P], xT[:, bass.ds(c * CN + j * PN + k * QN, QN)], start=True, stop=True)
                        m.then_inc(mm, 1)
                with pe.Fori(0, NC) as c:
                    pe.wait_ge(staged, c + 1)
                    pe.wait_ge(used, c + 1)
                    for k in range(CT):
                        m = nc.tensor.matmul(psv(2 + k // PT, PT, P)[:, k % PT, :], ys[:, k * P:(k + 1) * P], WA[:, P:2 * P], start=True, stop=True)
                    m.then_inc(mm, 1)

            @block.scalar
            def _(act):
                act.sem_inc(lin, PARTS)
                act.wait_ge(ld, 80)
                with act.Fori(0, NC) as c:
                    for j in range(PARTS):
                        act.wait_ge(mm, PARTS * c + j + 1)
                        met(act)
                        nc.scalar.activation(x1[:, bass.ds(c * CN + j * PN, PN)].rearrange("p (a b) -> p a b", a=2), PS[j][:, :, 0:QN],
                                             ACT.Identity, bias=cols[:, 0:1]).then_inc(lin, 1)
                act.wait_ge(bs, 3)
                nc.scalar.activation(sq, x1[:, 0:N], ACT.Square, accum_out=cols[:, 4:5]).then_inc(bact, 1)
                act.wait_ge(bs, 5)
                nc.scalar.activation(cols[:, 6:7], cols[:, 5:6], ACT.Ln).then_inc(bact, 1)
                nc.scalar.activation(dinv[:, :], deg, ACT.Ln).then_inc(bact, 1)
                act.wait_ge(bact, 3)
                nc.scalar.activation(cols[:, 6:7], cols[:, 6:7], ACT.Exp, scale=-0.5).then_inc(bact, 1)
                nc.scalar.activation(dinv[:, :], dinv[:, :], ACT.Exp, scale=-0.5).then_inc(bact, 1)
                act.wait_ge(bs, 16)
                with act.Fori(0, NC) as c:
                    act.wait_ge(mm, PARTS * NC + c)
                    met(act)
                    nc.scalar.copy(ys, x1[:, bass.ds(c * CN, CN)]).then_inc(staged, 1)

            @block.vector
            def _(dve):
                s = Steps(dve, bs)
                dve.wait_ge(lin, PARTS * (NC + 1))
                s.link(dve.tensor_reduce(cols[:, 3:4], x1[:, 0:N], AX.X, ALU.add))
                s.link(dve.tensor_scalar(cols[:, 3:4], cols[:, 3:4], -1.0 / N, None, ALU.mult))
                s.link(dve.tensor_scalar(x1, x1, cols[:, 3:4], None, ALU.add))
                dve.wait_ge(bact, 1)
                s.link(dve.tensor_scalar(cols[:, 5:6], cols[:, 4:5], 1.0 / N, BN_EPS, ALU.mult, ALU.add))
                s.link(dve.tensor_copy(dgc, deg))
                dve.wait_ge(bact, 5)
                newton(dve, s, cols[:, 6:7], cols[:, 5:6], cols[:, 7:8])
                newton(dve, s, dinv[:, :], dgc, dgw)
                s.link(dve.tensor_tensor(cols[:, 6:7], cols[:, 6:7], cols[:, 1:2], ALU.mult))
                s.link(dve.tensor_scalar(x1, x1, cols[:, 6:7], cols[:, 2:3], ALU.mult, ALU.add))
                s.link(dve.scalar_tensor_tensor(x1, x1, 0.01, x1, ALU.mult, ALU.max))
                assert s.n == 16
                dve.sem_inc(used, 1)
                with dve.Fori(0, NC) as c:
                    s = Steps(dve, bs, PARTS * c + 16)
                    dve.wait_ge(mm, PARTS * NC + c + 1)
                    dve.wait_ge(row_free, c + 1)
                    for j in range(PARTS):
                        s.link(dve.tensor_tensor(hrow[:, part(j), :], psv(2 + j, PT, P), over(dinv[:, bass.ds(c * CT + j * PT, PT)], P, PT, P), ALU.mult))
                    met(dve)
                    dve.tensor_copy(hkeep[:, bass.ds(c * CT, CT), :], hrow).then_inc(used, 1)

        def gather_engines(block, table, idx, g, idx_ready, gath, agg):
            @block.sync
            def _(sp):
                def load_idx(i, b):
                    sp.dma_start(idx[:, b, :], a["src_et"][:, bass.ds((i * SLOTS + b) * KT, KT)]).then_inc(idx_ready[b], 16)
                for b in range(SLOTS):
                    load_idx(0, b)
                with sp.Fori(0, NR - 1) as i:
                    for b in range(SLOTS):
                        sp.wait_ge(gath[b], 16 * KT * (i + 1))
                        met(sp)
                        load_idx(i + 1, b)

            @block.gpsimd
            def _(pool):
                with pool.Fori(0, NR) as i:
                    for b in range(SLOTS):
                        pool.wait_ge(idx_ready[b], 16 * (i + 1))
                        pool.wait_ge(agg, i * SLOTS + b + 1)
                        met(pool)
                        for k in range(KT):
                            pool.indirect_dma_start(
                                out=g[:, b, k, :], out_offset=None, in_=table,
                                in_offset=bass.IndirectOffsetOnAxis(ap=idx[:, b, k:k + 1], axis=0)).then_inc(gath[b], 16)

        idx_ready, gath, oh_done, agg, acc_step = sems("gcn_idx"), sems("gcn_gathered"), sem("gcn_onehot"), sem("gcn_sums"), sem("gcn_added")
        A = Arena(TMP, 0, TW)
        idx = A.take(SLOTS, KT, dtype=U32)
        g = A.take(SLOTS, KT, P)
        oh = A.take(2, KT, P)
        with nc.Block() as block:
            gather_engines(block, tab1_d, idx, g, idx_ready, gath, agg)

            @block.tensor
            def _(pe):
                pe.sem_inc(agg, SLOTS)

                def program(narrow):
                    with pe.Fori(0, NR) as i:
                        for b in range(SLOTS):
                            pe.wait_ge(oh_done, i * SLOTS + b + 1)
                            pe.wait_ge(gath[b], 16 * KT * (i + 1))
                            sum_bank_free(pe, acc_step, i, b, narrow)
                            for k in range(KT):
                                bank, c, start, stop = sum_place(narrow, b, k)
                                m = nc.tensor.matmul(PS[bank][:, 0, c:c + P], g[:, b, k, :], oh[:, b % 2, k, :], start=start, stop=stop)
                            m.then_inc(agg, 1)
                either(pe, program)

            @block.vector
            def _(dve):
                def prepare(n, b):
                    dve.wait_ge(agg, n + 3)
                    onehot(dve, oh[:, b % 2, :, :], n).then_inc(oh_done, 1)

                def program(narrow):
                    def round_(i, last):
                        for b in range(SLOTS):
                            if b < SLOTS - 1 or not last:
                                prepare(i * SLOTS + b + 1, b + 1)
                            accumulate(dve, acc_step, agg, SLOTS, i, b, narrow, lambda first: AC[:, bass.ds(first, P)],
                                       lambda bank, c: PS[bank][:, 0, c:c + P])

                    prepare(0, 0)
                    with dve.Fori(0, NR - 1) as i:
                        round_(i, False)
                    round_(NR - 1, True)

                dve.memset(acc1, 0.0).then_inc(acc_step, 1)
                dve.sem_inc(acc_step, 7)
                either(dve, program)

        ld, staged, mm, used, fs, acts, vrdy, rrdy, lnd, xt, xc = (sem("gcn_end_loads"), sem("gcn_end_staged"), sem("gcn_end_products"), sem("gcn_end_used"),
            sem("gcn_end_dve"), sem("gcn_end_exp"), sem("gcn_end_var"), sem("gcn_end_rstd"), sem("gcn_end_ln"), sem("gcn_end_x_t"), sem("gcn_end_x_copied"))
        A = Arena(TMP, 0, TW)
        ac = A.take(CN)
        t = A.take(CT, P)
        q = A.take(CT, P)
        sm, vr, rs, ls = A.take(CT), A.take(CT), A.take(CT), A.take(CT)
        bg = A.take(P)
        with nc.Block() as block:
            @block.sync
            def _(sp):
                sp.dma_start(bg, row_bc("L1_gnn_bg")).then_inc(ld, 16)
                sp.wait_ge(ld, 16)

            @block.scalar
            def _(act):
                with act.Fori(0, NC) as c:
                    act.wait_ge(mm, c + 1)
                    met(act)
                    nc.scalar.copy(ac, AC[:, bass.ds(c * CN, CN)]).then_inc(staged, 1)
                    act.wait_ge(acts, 4 * c + 1)
                    nc.scalar.activation(q, t, ACT.Exp).then_inc(acts, 1)
                    act.wait_ge(acts, 4 * c + 3)
                    nc.scalar.activation(ls, ls, ACT.Ln).then_inc(acts, 1)
                    rstd_act(act, lnd, vr, rs, vrdy, rrdy, c)
                    keep_x(act, c, (2, 3), xt, xc)

            @block.tensor
            def _(pe):
                pe.sem_inc(mm, 1)
                pe.sem_inc(xc, PARTS)
                with pe.Fori(0, NC) as c:
                    pe.wait_ge(staged, c + 1)
                    for k in range(CT):
                        m = nc.tensor.transpose(psv(k // PT, PT, P)[:, k % PT, :], ac[:, k * P:(k + 1) * P], ident[:, :])
                    m.then_inc(mm, 1)
                    pe.wait_ge(used, c + 1)
                    pe.wait_ge(xc, PARTS * (c + 1))
                    transpose_x(pe, t, (2, 3), xt)

            @block.vector
            def _(dve):
                dve.wait_ge(ld, 16)
                per = 30
                with dve.Fori(0, NC) as c:
                    s = Steps(dve, fs, c * per)
                    dve.wait_ge(mm, c + 2)
                    dve.wait_ge(xc, PARTS * (c + 1))
                    for j in range(PARTS):
                        s.link(dve.tensor_tensor(t[:, part(j), :], psv(j, PT, P), hkeep[:, bass.ds(c * CT + j * PT, PT), :], ALU.add))
                    s.link(dve.tensor_tensor(t, t, over(dinv[:, bass.ds(c * CT, CT)], P, CT, P), ALU.mult))
                    s.link(dve.tensor_tensor(t, t, bg.unsqueeze(1).to_broadcast([P, CT, P]), ALU.add))
                    s.link(dve.tensor_reduce(sm, t, AX.X, ALU.max))
                    s.link(dve.tensor_tensor(t, t, over(sm, P, CT, P), ALU.subtract))
                    dve.sem_inc(acts, 1)
                    dve.wait_ge(acts, 4 * c + 2)
                    s.link(dve.tensor_reduce(ls, q, AX.X, ALU.add))
                    dve.sem_inc(acts, 1)
                    dve.wait_ge(acts, 4 * c + 4)
                    s.link(dve.tensor_tensor(t, t, over(ls, P, CT, P), ALU.subtract))
                    residual_out(dve, s, t, q, sm, vr, rs, vrdy, rrdy, c, 1, 0)
                    dve.sem_inc(fs, per - s.n)
                    dve.sem_inc(used, 1)

        layer_ends()

        ld, ts, td = sem("hgt_prep_loads"), sem("hgt_prep_type"), sem("hgt_prep_dve")
        T8kvq, T8s = WA[0:NTYPE, 0:3 * P], rows[0:NTYPE, 0:P]
        embT = TMP[:, 0:NTYPE]
        rel = cols[0:NREL, 0:H2]
        names = ("L2_gnn_Wk", "L2_gnn_Wv", "L2_gnn_Wq", "L2_gnn_Wskip")
        with nc.Block() as block:
            @block.sync
            def _(sp):
                for j, n_ in enumerate(names):
                    sp.dma_start(WB[:, j * P:(j + 1) * P], a[n_][0:P, :]).then_inc(ld, 16)
                    sp.dma_start(typ[:, j * P:(j + 1) * P], a[n_][P:2 * P, :]).then_inc(ld, 16)
                sp.dma_start(WB[:, 4 * P:5 * P], a["L2_gnn_Wo"]).then_inc(ld, 16)
                sp.dma_start(embT, a["L2_gnn_type_emb_T"]).then_inc(ld, 16)
                sp.dma_start(rel, a["L2_gnn_rel_scale"]).then_inc(ld, 16)
                sp.wait_ge(ld, 16 * 11)

            @block.tensor
            def _(pe):
                pe.wait_ge(ld, 16 * 11)
                nc.tensor.matmul(PS[0][0:NTYPE, 0, :], embT, typ[:, 0:4 * P], start=True, stop=True).then_inc(ts, 1)

            @block.vector
            def _(dve):
                dve.wait_ge(ts, 1)
                s = Steps(dve, td)
                s.link(dve.tensor_copy(T8kvq, PS[0][0:NTYPE, 0, 0:3 * P]))
                s.link(dve.tensor_copy(T8s, PS[0][0:NTYPE, 0, 3 * P:4 * P]))
                s.link(dve.tensor_scalar(rel, rel, 1.0 / float(np.sqrt(C2)), None, ALU.mult))

        tld, staged, mm, evac, ohd, stored, row_free = (sem("hgt_type_loads"), sem("hgt_staged"), sem("hgt_products"), sem("hgt_copied"),
            sem("hgt_type_onehot"), sem("hgt_stored"), sem("hgt_row_free"))
        A = Arena(TMP, 0, TW)
        xs = A.take(CN)
        nt8 = A.take(CN, parts=NTYPE, dtype=I32)
        oh8 = A.take(CN, parts=NTYPE)
        kvq = Arena(PM, 0, T * Z0).take(CT, 3 * P)
        pairs = CT // 2

        def load_types(sp, c, tld):
            sp.dma_start(nt8, a["type_row"][0, bass.ds(c * CN, CN)].partition_broadcast(NTYPE)).then_inc(tld, 16)

        with nc.Block() as block:
            @block.sync
            def _(sp):
                sp.sem_inc(row_free, 1)
                with sp.Fori(0, NC) as c:
                    sp.wait_ge(row_free, c + 1)
                    met(sp)
                    load_types(sp, c, tld)
                    sp.wait_ge(evac, pairs * (c + 2) - 1)
                    met(sp)
                    sp.dma_start(table_rows(kv_d, c, 2 * P), kvq[:, :, 0:2 * P]).then_inc(stored, 16)
                    sp.dma_start(table_rows(q_d, c, P), kvq[:, :, 2 * P:3 * P]).then_inc(stored, 16)
                    sp.wait_ge(stored, 32 * (c + 1))
                    sp.sem_inc(row_free, 1)

            @block.vector
            def _(dve):
                with dve.Fori(0, NC) as c:
                    dve.wait_ge(tld, 16 * (c + 1))
                    dve.wait_ge(mm, pairs * c + 1)
                    dve.tensor_scalar(oh8, nt8, iota_p[0:NTYPE, 0:1], None, ALU.is_equal).then_inc(ohd, 1)

            @block.scalar
            def _(act):
                act.sem_inc(evac, pairs - 1)
                with act.Fori(0, NC) as c:
                    act.wait_ge(mm, pairs * c + 1)
                    met(act)
                    nc.scalar.copy(xs, xT[:, bass.ds(c * CN, CN)]).then_inc(staged, 1)
                    act.wait_ge(row_free, c + 1)
                    met(act)
                    for j in range(pairs):
                        act.wait_ge(mm, pairs * c + j + 2)
                        nc.scalar.copy(kvq[:, 2 * j:2 * j + 2, :], PS[j % 4][:, :, 0:3 * P]).then_inc(evac, 1)

            @block.tensor
            def _(pe):
                pe.sem_inc(mm, 1)
                with pe.Fori(0, NC) as c:
                    pe.wait_ge(staged, c + 1)
                    pe.wait_ge(ohd, c + 1)
                    for k in range(CT):
                        if k in (0, 8):
                            pe.wait_ge(evac, pairs * c + pairs - 1 + k // 8)
                        ps = PS[k // 2 % 4][:, k % 2, 0:3 * P]
                        nc.tensor.matmul(ps, xs[:, k * P:(k + 1) * P], WB[:, 0:3 * P], start=True, stop=False)
                        m = nc.tensor.matmul(ps, oh8[:, k * P:(k + 1) * P], T8kvq, start=False, stop=True)
                        if k % 2 == 1:
                            m.then_inc(mm, 1)

        idx_ready, lr_ready, q_ready, rel_ready = sems("h1_idx", 2), sems("h1_local_dst", 2), sems("h1_q_rows", 2), sems("h1_relations", 2)
        gath, kept = sems("h1_gathered"), sems("h1_kept")
        oh_done, q_mm, q_used, scored = sem("h1_onehot"), sem("h1_product"), sem("h1_q_used"), sem("h1_dve")
        A = Arena(AC, 0, T * 2 * H0)
        g = A.take(SLOTS, KT, 2 * P)
        qw = A.take(2, HALF, P)
        lrb = A.take(SLOTS, KT * P)
        relb = A.take(SLOTS, KT * P, parts=NREL, dtype=I32)
        ohT = A.take(2, KT * P)
        A = Arena(TMP, 0, TW)
        idx = A.take(2, HALF, dtype=U32)
        oh16 = A.take(2, KT * P, parts=NREL)
        prod = A.take(KT, P)
        dot = A.take(KT, H2)
        with nc.Block() as block:
            @block.sync
            def _(sp):
                def program(narrow):
                    def load_rows(i, h):
                        at = bass.ds((i * 2 + h) * HALF * P, HALF * P)
                        sp.dma_start(lrb[:, 2 * h:2 * h + 2, :].rearrange("p b e -> p (b e)"), lrow_d[0, at].partition_broadcast(P)).then_inc(lr_ready[h], 16)
                        sp.dma_start(relb[:, 2 * h:2 * h + 2, :].rearrange("p b e -> p (b e)"), a["rel_row"][0, at].partition_broadcast(NREL)).then_inc(rel_ready[h], 16)

                    first_pass_loads(sp, narrow, lambda i, h: load_node_windows(sp, narrow, i, h, qw, q_d, q_ready),
                                     load_rows, gath, oh_done, q_mm)
                either(sp, program)
                for b in range(SLOTS):
                    sp.wait_ge(kept[b], 16 * (NR + 1))

            @block.gpsimd
            def _(pool):
                with pool.Fori(0, NR) as i:
                    for b in range(SLOTS):
                        pool.wait_ge(idx_ready[b // 2], 16 * (i + 1))
                        pool.wait_ge(kept[b], 16 * (i + 1))
                        pool.wait_ge(q_used, i * SLOTS + b + 1)
                        met(pool)
                        for k in range(KT):
                            pool.indirect_dma_start(
                                out=g[:, b, k, :], out_offset=None, in_=kv_d,
                                in_offset=bass.IndirectOffsetOnAxis(ap=idx[:, b // 2, (b % 2) * KT + k:(b % 2) * KT + k + 1], axis=0)).then_inc(gath[b], 16)

            @block.scalar
            def _(act):
                for b in range(SLOTS):
                    act.sem_inc(kept[b], 16)
                with act.Fori(0, NR) as i:
                    for b in range(SLOTS):
                        act.wait_ge(gath[b], 16 * KT * (i + 1))
                        met(act)
                        act.dma_start(edge_d[:, bass.ds((i * SLOTS + b) * KT, KT), :], g[:, b, :, P:2 * P]).then_inc(kept[b], 16)

            @block.vector
            def _(dve):
                def prepare(i, b, n):
                    dve.wait_ge(lr_ready[b // 2], 16 * (i + 1))
                    dve.wait_ge(rel_ready[b // 2], 16 * (i + 1))
                    dve.wait_ge(q_mm, n + 1)
                    dve.tensor_scalar(oh16[:, b % 2, :], relb[:, b, :], iota_p[0:NREL, 0:1], None, ALU.is_equal)
                    dve.tensor_scalar(ohT[:, b % 2, :], lrb[:, b, :], iota_p[:, 0:1], None, ALU.is_equal).then_inc(oh_done, 1)

                def score(i, b, n):
                    s = Steps(dve, scored, 2 * n)
                    dve.wait_ge(q_mm, n + 3)
                    dve.wait_ge(gath[b], 16 * KT * (i + 1))
                    s.link(dve.tensor_tensor(prod, psv(b % 2, KT, P), g[:, b, :, 0:P], ALU.mult))
                    s.link(dve.tensor_reduce(dot, prod.rearrange("p k (h c) -> p k h c", c=C2), AX.X, ALU.add))
                    dve.tensor_tensor(pm2[:, bass.ds(n * KT, KT), :], dot, psv(2 + b % 2, KT, H2), ALU.mult).then_inc(q_used, 1)

                dve.sem_inc(q_used, SLOTS)
                prepare(0, 0, 0)

                def round_(i, last):
                    for b in range(SLOTS):
                        n = i * SLOTS + b
                        if b < SLOTS - 1:
                            prepare(i, b + 1, n + 1)
                        elif not last:
                            prepare(i + 1, 0, n + 1)
                        score(i, b, n)

                with dve.Fori(0, NR - 1) as i:
                    round_(i, False)
                round_(NR - 1, True)

            @block.tensor
            def _(pe):
                pe.sem_inc(q_mm, 2)

                def program(narrow):
                    with pe.Fori(0, NR) as i:
                        for b in range(SLOTS):
                            n = i * SLOTS + b
                            pe.wait_ge(oh_done, n + 1)
                            pe.wait_ge(q_ready[b // 2], windows_loaded(narrow, i))
                            pe.wait_ge(q_used, n + 3)
                            for k in range(KT):
                                w = slice(k * P, (k + 1) * P)
                                nc.tensor.matmul(psv(2 + b % 2, KT, H2)[:, k, :], oh16[:, b % 2, w], rel, start=True, stop=True)
                                m = nc.tensor.matmul(psv(b % 2, KT, P)[:, k, :], ohT[:, b % 2, w], qw[:, b // 2, window_of(narrow, b, k), :],
                                                     start=True, stop=True)
                            m.then_inc(q_mm, 1)
                either(pe, program)

        ts, td, ta = sem("h_max_t"), sem("h_max_dve"), sem("h_exp")
        top = TMP[:, 0:1]
        top1 = TMP[0:1, 4:5]
        with nc.Block() as block:
            @block.vector
            def _(dve):
                s = Steps(dve, td)
                tail = pm2[:, T - ROUND:T, :]
                s.link(dve.tensor_tensor(tail, tail, over(padneg[:, :], P, ROUND, H2), ALU.add))
                s.link(dve.tensor_reduce(top, PM[:, 0:T * H2], AX.X, ALU.max))
                dve.wait_ge(ts, 1)
                s.link(dve.tensor_reduce(top1, PS[0][0:1, 0, 0:P], AX.X, ALU.max))
                dve.wait_ge(ts, 2)
                s.link(dve.tensor_scalar(top, PS[0][:, 1, 0:1], -1.0, None, ALU.mult))

            @block.tensor
            def _(pe):
                pe.wait_ge(td, 2)
                nc.tensor.transpose(PS[0][0:1, 0, 0:P], top, ident[:, :]).then_inc(ts, 1)
                pe.wait_ge(td, 3)
                nc.tensor.matmul(PS[0][:, 1, 0:1], ones[0:1, :], top1, start=True, stop=True).then_inc(ts, 1)

            @block.scalar
            def _(act):
                act.wait_ge(td, 4)
                nc.scalar.activation(PM[:, 0:T * H2], PM[:, 0:T * H2], ACT.Exp, bias=top).then_inc(ta, 1)

        weighted_pass("hgt_sum", pm2, H2, C2, H2)

        ld, tld, staged, mm, used, fs, acts, vrdy, rrdy, lnd, xt, xc = (sem("hgt_end_loads"), sem("hgt_end_types"), sem("hgt_end_staged"),
            sem("hgt_end_products"), sem("hgt_end_used"), sem("hgt_end_dve"), sem("hgt_end_exp"), sem("hgt_end_var"), sem("hgt_end_rstd"),
            sem("hgt_end_ln"), sem("hgt_end_x_t"), sem("hgt_end_x_copied"))
        A = Arena(PM, 0, T * Z0)
        rb = A.take(3, P)
        xs = A.take(CN)
        ac = A.take(CN)
        zc = A.take(CN, parts=H2)
        t = A.take(CT, P)
        q = A.take(CT, P)
        nt8 = A.take(CN, parts=NTYPE, dtype=I32)
        oh8 = A.take(CN, parts=NTYPE)
        sm, vr, rs = A.take(CT), A.take(CT), A.take(CT)
        with nc.Block() as block:
            @block.sync
            def _(sp):
                for j, n_ in enumerate(("L2_gnn_bo", "L2_gnn_gamma", "L2_gnn_beta")):
                    sp.dma_start(rb[:, j, :], row_bc(n_)).then_inc(ld, 16)
                with sp.Fori(0, NC) as c:
                    sp.dma_start(nt8, a["type_row"][0, bass.ds(c * CN, CN)].partition_broadcast(NTYPE)).then_inc(tld, 16)
                    sp.wait_ge(used, c + 1)
                    met(sp)
                sp.wait_ge(ld, 48)

            @block.scalar
            def _(act):
                act.sem_inc(acts, 1)
                with act.Fori(0, NC) as c:
                    act.wait_ge(mm, 2 * c + 1)
                    met(act)
                    nc.scalar.copy(xs, xT[:, bass.ds(c * CN, CN)]).then_inc(staged, 1)
                    nc.scalar.copy(ac, acc2[:, 0, bass.ds(c * CN, CN)]).then_inc(staged, 1)
                    nc.scalar.copy(zc, acc2[0:H2, 1, bass.ds(c * CN, CN)]).then_inc(staged, 1)
                    rstd_act(act, lnd, vr, rs, vrdy, rrdy, 2 * c)
                    act.wait_ge(acts, 2 * c + 2)
                    nc.scalar.activation(q, q, ACT.Exp).then_inc(acts, 1)
                    rstd_act(act, lnd, vr, rs, vrdy, rrdy, 2 * c + 1)
                    keep_x(act, c, (0, 1), xt, xc)

            @block.tensor
            def _(pe):
                pe.sem_inc(mm, 1)
                with pe.Fori(0, NC) as c:
                    pe.wait_ge(staged, 3 * c + 3)
                    pe.wait_ge(xc, PARTS * (c + 1))
                    for j in range(PARTS * 2):
                        m = nc.tensor.matmul(PS[j // 2][:, j % 2, 0:QN], headmap[:, :], zc[:, j * QN:(j + 1) * QN], start=True, stop=True)
                    m.then_inc(mm, 1)
                    pe.wait_ge(fs, c * 60 + 5)
                    for k in range(CT):
                        w = slice(k * P, (k + 1) * P)
                        ps = psv(2 + k // PT, PT, P)[:, k % PT, :]
                        nc.tensor.matmul(ps, ac[:, w], WB[:, 4 * P:5 * P], start=True, stop=False)
                        nc.tensor.matmul(ps, xs[:, w], WB[:, 3 * P:4 * P], start=False, stop=False)
                        m = nc.tensor.matmul(ps, oh8[:, w], T8s, start=False, stop=True)
                    m.then_inc(mm, 1)
                    pe.wait_ge(used, c + 1)
                    transpose_x(pe, t, (0, 1), xt)

            @block.vector
            def _(dve):
                dve.wait_ge(ld, 48)
                dve.sem_inc(xc, PARTS)
                per = 60
                with dve.Fori(0, NC) as c:
                    s = Steps(dve, fs, c * per)
                    dve.wait_ge(mm, 2 * c + 2)
                    qv = q.rearrange("p a b -> p (a b)")
                    for j in range(PARTS):
                        s.link(dve.tensor_scalar(qv[:, j * PN:(j + 1) * PN].rearrange("p (a b) -> p a b", a=2), PS[j][:, :, 0:QN], SM_EPS, None, ALU.add))
                    s.link(dve.reciprocal(qv, qv))
                    s.link(dve.tensor_tensor(ac, ac, qv, ALU.mult))
                    dve.wait_ge(tld, 16 * (c + 1))
                    s.link(dve.tensor_scalar(oh8, nt8, iota_p[0:NTYPE, 0:1], None, ALU.is_equal))
                    dve.wait_ge(mm, 2 * c + 3)
                    for j in range(PARTS):
                        s.link(dve.tensor_tensor(t[:, part(j), :], psv(2 + j, PT, P), rb[:, 0, :].unsqueeze(1).to_broadcast([P, PT, P]), ALU.add))
                    layer_norm(dve, s, t, q, sm, vr, rs, vrdy, rrdy, 2 * c)
                    s.link(dve.tensor_tensor(t, t, rb[:, 1, :].unsqueeze(1).to_broadcast([P, CT, P]), ALU.mult))
                    s.link(dve.tensor_tensor(t, t, rb[:, 2, :].unsqueeze(1).to_broadcast([P, CT, P]), ALU.add))
                    s.link(dve.tensor_scalar(q, t, 0.0, None, ALU.min))
                    dve.sem_inc(acts, 1)
                    dve.wait_ge(acts, 2 * c + 3)
                    s.link(dve.tensor_scalar(q, q, -1.0, None, ALU.add))
                    s.link(dve.scalar_tensor_tensor(t, t, 0.0, q, ALU.max, ALU.add))
                    residual_out(dve, s, t, q, sm, vr, rs, vrdy, rrdy, c, 2, 1)
                    dve.sem_inc(fs, per - s.n)
                    dve.sem_inc(used, 1)

        layer_ends()

        ld, cd, ca, bt = sem("sch_loads"), sem("sch_dve"), sem("sch_sin"), sem("sch_bias")
        A = Arena(PM, 0, T * Z0)
        cw = A.take(T)
        after_cw = A.at
        wq = A.take(T)
        wk = A.take(T, dtype=I32)
        brow = typ[0:1, 0:P]
        bres = typ[0:1, P:2 * P]
        bsplit = typ[0:96, 2 * P:4 * P].bitcast(BF16)
        ones_b = typ[0:96, 4 * P:5 * P].bitcast(BF16)[:, 0:P]
        b1, cap1, l2b, cap2, capc = (cols[:, j:j + 1] for j in range(5))
        lin1, w1, w2, lin2, linw = WA[:, 0:P], WA[0:NG, P:2 * P], WA[:, 2 * P:3 * P], WB[:, 0:P], WB[:, P:2 * P]
        with nc.Block() as block:
            @block.sync
            def _(sp):
                for dst_, src_ in ((lin1, a["L3_gnn_lin1_w_T"]), (w1, a["L3_gnn_mlp_w1_T"]), (w2, a["L3_gnn_mlp_w2_T"]), (lin2, a["L3_gnn_lin2_w_T"]),
                                   (linw, a["L3_gnn_lin_w_T"]), (cw, a["w_et"]), (b1, col_in("L3_gnn_mlp_b1")), (l2b, col_in("L3_gnn_lin2_b")),
                                   (brow, a["L3_gnn_mlp_b2"].rearrange("(o f) -> o f", o=1))):
                    sp.dma_start(dst_, src_).then_inc(ld, 16)
                sp.wait_ge(ld, 144)

            @block.tensor
            def _(pe):
                pe.wait_ge(ld, 144)
                nc.tensor.matmul(PS[0][0:1, 0, 0:P], ones[:, 0:1], w2, start=True, stop=True).then_inc(bt, 1)

            @block.vector
            def _(dve):
                s = Steps(dve, cd)
                dve.wait_ge(ld, 144)
                s.link(dve.tensor_scalar(wk, cw, 0.05, None, ALU.mult))
                s.link(dve.tensor_copy(wq, wk))
                s.link(dve.scalar_tensor_tensor(wq, wq, -20.0, cw, ALU.mult, ALU.add))
                s.link(dve.scalar_tensor_tensor(wq, wq, -1.0, wq, ALU.mult, ALU.max))
                s.link(dve.tensor_scalar(cw, wq, -1.0, 20.0, ALU.mult, ALU.add))
                s.link(dve.tensor_tensor(wq, wq, cw, ALU.min))
                s.link(dve.tensor_scalar(wq, wq, -float(np.pi) / 10, float(np.pi) / 2, ALU.mult, ALU.add))
                s.link(dve.memset(capc, SP_CAP))
                s.link(dve.tensor_scalar(cap1, b1, -1.0, SP_CAP, ALU.mult, ALU.add))
                s.link(dve.tensor_scalar(cap2, l2b, -1.0, SP_CAP, ALU.mult, ALU.add))
                dve.wait_ge(ca, 1)
                s.link(dve.tensor_scalar(cw, wq, 0.5, 0.5, ALU.mult, ALU.add))
                dve.wait_ge(bt, 1)
                s.link(dve.scalar_tensor_tensor(brow, PS[0][0:1, 0, 0:P], -LN2, brow, ALU.mult, ALU.add))
                s.link(dve.memset(bsplit, 0.0))
                s.link(dve.memset(ones_b, 1.0))
                for j in range(3):
                    part = bsplit[32 * j:32 * j + 1, :].rearrange("p (k f) -> p k f", f=P)
                    s.link(dve.tensor_copy(part, brow.unsqueeze(1).to_broadcast([1, KT, P])))
                    s.link(dve.tensor_copy(bres, part[:, 0, :]))
                    s.link(dve.tensor_tensor(brow, brow, bres, ALU.subtract))

            @block.scalar
            def _(act):
                act.wait_ge(cd, 7)
                nc.scalar.activation(wq, wq, ACT.Sin).then_inc(ca, 1)

        staged, mm, evac, stored, row_free = sem("sch_staged"), sem("sch_products"), sem("sch_copied"), sem("sch_stored"), sem("sch_row_free")
        A = Arena(TMP, 0, TW)
        xs = A.take(CN)
        hrow = A.take(CT, P)
        with nc.Block() as block:
            @block.sync
            def _(sp):
                sp.sem_inc(row_free, 1)
                with sp.Fori(0, NC) as c:
                    sp.wait_ge(evac, PARTS * (c + 1))
                    met(sp)
                    sp.dma_start(table_rows(tab3_d, c, P), hrow).then_inc(stored, 16)
                    sp.wait_ge(stored, 16 * (c + 1))
                    sp.sem_inc(row_free, 1)

            @block.scalar
            def _(act):
                with act.Fori(0, NC) as c:
                    act.wait_ge(mm, c + 1)
                    met(act)
                    nc.scalar.copy(xs, xT[:, bass.ds(c * CN, CN)]).then_inc(staged, 1)
                    act.wait_ge(mm, c + 2)
                    act.wait_ge(row_free, c + 1)
                    for j in range(PARTS):
                        nc.scalar.copy(hrow[:, part(j), :], psv(j, PT, P)).then_inc(evac, 1)

            @block.tensor
            def _(pe):
                pe.sem_inc(mm, 1)
                with pe.Fori(0, NC) as c:
                    pe.wait_ge(staged, c + 1)
                    for k in range(CT):
                        m = nc.tensor.matmul(psv(k // PT, PT, P)[:, k % PT, :], xs[:, k * P:(k + 1) * P], lin1, start=True, stop=True)
                    m.then_inc(mm, 1)

        idx_ready, gath, attr_ready = sems("sch_idx"), sems("sch_gathered"), sems("sch_attr")
        z_mm, sp_act, sp_done, w_mm, msg_done, oh_done, agg, acc_step, softs = (sem("sch_z"), sem("sch_log"), sem("sch_softplus"), sem("sch_filters"),
            sem("sch_messages"), sem("sch_onehot"), sem("sch_sums"), sem("sch_added"), sem("sch_act"))
        A = Arena(PM, after_cw, T * Z0)
        attr = A.take(SLOTS, KT * P, parts=NG)
        ex = A.take(2, 2, KT * P)
        soft = A.take(2, KT * P)
        msg = A.take(2, KT, P)
        oh = A.take(2, KT, P)
        A = Arena(TMP, 0, TW)
        idx = A.take(SLOTS, KT, dtype=U32)
        g = A.take(SLOTS, KT, P)
        zh = [PS[0], PS[3]]
        zb = [zh[b // 2][:, b % 2, :] for b in range(SLOTS)]
        wb = [PS[1][:, j, :].rearrange("p (k f) -> p k f", f=P) for j in range(2)]
        sb_ = [PS[2][:, j, :] for j in range(2)]
        with nc.Block() as block:
            @block.sync
            def _(sp):
                def load_idx(i, b):
                    sp.dma_start(idx[:, b, :], a["src_et"][:, bass.ds((i * SLOTS + b) * KT, KT)]).then_inc(idx_ready[b], 16)

                def load_attr(i, b):
                    sp.dma_start(attr[:, b, :], a["attrT"][:, bass.ds((i * SLOTS + b) * KT * P, KT * P)]).then_inc(attr_ready[b], 16)

                for b in range(SLOTS):
                    load_idx(0, b)
                    load_attr(0, b)
                with sp.Fori(0, NR - 1) as i:
                    for b in range(SLOTS):
                        sp.wait_ge(z_mm, i * SLOTS + b + 1)
                        met(sp)
                        load_attr(i + 1, b)
                        sp.wait_ge(gath[b], 16 * KT * (i + 1))
                        met(sp)
                        load_idx(i + 1, b)

            @block.gpsimd
            def _(pool):
                with pool.Fori(0, NR) as i:
                    for b in range(SLOTS):
                        pool.wait_ge(idx_ready[b], 16 * (i + 1))
                        pool.wait_ge(msg_done, i * SLOTS + b + 1)
                        met(pool)
                        for k in range(KT):
                            pool.indirect_dma_start(
                                out=g[:, b, k, :], out_offset=None, in_=tab3_d,
                                in_offset=bass.IndirectOffsetOnAxis(ap=idx[:, b, k:k + 1], axis=0)).then_inc(gath[b], 16)

            @block.tensor
            def _(pe):
                def filters_in(i, b, n):
                    pe.wait_ge(attr_ready[b], 16 * (i + 1))
                    pe.wait_ge(sp_done, n + 1)
                    nc.tensor.matmul(zb[b], w1, attr[:, b, :], start=True, stop=True).then_inc(z_mm, 1)

                def filters_out(b, n):
                    pe.wait_ge(sp_done, n + SLOTS + 1)
                    pe.wait_ge(msg_done, n + 3)
                    nc.tensor.matmul(PS[1][:, b % 2, :], ones_b, bsplit, start=True, stop=False, skip_group_check=True)
                    for k in range(KT):
                        m = nc.tensor.matmul(wb[b % 2][:, k, :], soft[:, b % 2, k * P:(k + 1) * P], w2, start=False, stop=(k == KT - 1),
                                             skip_group_check=True)
                    m.then_inc(w_mm, 1)

                def sums(i, b, n, narrow):
                    pe.wait_ge(msg_done, n + SLOTS + 1)
                    pe.wait_ge(oh_done, n + 1)
                    sum_bank_free(pe, acc_step, i, b, narrow)
                    for k in range(KT):
                        bank, c, start, stop = sum_place(narrow, b, k)
                        m = nc.tensor.matmul(sb_[bank][:, c:c + P], msg[:, b % 2, k, :], oh[:, b % 2, k, :], start=start, stop=stop)
                    m.then_inc(agg, 1)

                def program(narrow):
                    def round_(i, last):
                        for b in range(SLOTS):
                            n = i * SLOTS + b
                            if not last:
                                filters_in(i + 1, b, n + SLOTS)
                            if b + 1 < SLOTS or not last:
                                filters_out((b + 1) % SLOTS, n + 1)
                            sums(i, b, n, narrow)

                    for b in range(SLOTS):
                        filters_in(0, b, b)
                    filters_out(0, 0)
                    with pe.Fori(0, NR - 1) as i:
                        round_(i, False)
                    round_(NR - 1, True)
                either(pe, program)

            @block.scalar
            def _(act):
                with act.Fori(0, NR) as i:
                    for h in range(2):
                        s = Steps(act, softs, 2 * (2 * i + h))
                        groups = i * SLOTS + 2 * h + 2
                        act.wait_ge(z_mm, groups)
                        act.wait_ge(sp_done, groups)
                        e = ex[:, h, :, :]
                        s.link(nc.scalar.activation(e, zh[h][:, :, :], ACT.Relu, bias=cap1, scale=-1.0))
                        s.link(nc.scalar.activation(e, e, ACT.Exp, bias=capc, scale=-1.0))
                        nc.scalar.activation(e, e, ACT.Ln, bias=1.0).then_inc(sp_act, 1)

            @block.vector
            def _(dve):
                def softplus(i, b, n):
                    dve.wait_ge(sp_act, 2 * i + b // 2 + 1)
                    dve.wait_ge(w_mm, n + 1)
                    dve.scalar_tensor_tensor(soft[:, b % 2, :], zb[b], b1, ex[:, b // 2, b % 2, :], ALU.add, ALU.max).then_inc(sp_done, 1)

                def messages(i, b, n):
                    dve.wait_ge(w_mm, n + 3)
                    dve.wait_ge(gath[b], 16 * KT * (i + 1))
                    dve.wait_ge(agg, n + 1)
                    dve.tensor_tensor(msg[:, b % 2, :, :], wb[b % 2], g[:, b, :, :], ALU.mult).then_inc(msg_done, 1)
                    for k in range(KT):
                        t_ = bass.ds(n * KT + k, 1)
                        m = dve.scalar_tensor_tensor(oh[:, b % 2, k, :], iota_f[:, :], lr[:, t_], cw[:, t_].to_broadcast([P, P]), ALU.is_equal, ALU.mult)
                    m.then_inc(oh_done, 1)

                def program(narrow):
                    def round_(i, last):
                        for b in range(SLOTS):
                            n = i * SLOTS + b
                            if b + 1 < SLOTS:
                                softplus(i, b + 1, n + 1)
                            elif not last:
                                softplus(i + 1, 0, n + 1)
                            messages(i, b, n)
                            accumulate(dve, acc_step, agg, 2, i, b, narrow, lambda first: AC[:, bass.ds(first, P)],
                                       lambda bank, c: sb_[bank][:, c:c + P])

                    softplus(0, 0, 0)
                    with dve.Fori(0, NR - 1) as i:
                        round_(i, False)
                    round_(NR - 1, True)

                dve.memset(acc1, 0.0).then_inc(acc_step, 1)
                dve.sem_inc(acc_step, 7)
                dve.sem_inc(sp_done, SLOTS)
                dve.sem_inc(msg_done, SLOTS)
                dve.sem_inc(w_mm, 2)
                dve.sem_inc(agg, 2)
                either(dve, program)

        ld, mm, used, fs, acts, vrdy, rrdy, lnd, z_act, st = (sem("sch_end_loads"), sem("sch_end_products"), sem("sch_end_used"), sem("sch_end_dve"),
            sem("sch_end_soft"), sem("sch_end_var"), sem("sch_end_rstd"), sem("sch_end_ln"), sem("sch_end_log"), sem("sch_end_stored"))
        A = Arena(TMP, 0, TW)
        e_ = A.take(PARTS, 2, QN)
        so = A.take(PARTS, 2, QN)
        t = A.take(CT, P)
        q = A.take(CT, P)
        sm, vr, rs = A.take(CT), A.take(CT), A.take(CT)
        lb = A.take(P)
        with nc.Block() as block:
            @block.sync
            def _(sp):
                sp.dma_start(lb, row_bc("L3_gnn_lin_b")).then_inc(ld, 16)
                with sp.Fori(0, NC) as c:
                    sp.wait_ge(used, c + 1)
                    met(sp)
                    sp.dma_start(table_rows(out, c, P), xn[:, bass.ds(c * CT, CT), :]).then_inc(st, 16)
                sp.wait_ge(st, 16 * NC)

            @block.tensor
            def _(pe):
                with pe.Fori(0, NC) as c:
                    pe.wait_ge(acts, c + 1)
                    for j in range(PARTS * 2):
                        m = nc.tensor.matmul(PS[j // 2][:, j % 2, 0:QN], lin2, AC[:, bass.ds(c * CN + j * QN, QN)], start=True, stop=True)
                    m.then_inc(mm, 1)
                    pe.wait_ge(fs, c * 40 + 3)
                    sv_ = so.rearrange("p a b c -> p (a b c)")
                    for k in range(CT):
                        m = nc.tensor.matmul(psv(2 + k // PT, PT, P)[:, k % PT, :], sv_[:, k * P:(k + 1) * P], linw, start=True, stop=True)
                    m.then_inc(mm, 1)

            @block.scalar
            def _(act):
                with act.Fori(0, NC) as c:
                    s = Steps(act, z_act, 4 * c)
                    act.wait_ge(mm, 2 * c + 1)
                    for j in range(PARTS):
                        s.link(nc.scalar.activation(e_[:, j, :, :], PS[j][:, :, 0:QN], ACT.Relu, bias=cap2, scale=-1.0))
                    s.link(nc.scalar.activation(e_, e_, ACT.Exp, bias=capc, scale=-1.0))
                    s.link(nc.scalar.activation(e_, e_, ACT.Ln, bias=1.0))
                    rstd_act(act, lnd, vr, rs, vrdy, rrdy, c)

            @block.vector
            def _(dve):
                dve.wait_ge(ld, 16)
                dve.sem_inc(acts, 1)
                per = 40
                with dve.Fori(0, NC) as c:
                    s = Steps(dve, fs, c * per)
                    dve.wait_ge(z_act, 4 * c + 4)
                    for j in range(PARTS):
                        s.link(dve.scalar_tensor_tensor(so[:, j, :, :], PS[j][:, :, 0:QN], l2b, e_[:, j, :, :], ALU.add, ALU.max))
                    s.link(dve.tensor_scalar(so, so, -LN2, None, ALU.add))
                    dve.wait_ge(mm, 2 * c + 2)
                    for j in range(PARTS):
                        s.link(dve.tensor_tensor(t[:, part(j), :], psv(2 + j, PT, P), lb.unsqueeze(1).to_broadcast([P, PT, P]), ALU.add))
                    dve.sem_inc(acts, 1)
                    residual_out(dve, s, t, q, sm, vr, rs, vrdy, rrdy, c, 1, 0)
                    dve.sem_inc(fs, per - s.n)
                    dve.sem_inc(used, 1)


_WEIGHTS = ["L0_gnn_W", "L0_gnn_skip_W", "L0_gnn_gat_bias", "L0_gnn_skip_b", "L0_gnn_ln_g", "L0_gnn_ln_b", "L1_gnn_blin", "L1_gnn_gamma",
            "L1_gnn_beta", "L1_gnn_bg", "L2_gnn_type_emb", "L2_gnn_Wk", "L2_gnn_Wq", "L2_gnn_Wv", "L2_gnn_rel_scale", "L2_gnn_Wo",
            "L2_gnn_bo", "L2_gnn_Wskip", "L2_gnn_gamma", "L2_gnn_beta", "L3_gnn_mlp_b1", "L3_gnn_mlp_b2", "L3_gnn_lin2_b", "L3_gnn_lin_b"]
_TRANSPOSED = ["L1_gnn_Wlin", "L1_gnn_Wg", "L2_gnn_type_emb", "L3_gnn_mlp_w1", "L3_gnn_mlp_w2", "L3_gnn_lin1_w", "L3_gnn_lin2_w", "L3_gnn_lin_w"]


def kernel(**inputs):
    import numpy as _np
    import concourse.bacc as _bacc
    from concourse import mybir as _mybir
    from concourse.bass_utils import run_bass_kernel_spmd as _run

    i = {k: _np.asarray(v) for k, v in inputs.items()}

    def edges(v, fill, shift=0):
        v = _np.concatenate([v, _np.full((EP - E,) + v.shape[1:], fill, v.dtype)])
        if shift:
            v = _np.concatenate([_np.full(1, -1, v.dtype), v[:-1]]) if shift < 0 else _np.concatenate([v[1:], _np.full(1, -1, v.dtype)])
        return v

    def by_tile(v):
        return v.reshape(T, P).T

    def nodes(v):
        return _np.concatenate([v, _np.zeros((NP - N,) + v.shape[1:], v.dtype)])

    arrays = {k: i[k] for k in _WEIGHTS}
    arrays |= {k + "_T": i[k].T for k in _TRANSPOSED}
    dst = edges(i["dst"], N)
    arrays |= {
        "x": nodes(i["x"]), "xT": nodes(i["x"]).T,
        "src_et": _np.ascontiguousarray(by_tile(edges(i["src"], 0))).view(_np.uint32),
        "dst_et": by_tile(dst), "dst_prev_et": by_tile(edges(i["dst"], N, -1)),
        "dst_first": dst[::P].reshape(1, T),
        "dst_round_first": _np.repeat(dst[::RW], ROUND).reshape(1, T), "dst_round_last": dst[RW - 1::RW].reshape(1, NR),
        "dst_rows": dst.reshape(NR, RW), "dst_prev_rows": edges(i["dst"], N, -1).reshape(NR, RW),
        "dst_next_rows": edges(i["dst"], N, 1).reshape(NR, RW),
        "w_et": by_tile(edges(i["edge_weight"], 0)), "rel_row": edges(i["edge_type_16"], 0).reshape(1, EP),
        "attrT": edges(i["edge_attr_50"], 0).T, "type_row": nodes(i["node_type_8"]).reshape(1, NP),
        "att_src": i["L0_gnn_att_src"].reshape(P), "att_dst": i["L0_gnn_att_dst"].reshape(P),
    }
    nc = _bacc.Bacc("TRN2", target_bir_lowering=False, num_devices=1)
    args, fed = {}, {}
    for name, v in arrays.items():
        v = _np.ascontiguousarray(v)
        fed[f"in_{name}"] = v
        args[name] = nc.dram_tensor(f"in_{name}", v.shape, _mybir.dt.from_np(v.dtype), kind="ExternalInput").ap()
    out = nc.dram_tensor("out_0", (NP, P), _mybir.dt.float32, kind="ExternalOutput").ap()
    build(nc, args, out)
    r = _run(nc, [fed], core_ids=[0])
    return r.results[0]["out_0"][:N]
```
